# Optimizing a Trainium2 kernel written in Bass

```python
import numpy as np
import jax
import jax.numpy as jnp

def _softmax(x, axis=-1):
    return jax.nn.softmax(x, axis=axis)

def _gelu(x):
    return jax.nn.gelu(x, approximate=True)

def _silu(x):
    return jax.nn.silu(x)

def _sigmoid(x):
    return jax.nn.sigmoid(x)

def _layernorm(x, axis=-1, eps=1e-05):
    m = jnp.mean(x, axis=axis, keepdims=True)
    v = jnp.var(x, axis=axis, keepdims=True)
    return (x - m) / jnp.sqrt(v + eps)

def _scatter_add(tgt, idx, src, axis=0):
    return tgt.at[idx].add(src)

def _segment_sum(src, seg, n):
    return jax.ops.segment_sum(src, seg, n)
kernel_name = 'mk_macaron_d4_jaxref_r8_d59939'

def setup_inputs(seed: int=0):
    np.random.seed(seed)
    _w = jnp.asarray

    def _L0_attn_setup():
        import jax, jax.numpy as jnp
        import numpy as np
        THETA = 10000.0

        def _rope(x, pos):
            hd = x.shape[-1]
            inv_freq = 1.0 / THETA ** (jnp.arange(0, hd, 2, dtype=jnp.float32) / hd)
            ang = pos.astype(jnp.float32)[:, None] * inv_freq[None, :]
            cos, sin = (jnp.cos(ang), jnp.sin(ang))
            x1, x2 = (x[..., 0::2], x[..., 1::2])
            r1 = x1 * cos - x2 * sin
            r2 = x1 * sin + x2 * cos
            return jnp.stack([r1, r2], axis=-1).reshape(x.shape)
        key = jax.random.key(seed)
        ks = jax.random.split(key, 5)
        b, s, d = (2, 256, 128)
        scale = 0.02
        return {'x': jax.random.normal(ks[0], (b, s, d), dtype=jnp.float32), 'Wq': jax.random.normal(ks[1], (d, d), dtype=jnp.float32) * scale, 'Wk': jax.random.normal(ks[2], (d, d), dtype=jnp.float32) * scale, 'Wv': jax.random.normal(ks[3], (d, d), dtype=jnp.float32) * scale, 'Wo': jax.random.normal(ks[4], (d, d), dtype=jnp.float32) * scale}
    _L0_attn_in = _L0_attn_setup()

    def _L0_ffn_setup():
        import jax, jax.numpy as jnp
        import numpy as np
        E = 16
        F_C = 2.0
        D = 128
        I = 4 * D
        IS = 2 * D
        B, S = (4, 128)
        key = jax.random.key(seed)
        ks = jax.random.split(key, 8)
        w = 0.02
        return {'hidden_states': jax.random.normal(ks[0], (B, S, D), dtype=jnp.float32), 'gate_w': jax.random.normal(ks[1], (E, D), dtype=jnp.float32) * w, 'Wg': jax.random.normal(ks[2], (E, I, D), dtype=jnp.float32) * w, 'Wu': jax.random.normal(ks[3], (E, I, D), dtype=jnp.float32) * w, 'Wd': jax.random.normal(ks[4], (E, D, I), dtype=jnp.float32) * w, 'Sg': jax.random.normal(ks[5], (IS, D), dtype=jnp.float32) * w, 'Su': jax.random.normal(ks[6], (IS, D), dtype=jnp.float32) * w, 'Sd': jax.random.normal(ks[7], (D, IS), dtype=jnp.float32) * w}
    _L0_ffn_in = _L0_ffn_setup()

    def _L1_attn_setup():
        import jax, jax.numpy as jnp
        import numpy as np
        import math
        E, N, K, R = (128, 16, 4, 64)
        B, L = (2, 256)
        key = jax.random.key(seed)
        ks = jax.random.split(key, 8)
        gn = lambda k, sh, sc: jax.random.normal(k, sh, dtype=jnp.float32) * sc
        W_z = gn(ks[0], (E, E), E ** (-0.5))
        W_params = gn(ks[1], (R + 2 * N, E), E ** (-0.5))
        conv_w = gn(ks[2], (E, 1, K), 0.5)
        dt_std = R ** (-0.5) * 0.1
        W_dt = jax.random.uniform(ks[3], (E, R), jnp.float32, -dt_std, dt_std)
        b_dt = jnp.full((E,), math.log(math.expm1(0.001)), dtype=jnp.float32)
        A_log = jnp.tile(jnp.log(jnp.arange(1, N + 1, dtype=jnp.float32))[None, :], (E, 1))
        D = jnp.ones((E,), dtype=jnp.float32)
        W_out = gn(ks[4], (E, E), E ** (-0.5))
        x = jax.random.normal(ks[5], (B, L, E), dtype=jnp.float32)
        return dict(x=x, W_z=W_z, W_params=W_params, conv_w=conv_w, W_dt=W_dt, b_dt=b_dt, A_log=A_log, D=D, W_out=W_out)
    _L1_attn_in = _L1_attn_setup()

    def _L1_ffn_setup():
        import jax, jax.numpy as jnp
        import numpy as np
        D_MODEL, D_FF, N_EXPERTS, TOP_K = (128, 256, 8, 2)
        B, S = (2, 256)
        key = jax.random.key(seed)
        ks = jax.random.split(key, 6)
        sd = 1.0 / np.sqrt(D_MODEL)
        sf = 1.0 / np.sqrt(D_FF)
        return {'x': jax.random.normal(ks[0], (B, S, D_MODEL), jnp.float32), 'router_w': jax.random.normal(ks[1], (N_EXPERTS, D_MODEL), jnp.float32) * sd, 'gate_w': jax.random.normal(ks[2], (N_EXPERTS, D_MODEL, D_FF), jnp.float32) * sd, 'gate_b': jnp.zeros((N_EXPERTS, D_FF), jnp.float32), 'up_w': jax.random.normal(ks[3], (N_EXPERTS, D_MODEL, D_FF), jnp.float32) * sd, 'up_b': jnp.zeros((N_EXPERTS, D_FF), jnp.float32), 'down_w': jax.random.normal(ks[4], (N_EXPERTS, D_FF, D_MODEL), jnp.float32) * sf, 'down_b': jnp.zeros((N_EXPERTS, D_MODEL), jnp.float32)}
    _L1_ffn_in = _L1_ffn_setup()

    def _L2_attn_setup():
        import jax, jax.numpy as jnp
        import numpy as np
        H, DK, DV, CHUNK = (4, 32, 32, 32)

        def _silu(x):
            return x * jax.nn.sigmoid(x)

        def _l2norm(x, eps=1e-06):
            return x * jax.lax.rsqrt(jnp.sum(x * x, -1, keepdims=True) + eps)

        def _rmsnorm(x, w, eps=1e-05):
            return x * jax.lax.rsqrt(jnp.mean(x * x, -1, keepdims=True) + eps) * w

        def _causal_dwconv(x, w):
            C = x.shape[-1]
            K = w.shape[-1]
            xp = jnp.pad(x, ((0, 0), (K - 1, 0), (0, 0))).transpose(0, 2, 1)
            y = jax.lax.conv_general_dilated(xp, w[:, None, :], (1,), 'VALID', feature_group_count=C, dimension_numbers=('NCH', 'OIH', 'NCH'))
            return y.transpose(0, 2, 1)

        def _fir(x, filt):
            B, L, h, d = x.shape
            y = _causal_dwconv(x.reshape(B, L, h * d), filt.reshape(h * d, -1))
            return y.reshape(B, L, h, d)

        def _delta_rule_chunkwise(q, k, v, beta):
            b, h, L, dk = q.shape
            dv = v.shape[-1]
            n = L // CHUNK
            q = _l2norm(q)
            k = _l2norm(k)
            v = v * beta[..., None]
            k_beta = k * beta[..., None]
            rs = lambda t: t.reshape(b, h, n, CHUNK, -1)
            q, k, v, k_beta = (rs(q), rs(k), rs(v), rs(k_beta))
            eye = jnp.eye(CHUNK, dtype=q.dtype)
            strict_lower = jnp.tril(jnp.ones((CHUNK, CHUNK), bool), -1)
            A = jnp.where(strict_lower, jnp.einsum('bhncd,bhnsd->bhncs', k_beta, k), 0.0)
            attn_inv = jax.scipy.linalg.solve_triangular(eye + A, jnp.broadcast_to(eye, A.shape), lower=True)
            u = attn_inv @ v
            w = attn_inv @ k_beta
            incl_lower = jnp.tril(jnp.ones((CHUNK, CHUNK), bool))

            def step(S, inp):
                q_i, k_i, u_i, w_i = inp
                attn_local = jnp.where(incl_lower, q_i @ jnp.swapaxes(k_i, -1, -2), 0.0)
                u_t = u_i - w_i @ S
                o_i = q_i @ S + attn_local @ u_t
                return (S + jnp.swapaxes(k_i, -1, -2) @ u_t, o_i)
            S0 = jnp.zeros((b, h, dk, dv), q.dtype)
            xs = tuple((jnp.moveaxis(t, 2, 0) for t in (q, k, u, w)))
            S, out = jax.lax.scan(step, S0, xs)
            return (jnp.moveaxis(out, 0, 2).reshape(b, h, L, dv), S)

        def _stats(x):
            return jnp.stack([x.mean(-1), x.var(-1), jnp.abs(x).mean(-1), jnp.sqrt(jnp.sum(x * x, -1))], -1)

        def _forward(x, Wq, Wk, Wv, Wb, conv_q, conv_k, conv_v, fir_long, fir_short, W1, b1, W2, b2, log_temp, base_bias, conv_residual_logit, rms_w, Wo):
            B, L, D = x.shape
            q = _silu(_causal_dwconv(x @ Wq, conv_q)).reshape(B, L, H, DK)
            k = _silu(_causal_dwconv(x @ Wk, conv_k)).reshape(B, L, H, DK)
            v = _silu(_causal_dwconv(x @ Wv, conv_v)).reshape(B, L, H, DV)
            beta = jax.nn.sigmoid(x @ Wb)
            delta, _S = _delta_rule_chunkwise(q.transpose(0, 2, 1, 3), k.transpose(0, 2, 1, 3), v.transpose(0, 2, 1, 3), beta.transpose(0, 2, 1))
            delta = delta.transpose(0, 2, 1, 3)
            f_short = _fir(v, fir_short)
            f_long = _fir(v, fir_long)
            stats = jnp.concatenate([_stats(f_short), _stats(f_long), _stats(delta), _stats(v)], -1)
            hidden_exp = jnp.broadcast_to(x[:, :, None, :], (B, L, H, D))
            gate_in = jnp.concatenate([hidden_exp, stats], -1)
            h1 = jax.nn.gelu(gate_in @ W1 + b1, approximate=False)
            logits = h1 @ W2 + b2 + base_bias
            temp = jax.nn.softplus(log_temp) + 0.0001
            p = jax.nn.softmax(logits / temp[:, None], -1)
            eps = 0.05
            p = jnp.maximum(p, jnp.array([eps, eps, 0.0, 0.0], p.dtype))
            p = p / jnp.sum(p, -1, keepdims=True)
            o = p[..., 0:1] * f_short + p[..., 1:2] * f_long + p[..., 2:3] * delta + p[..., 3:4] * v
            o = o + 0.5 * jax.nn.sigmoid(conv_residual_logit)[None, None, :, None] * f_short
            o = _rmsnorm(o, rms_w)
            return o.reshape(B, L, H * DV) @ Wo
        key = jax.random.key(seed)
        ks = jax.random.split(key, 13)
        B, L, D = (2, 256, 128)
        f = jnp.float32
        n = lambda k, shape, s=0.02: jax.random.normal(k, shape, f) * s
        return {'x': jax.random.normal(ks[0], (B, L, D), f), 'Wq': n(ks[1], (D, D)), 'Wk': n(ks[2], (D, D)), 'Wv': n(ks[3], (D, D)), 'Wb': n(ks[4], (D, H)), 'conv_q': n(ks[5], (D, 4), 0.1), 'conv_k': n(ks[6], (D, 4), 0.1), 'conv_v': n(ks[7], (D, 4), 0.1), 'fir_long': n(ks[8], (H, DV, 64)), 'fir_short': n(ks[9], (H, DV, 5)), 'W1': n(ks[10], (D + 16, D)), 'b1': jnp.zeros((D,), f), 'W2': n(ks[11], (D, 4)), 'b2': jnp.zeros((4,), f), 'log_temp': jnp.full((H,), float(np.log(np.expm1(0.7))), f), 'base_bias': jnp.tile(jnp.array([-0.5, -0.5, 1.0, 3.0], f), (H, 1)), 'conv_residual_logit': jnp.full((H,), -2.0, f), 'rms_w': jnp.ones((DV,), f), 'Wo': n(ks[12], (D, D))}
    _L2_attn_in = _L2_attn_setup()

    def _L2_ffn_setup():
        import jax, jax.numpy as jnp
        import numpy as np

        def _binarize(w):
            alpha = jax.lax.stop_gradient(jnp.mean(jnp.abs(w), axis=1, keepdims=True))
            bw = alpha * jnp.sign(w)
            return w + jax.lax.stop_gradient(bw - w)
        key = jax.random.key(seed)
        k1, k2, k3, k4, k5 = jax.random.split(key, 5)
        D, H = (128, 512)
        x = jax.random.normal(k1, (64, 196, D), dtype=jnp.float32)
        w1 = jax.random.normal(k2, (H, D), dtype=jnp.float32) * 0.02
        b1 = jax.random.normal(k3, (H,), dtype=jnp.float32) * 0.02
        w2 = jax.random.normal(k4, (D, H), dtype=jnp.float32) * 0.02
        b2 = jax.random.normal(k5, (D,), dtype=jnp.float32) * 0.02
        return {'x': x, 'w1': w1, 'b1': b1, 'w2': w2, 'b2': b2}
    _L2_ffn_in = _L2_ffn_setup()

    def _L3_attn_setup():
        import jax, jax.numpy as jnp
        import numpy as np
        D = 128
        DI = 256
        HS = 16
        PS = DI // HS
        NS = 64
        KC = 4
        CHUNK = 64
        HA = 16
        HKV = 4
        PA = D // HA
        MLP_MULT = 4
        ROPE_BASE = 10000.0
        B_SZ = 2
        L_SEQ = 256

        def rms_norm(x):
            eps = jnp.asarray(jnp.finfo(x.dtype).eps, x.dtype)
            return x * jax.lax.rsqrt(jnp.mean(jnp.square(x), axis=-1, keepdims=True) + eps)

        def silu(x):
            return x * jax.nn.sigmoid(x)

        def apply_rope(x, cos, sin):
            half = x.shape[-1] // 2
            x1, x2 = (x[..., :half], x[..., half:])
            return jnp.concatenate([x1 * cos + x2 * sin, -x1 * sin + x2 * cos], axis=-1)

        def selective_scan(x, A, Bm, Cm, dt, chunk):
            Bb, L, H, P = x.shape
            N = Bm.shape[-1]
            decay = jnp.exp(A * dt)
            nc = L // chunk
            xp = x.reshape(Bb, nc, chunk, H, P).transpose(0, 1, 3, 2, 4)
            Bp = Bm.reshape(Bb, nc, chunk, H, N).transpose(0, 1, 3, 2, 4)
            Cp = Cm.reshape(Bb, nc, chunk, H, N).transpose(0, 1, 3, 2, 4)
            x_dt = xp * dt[None, None, :, None, None]
            idx = jnp.arange(chunk)
            diff = idx[:, None] - idx[None, :]
            Lm = jnp.where(diff >= 0, decay[:, None, None] ** jnp.maximum(diff, 0), 0.0)
            CB = jnp.einsum('bchqn,bchkn->bchqk', Cp, Bp)
            y_diag = jnp.einsum('bchqk,bchkp->bchqp', CB * Lm[None, None], x_dt)
            decay_rev = decay[:, None] ** (chunk - 1 - idx)[None, :]
            states = jnp.einsum('bchtn,bchtp->bchnp', Bp * decay_rev[None, None, :, :, None], x_dt)
            ci = jnp.arange(nc)
            shift = ci[:, None] - ci[None, :] - 1
            cdec = decay ** chunk
            M = jnp.where(shift >= 0, cdec[:, None, None] ** jnp.maximum(shift, 0), 0.0)
            h_carry = jnp.einsum('hij,bjhnp->bihnp', M, states)
            decay_out = decay[:, None] ** (idx + 1)[None, :]
            y_off = jnp.einsum('bchtn,bchnp->bchtp', Cp, h_carry) * decay_out[None, None, :, :, None]
            y = (y_diag + y_off).transpose(0, 1, 3, 2, 4).reshape(Bb, L, H, P)
            return y

        def mlp(n, fc_w, proj_w):
            h = jax.nn.relu(n @ fc_w)
            return jnp.square(h) @ proj_w
        key = jax.random.key(seed)
        ks = jax.random.split(key, 24)
        w = lambda k, shp, s=0.02: jax.random.normal(k, shp, jnp.float32) * s
        dt_init = jax.random.uniform(ks[0], (HS,), jnp.float32, 0.001, 0.1)
        dt_bias = dt_init + jnp.log(-jnp.expm1(-dt_init))
        return {'x': jax.random.normal(ks[1], (B_SZ, L_SEQ, D), jnp.float32), 'in_proj_w': w(ks[2], (D, 2 * DI)), 'conv_w': w(ks[3], (DI, KC), 0.2), 'conv_b': jnp.zeros((DI,), jnp.float32), 'B_proj_w': w(ks[4], (D, HS * NS)), 'C_proj_w': w(ks[5], (D, HS * NS)), 'dt_bias': dt_bias, 'A_log': jnp.log(jnp.arange(1, HS + 1, dtype=jnp.float32)), 'D_param': jnp.ones((HS,), jnp.float32), 'out_proj_w': w(ks[6], (DI, D)), 'resid_mix_m': jnp.stack([jnp.ones(D), jnp.zeros(D)]).astype(jnp.float32), 'mamba_scale': jnp.ones((D,), jnp.float32), 'm_fc_w': w(ks[7], (D, MLP_MULT * D)), 'm_proj_w': w(ks[8], (MLP_MULT * D, D)), 'm_mlp_scale': jnp.ones((D,), jnp.float32), 'resid_mix_a': jnp.stack([jnp.ones(D), jnp.zeros(D)]).astype(jnp.float32), 'q_w': w(ks[9], (D, D)), 'k_w': w(ks[10], (D, HKV * PA)), 'v_w': w(ks[11], (D, HKV * PA)), 'o_w': w(ks[12], (D, D)), 'q_gain': jnp.full((HA,), 1.0, jnp.float32), 'attn_scale': jnp.ones((D,), jnp.float32), 'a_fc_w': w(ks[13], (D, MLP_MULT * D)), 'a_proj_w': w(ks[14], (MLP_MULT * D, D)), 'a_mlp_scale': jnp.ones((D,), jnp.float32)}
    _L3_attn_in = _L3_attn_setup()

    def _L3_ffn_setup():
        import jax, jax.numpy as jnp
        import numpy as np
        B, S, H, D, E = (4, 128, 128, 512, 8)
        key = jax.random.key(seed)
        ks = jax.random.split(key, 12)

        def init(k, shape, fan_in):
            return jax.random.normal(k, shape, jnp.float32) / np.float32(np.sqrt(fan_in))
        return {'x': jax.random.normal(ks[0], (B, S, H), jnp.float32), 'Wq': init(ks[1], (H, H), H), 'bq': jnp.zeros((H,), jnp.float32), 'Wk': init(ks[2], (H, H), H), 'bk': jnp.zeros((H,), jnp.float32), 'Wv': init(ks[3], (H, H), H), 'bv': jnp.zeros((H,), jnp.float32), 'Wo': init(ks[4], (H, H), H), 'bo': jnp.zeros((H,), jnp.float32), 'Wg': init(ks[5], (H, E), H), 'bg': jnp.zeros((E,), jnp.float32), 'W1': init(ks[6], (E, H, D), H), 'b1': jnp.zeros((E, D), jnp.float32), 'W2': init(ks[7], (E, D, H), D), 'b2': jnp.zeros((E, H), jnp.float32)}
    _L3_ffn_in = _L3_ffn_setup()
    _d = {'L0_attn_x': _L0_attn_in['x'], 'L0_attn_Wq': _L0_attn_in['Wq'], 'L0_attn_Wk': _L0_attn_in['Wk'], 'L0_attn_Wv': _L0_attn_in['Wv'], 'L0_attn_Wo': _L0_attn_in['Wo'], 'L0_ffn_gate_w': _L0_ffn_in['gate_w'], 'L0_ffn_Wg': _L0_ffn_in['Wg'], 'L0_ffn_Wu': _L0_ffn_in['Wu'], 'L0_ffn_Wd': _L0_ffn_in['Wd'], 'L0_ffn_Sg': _L0_ffn_in['Sg'], 'L0_ffn_Su': _L0_ffn_in['Su'], 'L0_ffn_Sd': _L0_ffn_in['Sd'], 'L1_attn_W_z': _L1_attn_in['W_z'], 'L1_attn_W_params': _L1_attn_in['W_params'], 'L1_attn_conv_w': _L1_attn_in['conv_w'], 'L1_attn_W_dt': _L1_attn_in['W_dt'], 'L1_attn_b_dt': _L1_attn_in['b_dt'], 'L1_attn_A_log': _L1_attn_in['A_log'], 'L1_attn_D': _L1_attn_in['D'], 'L1_attn_W_out': _L1_attn_in['W_out'], 'L1_ffn_router_w': _L1_ffn_in['router_w'], 'L1_ffn_gate_w': _L1_ffn_in['gate_w'], 'L1_ffn_gate_b': _L1_ffn_in['gate_b'], 'L1_ffn_up_w': _L1_ffn_in['up_w'], 'L1_ffn_up_b': _L1_ffn_in['up_b'], 'L1_ffn_down_w': _L1_ffn_in['down_w'], 'L1_ffn_down_b': _L1_ffn_in['down_b'], 'L2_attn_Wq': _L2_attn_in['Wq'], 'L2_attn_Wk': _L2_attn_in['Wk'], 'L2_attn_Wv': _L2_attn_in['Wv'], 'L2_attn_Wb': _L2_attn_in['Wb'], 'L2_attn_conv_q': _L2_attn_in['conv_q'], 'L2_attn_conv_k': _L2_attn_in['conv_k'], 'L2_attn_conv_v': _L2_attn_in['conv_v'], 'L2_attn_fir_long': _L2_attn_in['fir_long'], 'L2_attn_fir_short': _L2_attn_in['fir_short'], 'L2_attn_W1': _L2_attn_in['W1'], 'L2_attn_b1': _L2_attn_in['b1'], 'L2_attn_W2': _L2_attn_in['W2'], 'L2_attn_b2': _L2_attn_in['b2'], 'L2_attn_log_temp': _L2_attn_in['log_temp'], 'L2_attn_base_bias': _L2_attn_in['base_bias'], 'L2_attn_conv_residual_logit': _L2_attn_in['conv_residual_logit'], 'L2_attn_rms_w': _L2_attn_in['rms_w'], 'L2_attn_Wo': _L2_attn_in['Wo'], 'L2_ffn_w1': _L2_ffn_in['w1'], 'L2_ffn_b1': _L2_ffn_in['b1'], 'L2_ffn_w2': _L2_ffn_in['w2'], 'L2_ffn_b2': _L2_ffn_in['b2'], 'L3_attn_in_proj_w': _L3_attn_in['in_proj_w'], 'L3_attn_conv_w': _L3_attn_in['conv_w'], 'L3_attn_conv_b': _L3_attn_in['conv_b'], 'L3_attn_B_proj_w': _L3_attn_in['B_proj_w'], 'L3_attn_C_proj_w': _L3_attn_in['C_proj_w'], 'L3_attn_dt_bias': _L3_attn_in['dt_bias'], 'L3_attn_A_log': _L3_attn_in['A_log'], 'L3_attn_D_param': _L3_attn_in['D_param'], 'L3_attn_out_proj_w': _L3_attn_in['out_proj_w'], 'L3_attn_resid_mix_m': _L3_attn_in['resid_mix_m'], 'L3_attn_mamba_scale': _L3_attn_in['mamba_scale'], 'L3_attn_m_fc_w': _L3_attn_in['m_fc_w'], 'L3_attn_m_proj_w': _L3_attn_in['m_proj_w'], 'L3_attn_m_mlp_scale': _L3_attn_in['m_mlp_scale'], 'L3_attn_resid_mix_a': _L3_attn_in['resid_mix_a'], 'L3_attn_q_w': _L3_attn_in['q_w'], 'L3_attn_k_w': _L3_attn_in['k_w'], 'L3_attn_v_w': _L3_attn_in['v_w'], 'L3_attn_o_w': _L3_attn_in['o_w'], 'L3_attn_q_gain': _L3_attn_in['q_gain'], 'L3_attn_attn_scale': _L3_attn_in['attn_scale'], 'L3_attn_a_fc_w': _L3_attn_in['a_fc_w'], 'L3_attn_a_proj_w': _L3_attn_in['a_proj_w'], 'L3_attn_a_mlp_scale': _L3_attn_in['a_mlp_scale'], 'L3_ffn_Wq': _L3_ffn_in['Wq'], 'L3_ffn_bq': _L3_ffn_in['bq'], 'L3_ffn_Wk': _L3_ffn_in['Wk'], 'L3_ffn_bk': _L3_ffn_in['bk'], 'L3_ffn_Wv': _L3_ffn_in['Wv'], 'L3_ffn_bv': _L3_ffn_in['bv'], 'L3_ffn_Wo': _L3_ffn_in['Wo'], 'L3_ffn_bo': _L3_ffn_in['bo'], 'L3_ffn_Wg': _L3_ffn_in['Wg'], 'L3_ffn_bg': _L3_ffn_in['bg'], 'L3_ffn_W1': _L3_ffn_in['W1'], 'L3_ffn_b1': _L3_ffn_in['b1'], 'L3_ffn_W2': _L3_ffn_in['W2'], 'L3_ffn_b2': _L3_ffn_in['b2']}
    _x0 = _d['L0_attn_x']
    _d['L0_attn_x'] = jax.random.normal(jax.random.fold_in(jax.random.key(seed), 1), (8, 256, 128), dtype=_x0.dtype)
    del _x0
    return _d

def reference(L0_attn_x, L0_attn_Wq, L0_attn_Wk, L0_attn_Wv, L0_attn_Wo, L0_ffn_gate_w, L0_ffn_Wg, L0_ffn_Wu, L0_ffn_Wd, L0_ffn_Sg, L0_ffn_Su, L0_ffn_Sd, L1_attn_W_z, L1_attn_W_params, L1_attn_conv_w, L1_attn_W_dt, L1_attn_b_dt, L1_attn_A_log, L1_attn_D, L1_attn_W_out, L1_ffn_router_w, L1_ffn_gate_w, L1_ffn_gate_b, L1_ffn_up_w, L1_ffn_up_b, L1_ffn_down_w, L1_ffn_down_b, L2_attn_Wq, L2_attn_Wk, L2_attn_Wv, L2_attn_Wb, L2_attn_conv_q, L2_attn_conv_k, L2_attn_conv_v, L2_attn_fir_long, L2_attn_fir_short, L2_attn_W1, L2_attn_b1, L2_attn_W2, L2_attn_b2, L2_attn_log_temp, L2_attn_base_bias, L2_attn_conv_residual_logit, L2_attn_rms_w, L2_attn_Wo, L2_ffn_w1, L2_ffn_b1, L2_ffn_w2, L2_ffn_b2, L3_attn_in_proj_w, L3_attn_conv_w, L3_attn_conv_b, L3_attn_B_proj_w, L3_attn_C_proj_w, L3_attn_dt_bias, L3_attn_A_log, L3_attn_D_param, L3_attn_out_proj_w, L3_attn_resid_mix_m, L3_attn_mamba_scale, L3_attn_m_fc_w, L3_attn_m_proj_w, L3_attn_m_mlp_scale, L3_attn_resid_mix_a, L3_attn_q_w, L3_attn_k_w, L3_attn_v_w, L3_attn_o_w, L3_attn_q_gain, L3_attn_attn_scale, L3_attn_a_fc_w, L3_attn_a_proj_w, L3_attn_a_mlp_scale, L3_ffn_Wq, L3_ffn_bq, L3_ffn_Wk, L3_ffn_bk, L3_ffn_Wv, L3_ffn_bv, L3_ffn_Wo, L3_ffn_bo, L3_ffn_Wg, L3_ffn_bg, L3_ffn_W1, L3_ffn_b1, L3_ffn_W2, L3_ffn_b2):

    def _L0_attn_ref(x, Wq, Wk, Wv, Wo):
        import jax, jax.numpy as jnp
        import numpy as np
        THETA = 10000.0

        def _rope(x, pos):
            hd = x.shape[-1]
            inv_freq = 1.0 / THETA ** (jnp.arange(0, hd, 2, dtype=jnp.float32) / hd)
            ang = pos.astype(jnp.float32)[:, None] * inv_freq[None, :]
            cos, sin = (jnp.cos(ang), jnp.sin(ang))
            x1, x2 = (x[..., 0::2], x[..., 1::2])
            r1 = x1 * cos - x2 * sin
            r2 = x1 * sin + x2 * cos
            return jnp.stack([r1, r2], axis=-1).reshape(x.shape)
        b, s, d = x.shape
        n_heads = 16
        hd = d // n_heads

        def split_heads(t):
            return t.reshape(b, s, n_heads, hd).transpose(0, 2, 1, 3)
        q = split_heads(x @ Wq.T)
        k = split_heads(x @ Wk.T)
        v = split_heads(x @ Wv.T)
        pos = jnp.arange(s)
        q = _rope(q, pos)
        k = _rope(k, pos)
        scores = jnp.einsum('bhqd,bhkd->bhqk', q, k) / jnp.sqrt(jnp.float32(hd))
        causal = jnp.tril(jnp.ones((s, s), dtype=bool))
        scores = jnp.where(causal, scores, -jnp.inf)
        attn = jax.nn.softmax(scores, axis=-1)
        ctx = jnp.einsum('bhqk,bhkd->bhqd', attn, v)
        ctx = ctx.transpose(0, 2, 1, 3).reshape(b, s, d)
        return ctx @ Wo.T

    def _L0_ffn_ref(hidden_states, gate_w, Wg, Wu, Wd, Sg, Su, Sd):
        import jax, jax.numpy as jnp
        import numpy as np
        E = 16
        F_C = 2.0
        D = 128
        I = 4 * D
        IS = 2 * D
        B, S = (4, 128)
        b, s, d = hidden_states.shape
        T = b * s
        C = int(T * F_C / E)
        flat_x = hidden_states.reshape(T, d)
        logits = flat_x @ gate_w.T
        scores = jax.nn.softmax(logits, axis=-1).T
        topk_weight, topk_idx = jax.lax.top_k(scores, C)
        xg = flat_x[topk_idx]
        g = jnp.einsum('ecd,eid->eci', xg, Wg)
        u = jnp.einsum('ecd,eid->eci', xg, Wu)
        h = jax.nn.gelu(g, approximate=False) * u
        eo = jnp.einsum('eci,edi->ecd', h, Wd)
        eo = eo * topk_weight[..., None]
        flat_out = jnp.zeros_like(flat_x).at[topk_idx.reshape(-1)].add(eo.reshape(-1, d))
        out = flat_out.reshape(b, s, d)
        sg = hidden_states @ Sg.T
        su = hidden_states @ Su.T
        shared = jax.nn.gelu(sg, approximate=False) * su @ Sd.T
        return out + shared

    def _L1_attn_ref(x, W_z, W_params, conv_w, W_dt, b_dt, A_log, D, W_out):
        import jax, jax.numpy as jnp
        import numpy as np
        import math
        E, N, K, R = (128, 16, 4, 64)
        B, L = (2, 256)
        b, l, e = x.shape
        n = A_log.shape[1]
        r = W_dt.shape[1]
        k = conv_w.shape[-1]
        z = x @ W_z.T
        params = x @ W_params.T
        dt_unproj = params[..., :r]
        C_proj = params[..., r + n:]
        dt = jax.nn.softplus(dt_unproj @ W_dt.T + b_dt)
        xc = jax.lax.conv_general_dilated(x.transpose(0, 2, 1), conv_w, (1,), [(k - 1, 0)], dimension_numbers=('NCH', 'OIH', 'NCH'), feature_group_count=e)
        u = jax.nn.silu(xc.transpose(0, 2, 1))
        A = -jnp.exp(A_log)
        A_tilde = jnp.exp(dt[..., None] * A[None, None])
        B_tilde = jnp.where(jnp.abs(A)[None, None] < 1e-05, dt[..., None], (A_tilde - 1.0) / (A[None, None] + 1e-10))
        h0 = B_tilde[:, 0] * u[:, 0, :, None]

        def step(h, inp):
            a, bt, uu = inp
            h_new = a * h + bt * uu[..., None]
            return (h_new, h_new)
        xs = (A_tilde[:, :-1].transpose(1, 0, 2, 3), B_tilde[:, :-1].transpose(1, 0, 2, 3), u[:, :-1].transpose(1, 0, 2))
        _, hs = jax.lax.scan(step, h0, xs)
        h = jnp.concatenate([h0[None], hs], axis=0).transpose(1, 0, 2, 3)
        y = jnp.einsum('bln,blen->ble', C_proj, h)
        y_ssm = y + u * D
        y_gated = y_ssm * jax.nn.silu(z)
        return y_gated @ W_out.T

    def _L1_ffn_ref(x, router_w, gate_w, gate_b, up_w, up_b, down_w, down_b):
        import jax, jax.numpy as jnp
        import numpy as np
        D_MODEL, D_FF, N_EXPERTS, TOP_K = (128, 256, 8, 2)
        B, S = (2, 256)
        b, s, d = x.shape
        xf = x.reshape(b * s, d)
        n = xf.shape[0]
        router_logits = xf @ router_w.T
        probs = jax.nn.softmax(router_logits, axis=-1)
        topv, topi = jax.lax.top_k(probs, TOP_K)
        mask = jnp.zeros_like(probs).at[jnp.arange(n)[:, None], topi].set(1.0)
        probs = probs * mask
        probs = probs / (probs.sum(axis=-1, keepdims=True) + 1e-09)
        g = jnp.einsum('nd,edf->nef', xf, gate_w) + gate_b
        u = jnp.einsum('nd,edf->nef', xf, up_w) + up_b
        h = jax.nn.silu(g) * u
        expert_out = jnp.einsum('nef,efd->ned', h, down_w) + down_b
        y = jnp.einsum('ne,ned->nd', probs, expert_out)
        return y.reshape(b, s, d)

    def _L2_attn_ref(x, Wq, Wk, Wv, Wb, conv_q, conv_k, conv_v, fir_long, fir_short, W1, b1, W2, b2, log_temp, base_bias, conv_residual_logit, rms_w, Wo):
        import jax, jax.numpy as jnp
        import numpy as np
        H, DK, DV, CHUNK = (4, 32, 32, 32)

        def _silu(x):
            return x * jax.nn.sigmoid(x)

        def _l2norm(x, eps=1e-06):
            return x * jax.lax.rsqrt(jnp.sum(x * x, -1, keepdims=True) + eps)

        def _rmsnorm(x, w, eps=1e-05):
            return x * jax.lax.rsqrt(jnp.mean(x * x, -1, keepdims=True) + eps) * w

        def _causal_dwconv(x, w):
            C = x.shape[-1]
            K = w.shape[-1]
            xp = jnp.pad(x, ((0, 0), (K - 1, 0), (0, 0))).transpose(0, 2, 1)
            y = jax.lax.conv_general_dilated(xp, w[:, None, :], (1,), 'VALID', feature_group_count=C, dimension_numbers=('NCH', 'OIH', 'NCH'))
            return y.transpose(0, 2, 1)

        def _fir(x, filt):
            B, L, h, d = x.shape
            y = _causal_dwconv(x.reshape(B, L, h * d), filt.reshape(h * d, -1))
            return y.reshape(B, L, h, d)

        def _delta_rule_chunkwise(q, k, v, beta):
            b, h, L, dk = q.shape
            dv = v.shape[-1]
            n = L // CHUNK
            q = _l2norm(q)
            k = _l2norm(k)
            v = v * beta[..., None]
            k_beta = k * beta[..., None]
            rs = lambda t: t.reshape(b, h, n, CHUNK, -1)
            q, k, v, k_beta = (rs(q), rs(k), rs(v), rs(k_beta))
            eye = jnp.eye(CHUNK, dtype=q.dtype)
            strict_lower = jnp.tril(jnp.ones((CHUNK, CHUNK), bool), -1)
            A = jnp.where(strict_lower, jnp.einsum('bhncd,bhnsd->bhncs', k_beta, k), 0.0)
            attn_inv = jax.scipy.linalg.solve_triangular(eye + A, jnp.broadcast_to(eye, A.shape), lower=True)
            u = attn_inv @ v
            w = attn_inv @ k_beta
            incl_lower = jnp.tril(jnp.ones((CHUNK, CHUNK), bool))

            def step(S, inp):
                q_i, k_i, u_i, w_i = inp
                attn_local = jnp.where(incl_lower, q_i @ jnp.swapaxes(k_i, -1, -2), 0.0)
                u_t = u_i - w_i @ S
                o_i = q_i @ S + attn_local @ u_t
                return (S + jnp.swapaxes(k_i, -1, -2) @ u_t, o_i)
            S0 = jnp.zeros((b, h, dk, dv), q.dtype)
            xs = tuple((jnp.moveaxis(t, 2, 0) for t in (q, k, u, w)))
            S, out = jax.lax.scan(step, S0, xs)
            return (jnp.moveaxis(out, 0, 2).reshape(b, h, L, dv), S)

        def _stats(x):
            return jnp.stack([x.mean(-1), x.var(-1), jnp.abs(x).mean(-1), jnp.sqrt(jnp.sum(x * x, -1))], -1)

        def _forward(x, Wq, Wk, Wv, Wb, conv_q, conv_k, conv_v, fir_long, fir_short, W1, b1, W2, b2, log_temp, base_bias, conv_residual_logit, rms_w, Wo):
            B, L, D = x.shape
            q = _silu(_causal_dwconv(x @ Wq, conv_q)).reshape(B, L, H, DK)
            k = _silu(_causal_dwconv(x @ Wk, conv_k)).reshape(B, L, H, DK)
            v = _silu(_causal_dwconv(x @ Wv, conv_v)).reshape(B, L, H, DV)
            beta = jax.nn.sigmoid(x @ Wb)
            delta, _S = _delta_rule_chunkwise(q.transpose(0, 2, 1, 3), k.transpose(0, 2, 1, 3), v.transpose(0, 2, 1, 3), beta.transpose(0, 2, 1))
            delta = delta.transpose(0, 2, 1, 3)
            f_short = _fir(v, fir_short)
            f_long = _fir(v, fir_long)
            stats = jnp.concatenate([_stats(f_short), _stats(f_long), _stats(delta), _stats(v)], -1)
            hidden_exp = jnp.broadcast_to(x[:, :, None, :], (B, L, H, D))
            gate_in = jnp.concatenate([hidden_exp, stats], -1)
            h1 = jax.nn.gelu(gate_in @ W1 + b1, approximate=False)
            logits = h1 @ W2 + b2 + base_bias
            temp = jax.nn.softplus(log_temp) + 0.0001
            p = jax.nn.softmax(logits / temp[:, None], -1)
            eps = 0.05
            p = jnp.maximum(p, jnp.array([eps, eps, 0.0, 0.0], p.dtype))
            p = p / jnp.sum(p, -1, keepdims=True)
            o = p[..., 0:1] * f_short + p[..., 1:2] * f_long + p[..., 2:3] * delta + p[..., 3:4] * v
            o = o + 0.5 * jax.nn.sigmoid(conv_residual_logit)[None, None, :, None] * f_short
            o = _rmsnorm(o, rms_w)
            return o.reshape(B, L, H * DV) @ Wo
        return _forward(x, Wq, Wk, Wv, Wb, conv_q, conv_k, conv_v, fir_long, fir_short, W1, b1, W2, b2, log_temp, base_bias, conv_residual_logit, rms_w, Wo)

    def _L2_ffn_ref(x, w1, b1, w2, b2):
        import jax, jax.numpy as jnp
        import numpy as np

        def _binarize(w):
            alpha = jax.lax.stop_gradient(jnp.mean(jnp.abs(w), axis=1, keepdims=True))
            bw = alpha * jnp.sign(w)
            return w + jax.lax.stop_gradient(bw - w)
        bw1 = _binarize(w1)
        h = jnp.einsum('bsd,hd->bsh', x, bw1) + b1
        h = jax.nn.gelu(h, approximate=False)
        bw2 = _binarize(w2)
        out = jnp.einsum('bsh,dh->bsd', h, bw2) + b2
        return out

    def _L3_attn_ref(x, in_proj_w, conv_w, conv_b, B_proj_w, C_proj_w, dt_bias, A_log, D_param, out_proj_w, resid_mix_m, mamba_scale, m_fc_w, m_proj_w, m_mlp_scale, resid_mix_a, q_w, k_w, v_w, o_w, q_gain, attn_scale, a_fc_w, a_proj_w, a_mlp_scale):
        import jax, jax.numpy as jnp
        import numpy as np
        D = 128
        DI = 256
        HS = 16
        PS = DI // HS
        NS = 64
        KC = 4
        CHUNK = 64
        HA = 16
        HKV = 4
        PA = D // HA
        MLP_MULT = 4
        ROPE_BASE = 10000.0
        B_SZ = 2
        L_SEQ = 256

        def rms_norm(x):
            eps = jnp.asarray(jnp.finfo(x.dtype).eps, x.dtype)
            return x * jax.lax.rsqrt(jnp.mean(jnp.square(x), axis=-1, keepdims=True) + eps)

        def silu(x):
            return x * jax.nn.sigmoid(x)

        def apply_rope(x, cos, sin):
            half = x.shape[-1] // 2
            x1, x2 = (x[..., :half], x[..., half:])
            return jnp.concatenate([x1 * cos + x2 * sin, -x1 * sin + x2 * cos], axis=-1)

        def selective_scan(x, A, Bm, Cm, dt, chunk):
            Bb, L, H, P = x.shape
            N = Bm.shape[-1]
            decay = jnp.exp(A * dt)
            nc = L // chunk
            xp = x.reshape(Bb, nc, chunk, H, P).transpose(0, 1, 3, 2, 4)
            Bp = Bm.reshape(Bb, nc, chunk, H, N).transpose(0, 1, 3, 2, 4)
            Cp = Cm.reshape(Bb, nc, chunk, H, N).transpose(0, 1, 3, 2, 4)
            x_dt = xp * dt[None, None, :, None, None]
            idx = jnp.arange(chunk)
            diff = idx[:, None] - idx[None, :]
            Lm = jnp.where(diff >= 0, decay[:, None, None] ** jnp.maximum(diff, 0), 0.0)
            CB = jnp.einsum('bchqn,bchkn->bchqk', Cp, Bp)
            y_diag = jnp.einsum('bchqk,bchkp->bchqp', CB * Lm[None, None], x_dt)
            decay_rev = decay[:, None] ** (chunk - 1 - idx)[None, :]
            states = jnp.einsum('bchtn,bchtp->bchnp', Bp * decay_rev[None, None, :, :, None], x_dt)
            ci = jnp.arange(nc)
            shift = ci[:, None] - ci[None, :] - 1
            cdec = decay ** chunk
            M = jnp.where(shift >= 0, cdec[:, None, None] ** jnp.maximum(shift, 0), 0.0)
            h_carry = jnp.einsum('hij,bjhnp->bihnp', M, states)
            decay_out = decay[:, None] ** (idx + 1)[None, :]
            y_off = jnp.einsum('bchtn,bchnp->bchtp', Cp, h_carry) * decay_out[None, None, :, :, None]
            y = (y_diag + y_off).transpose(0, 1, 3, 2, 4).reshape(Bb, L, H, P)
            return y

        def mlp(n, fc_w, proj_w):
            h = jax.nn.relu(n @ fc_w)
            return jnp.square(h) @ proj_w
        Bb, L, _ = x.shape
        x0 = x
        xm = resid_mix_m[0][None, None] * x + resid_mix_m[1][None, None] * x0
        n = rms_norm(xm)
        vg = n @ in_proj_w
        value, gate = (vg[..., :DI], vg[..., DI:])
        v_t = value.transpose(0, 2, 1)
        v_conv = jax.lax.conv_general_dilated(v_t, conv_w[:, None, :], (1,), [(KC - 1, 0)], feature_group_count=DI, dimension_numbers=('NCH', 'OIH', 'NCH')) + conv_b[None, :, None]
        value = silu(v_conv).transpose(0, 2, 1).reshape(Bb, L, HS, PS)
        Bm = (xm @ B_proj_w).reshape(Bb, L, HS, NS)
        Cm = (xm @ C_proj_w).reshape(Bb, L, HS, NS)
        dt = jax.nn.softplus(dt_bias)
        A = -jnp.exp(A_log)
        y = selective_scan(value, A, Bm, Cm, dt, CHUNK)
        y = y + D_param[None, None, :, None] * value
        y = y.reshape(Bb, L, DI) * silu(gate) @ out_proj_w
        xm = xm + mamba_scale[None, None] * y
        xm = xm + m_mlp_scale[None, None] * mlp(rms_norm(xm), m_fc_w, m_proj_w)
        xa = resid_mix_a[0][None, None] * xm + resid_mix_a[1][None, None] * x0
        n = rms_norm(xa)
        q = (n @ q_w).reshape(Bb, L, HA, PA).transpose(0, 2, 1, 3)
        k = (n @ k_w).reshape(Bb, L, HKV, PA).transpose(0, 2, 1, 3)
        v = (n @ v_w).reshape(Bb, L, HKV, PA).transpose(0, 2, 1, 3)
        q = rms_norm(q)
        k = rms_norm(k)
        inv_freq = 1.0 / ROPE_BASE ** (jnp.arange(0, PA, 2, dtype=jnp.float32) / PA)
        f = jnp.outer(jnp.arange(L, dtype=jnp.float32), inv_freq)
        cos, sin = (jnp.cos(f)[None, None], jnp.sin(f)[None, None])
        q = apply_rope(q, cos, sin) * q_gain[None, :, None, None]
        k = apply_rope(k, cos, sin)
        G = HA // HKV
        k = jnp.repeat(k, G, axis=1)
        v = jnp.repeat(v, G, axis=1)
        s = jnp.einsum('bhqd,bhkd->bhqk', q, k) / np.float32(np.sqrt(PA))
        mask = jnp.tril(jnp.ones((L, L), bool))
        s = jnp.where(mask[None, None], s, jnp.asarray(-jnp.inf, s.dtype))
        att = jax.nn.softmax(s, axis=-1)
        y = jnp.einsum('bhqk,bhkd->bhqd', att, v).transpose(0, 2, 1, 3).reshape(Bb, L, D)
        xa = xa + attn_scale[None, None] * (y @ o_w)
        xa = xa + a_mlp_scale[None, None] * mlp(rms_norm(xa), a_fc_w, a_proj_w)
        return xa

    def _L3_ffn_ref(x, Wq, bq, Wk, bk, Wv, bv, Wo, bo, Wg, bg, W1, b1, W2, b2):
        import jax, jax.numpy as jnp
        import numpy as np
        B, S, H, D, E = (4, 128, 128, 512, 8)
        q = x @ Wq + bq
        k = x @ Wk + bk
        v = x @ Wv + bv
        scale = jnp.asarray(1.0 / np.sqrt(H), x.dtype)
        scores = jnp.einsum('bqh,bkh->bqk', q, k) * scale
        attn = jax.nn.softmax(scores, axis=-1)
        a = jnp.einsum('bqk,bkh->bqh', attn, v) @ Wo + bo
        x = x + a
        gates = jax.nn.softmax(x @ Wg + bg, axis=-1)
        hmid = jax.nn.relu(jnp.einsum('bsh,ehd->bsed', x, W1) + b1)
        eout = jnp.einsum('bsed,edh->bseh', hmid, W2) + b2
        y = jnp.einsum('bse,bseh->bsh', gates, eout)
        return x + y
    x = L0_attn_x
    x = x + 0.5 * _L0_ffn_ref(_layernorm(x, axis=-1), L0_ffn_gate_w, L0_ffn_Wg, L0_ffn_Wu, L0_ffn_Wd, L0_ffn_Sg, L0_ffn_Su, L0_ffn_Sd)
    x = x + _L0_attn_ref(_layernorm(x, axis=-1), L0_attn_Wq, L0_attn_Wk, L0_attn_Wv, L0_attn_Wo)
    x = x + 0.5 * _L0_ffn_ref(_layernorm(x, axis=-1), L0_ffn_gate_w, L0_ffn_Wg, L0_ffn_Wu, L0_ffn_Wd, L0_ffn_Sg, L0_ffn_Su, L0_ffn_Sd)
    x = x + 0.5 * _L1_ffn_ref(_layernorm(x, axis=-1), L1_ffn_router_w, L1_ffn_gate_w, L1_ffn_gate_b, L1_ffn_up_w, L1_ffn_up_b, L1_ffn_down_w, L1_ffn_down_b)
    x = x + _L1_attn_ref(_layernorm(x, axis=-1), L1_attn_W_z, L1_attn_W_params, L1_attn_conv_w, L1_attn_W_dt, L1_attn_b_dt, L1_attn_A_log, L1_attn_D, L1_attn_W_out)
    x = x + 0.5 * _L1_ffn_ref(_layernorm(x, axis=-1), L1_ffn_router_w, L1_ffn_gate_w, L1_ffn_gate_b, L1_ffn_up_w, L1_ffn_up_b, L1_ffn_down_w, L1_ffn_down_b)
    x = x + 0.5 * _L2_ffn_ref(_layernorm(x, axis=-1), L2_ffn_w1, L2_ffn_b1, L2_ffn_w2, L2_ffn_b2)
    x = x + _L2_attn_ref(_layernorm(x, axis=-1), L2_attn_Wq, L2_attn_Wk, L2_attn_Wv, L2_attn_Wb, L2_attn_conv_q, L2_attn_conv_k, L2_attn_conv_v, L2_attn_fir_long, L2_attn_fir_short, L2_attn_W1, L2_attn_b1, L2_attn_W2, L2_attn_b2, L2_attn_log_temp, L2_attn_base_bias, L2_attn_conv_residual_logit, L2_attn_rms_w, L2_attn_Wo)
    x = x + 0.5 * _L2_ffn_ref(_layernorm(x, axis=-1), L2_ffn_w1, L2_ffn_b1, L2_ffn_w2, L2_ffn_b2)
    x = x + 0.5 * _L3_ffn_ref(_layernorm(x, axis=-1), L3_ffn_Wq, L3_ffn_bq, L3_ffn_Wk, L3_ffn_bk, L3_ffn_Wv, L3_ffn_bv, L3_ffn_Wo, L3_ffn_bo, L3_ffn_Wg, L3_ffn_bg, L3_ffn_W1, L3_ffn_b1, L3_ffn_W2, L3_ffn_b2)
    x = x + _L3_attn_ref(_layernorm(x, axis=-1), L3_attn_in_proj_w, L3_attn_conv_w, L3_attn_conv_b, L3_attn_B_proj_w, L3_attn_C_proj_w, L3_attn_dt_bias, L3_attn_A_log, L3_attn_D_param, L3_attn_out_proj_w, L3_attn_resid_mix_m, L3_attn_mamba_scale, L3_attn_m_fc_w, L3_attn_m_proj_w, L3_attn_m_mlp_scale, L3_attn_resid_mix_a, L3_attn_q_w, L3_attn_k_w, L3_attn_v_w, L3_attn_o_w, L3_attn_q_gain, L3_attn_attn_scale, L3_attn_a_fc_w, L3_attn_a_proj_w, L3_attn_a_mlp_scale)
    x = x + 0.5 * _L3_ffn_ref(_layernorm(x, axis=-1), L3_ffn_Wq, L3_ffn_bq, L3_ffn_Wk, L3_ffn_bk, L3_ffn_Wv, L3_ffn_bv, L3_ffn_Wo, L3_ffn_bo, L3_ffn_Wg, L3_ffn_bg, L3_ffn_W1, L3_ffn_b1, L3_ffn_W2, L3_ffn_b2)
    return x

_drawn_inputs = setup_inputs


def setup_inputs(seed=0):
    import zlib

    import numpy as np

    out = dict(_drawn_inputs(seed))
    spreads = {'L1_attn_b_dt': (-6.907255172729492, 0.2),
     'L1_attn_D': (1.0, 0.2),
     'L1_ffn_gate_b': (0.0, 0.1),
     'L1_ffn_up_b': (0.0, 0.1),
     'L1_ffn_down_b': (0.0, 0.1),
     'L2_attn_b1': (0.0, 0.8),
     'L2_attn_b2': (0.0, 0.8),
     'L2_attn_log_temp': (0.013658997602760792, 0.6),
     'L2_attn_conv_residual_logit': (-2.0, 0.6),
     'L2_attn_rms_w': (1.0, 0.2),
     'L3_attn_conv_b': (0.0, 0.8),
     'L3_attn_D_param': (1.0, 0.6),
     'L3_attn_mamba_scale': (1.0, 0.6),
     'L3_attn_m_mlp_scale': (1.0, 0.6),
     'L3_attn_q_gain': (1.0, 0.6),
     'L3_attn_attn_scale': (1.0, 0.6),
     'L3_attn_a_mlp_scale': (1.0, 0.6),
     'L3_ffn_bq': (0.0, 0.8),
     'L3_ffn_bk': (0.0, 0.8),
     'L3_ffn_bv': (0.0, 0.1),
     'L3_ffn_bo': (0.0, 0.1),
     'L3_ffn_bg': (0.0, 0.566),
     'L3_ffn_b1': (0.0, 0.523),
     'L3_ffn_b2': (0.0, 0.353)}
    factors = {'L0_attn_Wq': 8.0,
     'L0_attn_Wk': 8.0,
     'L0_ffn_gate_w': 6.711,
     'L0_ffn_Wg': 6.651,
     'L0_ffn_Wu': 7.316,
     'L0_ffn_Wd': 7.5,
     'L1_attn_W_dt': 8.0,
     'L2_attn_Wq': 6.182,
     'L2_attn_Wk': 6.1,
     'L2_attn_Wb': 8.0,
     'L2_attn_conv_q': 6.286,
     'L2_attn_conv_k': 6.189,
     'L2_attn_fir_long': 8.0,
     'L2_attn_fir_short': 8.0,
     'L2_attn_W1': 8.0,
     'L2_attn_W2': 8.0,
     'L2_ffn_b1': 8.0,
     'L2_ffn_b2': 2.72,
     'L3_attn_in_proj_w': 8.0,
     'L3_attn_conv_w': 8.0,
     'L3_attn_B_proj_w': 8.0,
     'L3_attn_C_proj_w': 8.0,
     'L3_attn_dt_bias': 8.0,
     'L3_attn_A_log': 8.0,
     'L3_attn_out_proj_w': 8.0,
     'L3_attn_m_fc_w': 5.811,
     'L3_attn_m_proj_w': 5.284,
     'L3_attn_resid_mix_a': 8.0,
     'L3_attn_q_w': 8.0,
     'L3_attn_k_w': 8.0,
     'L3_attn_v_w': 8.0,
     'L3_attn_o_w': 8.0,
     'L3_attn_a_fc_w': 5.652,
     'L3_attn_a_proj_w': 5.236}
    for name, (base, spread) in spreads.items():
        noise = np.random.default_rng([zlib.crc32(name.encode()), seed]).standard_normal(out[name].shape)
        drawn = base * np.exp(spread * noise) if base else spread * noise
        out[name] = jnp.asarray(drawn.astype(out[name].dtype))
    for name, factor in factors.items():
        out[name] = (out[name] * factor).astype(out[name].dtype)
    return out
```

```python
from contextlib import ExitStack

import numpy as np

import concourse.bass as bass
from concourse import mybir

F32 = mybir.dt.float32
BF16 = mybir.dt.bfloat16
I32 = mybir.dt.int32
U32 = mybir.dt.uint32
ALU = mybir.AluOpType
ACT = mybir.ActivationFunctionType
AX = mybir.AxisListType

P = 128
D = 128
SEQ = 256
TOKENS = 2048
GROUPS = 4
GT = TOKENS // GROUPS
T = GT // P
NB = GT // SEQ
ARENA = 16900
PAGE = 8192
STAGE_SEMS = 72


class Own:

    def __init__(self, eng, sem):
        self.eng, self.sem, self.n = eng, sem, 0

    def did(self, ins):
        self.n += 1
        ins.then_inc(self.sem, 1)

    def wait(self):
        if self.n:
            self.eng.wait_ge(self.sem, self.n)

    def step(self, ins):
        self.did(ins)
        self.wait()


class Kit:

    def __init__(self, nc, ctx, columns, width):
        self.nc, self.ctx, self.columns = nc, ctx, columns
        self.W = {"resident": ctx.enter_context(nc.sbuf_tensor("weights_sb", [P, width["resident"]], F32)),
                  "page": ctx.enter_context(nc.sbuf_tensor("weights_page", [P, PAGE], F32))}
        self.page_in = ctx.enter_context(nc.semaphore("page_in"))
        self.arena = ctx.enter_context(nc.sbuf_tensor("arena", [P, ARENA], F32))
        self.x = ctx.enter_context(nc.sbuf_tensor("x_res", [P, T, D], F32))
        self.n = ctx.enter_context(nc.sbuf_tensor("n_tok", [P, T, D], F32))
        self.nT = ctx.enter_context(nc.sbuf_tensor("nT", [P, GT], F32))
        self.identb = ctx.enter_context(nc.sbuf_tensor("ident_bf16", [P, P], BF16))
        self.maskb = ctx.enter_context(nc.sbuf_tensor("mask_bf16", [P, P], BF16))
        self.bank = [ctx.enter_context(nc.psum_tensor(f"bank{i}", [P, 512], F32)) for i in range(8)]
        self.arrived = ctx.enter_context(nc.semaphore("stage_arrived"))
        self.go = {e: ctx.enter_context(nc.semaphore(f"stage_go_{e}")) for e in ("pe", "act", "dve", "pool")}
        self.weights_in = ctx.enter_context(nc.semaphore("weights_in"))
        self.own_sems = {e: ctx.enter_context(nc.semaphore(f"own_{e}")) for e in ("act", "dve", "pool")}
        self.stage_sems = [ctx.enter_context(nc.semaphore(f"of_stage_{i}")) for i in range(STAGE_SEMS)]
        self.first, self.last = self.own_sems["act"].num, self.stage_sems[-1].num
        self.own = {}
        self.stage, self.names = 0, {}

    def sem(self, name):
        names = self.names.setdefault(self.stage, {})
        if name not in names:
            names[name] = self.stage_sems[len(names)]
        return names[name]

    def w(self, name):
        where, at, rows, n = self.columns[name]
        return self.W[where][0:rows, at:at + n]

    def row(self, name, a, b, lo=0, hi=None):
        where, at, rows, n = self.columns[name]
        return self.W[where][lo:rows if hi is None else hi, at + a:at + b]

    def end(self, eng, name):
        self.stage += 1
        eng.drain()
        if name == "sp":
            eng.wait_ge(self.arrived, 4)
            eng.sem_clear(range(self.arrived.num, self.arrived.num + 1))
            eng.sem_clear(range(self.first, self.last + 1))
            for e in self.go:
                eng.sem_inc(self.go[e], 1)
        else:
            eng.sem_inc(self.arrived, 1)
            eng.wait_ge(self.go[name], 1)
            eng.sem_clear(self.go[name])
            if name in self.own:
                self.own[name].n = 0


class Arena:

    def __init__(self, kit):
        self.kit, self.at = kit, 0

    def __call__(self, *shape, rows=P):
        n = int(np.prod(shape))
        v = self.kit.arena[0:rows, self.at:self.at + n]
        self.at += n
        assert self.at <= ARENA, self.at
        if len(shape) == 2:
            v = v.rearrange("p (a b) -> p a b", a=shape[0])
        elif len(shape) == 3:
            v = v.rearrange("p (a b c) -> p a b c", a=shape[0], b=shape[1])
        elif len(shape) == 4:
            v = v.rearrange("p (a b c d) -> p a b c d", a=shape[0], b=shape[1], c=shape[2])
        return v


def over(v, *shape):
    while len(v.shape) < len(shape):
        v = v.unsqueeze(len(v.shape))
    return v.to_broadcast(list(shape))


class Constants:

    def __init__(self, kit):
        self.k = kit

    def vector(self, dve):
        self.k.nc.vector.tensor_copy(self.k.identb[:, :], self.k.w("ident"))
        self.k.nc.vector.tensor_copy(self.k.maskb[:, :], self.k.w("mask_neg"))

    def tensor(self, eng):
        pass

    scalar = gpsimd = sync = tensor


def log1p_coefficients(degree=4):
    x = np.cos((np.arange(degree + 1) + 0.5) * np.pi / (degree + 1))
    z = np.sqrt((x + 1) / 18)
    c = np.polynomial.polynomial.polyfit(z * z, 2 * np.arctanh(z) / z, degree)
    return [float(v) for v in c]


LOG1P = log1p_coefficients()


def softplus(kit, dst, x, e, t1, t2):
    nc, own = kit.nc, kit.own["dve"]
    own.step(nc.vector.tensor_scalar(t1, e, 2.0, None, ALU.add))
    own.step(nc.vector.reciprocal(t2, t1))
    own.step(nc.vector.tensor_tensor(e, e, t2, ALU.mult))
    own.step(nc.vector.tensor_tensor(t1, e, e, ALU.mult))
    own.step(nc.vector.tensor_scalar(t2, t1, LOG1P[-1], None, ALU.mult))
    for c in LOG1P[-2:0:-1]:
        own.step(nc.vector.scalar_tensor_tensor(t2, t2, c, t1, ALU.add, ALU.mult))
    own.step(nc.vector.scalar_tensor_tensor(t2, t2, LOG1P[0], e, ALU.add, ALU.mult))
    return nc.vector.scalar_tensor_tensor(dst, x, 0.0, t2, ALU.max, ALU.add)


class Norm:

    def __init__(self, kit, mem, x, eps, rms=False, tag=""):
        self.k, self.x, self.eps, self.rms, self.tag = kit, x, eps, rms, tag
        self.stats = mem(T, 6)
        self.mv = mem(T, 2)
        self.var = mem(T)
        self.msq = mem(T)
        self.rstd = mem(T)

    def vector(self, dve):
        k, nc, own = self.k, self.k.nc, self.k.own["dve"]
        for t in range(T):
            own.did(nc.vector.bn_stats(self.stats[:, t, :], self.x[:, t, :]))
        own.wait()
        for t in range(T):
            own.did(nc.vector.bn_aggr(self.mv[:, t, :], self.stats[:, t, :]))
        own.wait()
        if self.rms:
            own.step(nc.vector.tensor_tensor(self.msq, self.mv[:, :, 0], self.mv[:, :, 0], ALU.mult))
            own.step(nc.vector.tensor_tensor(self.msq, self.msq, self.mv[:, :, 1], ALU.add))
            last = nc.vector.tensor_scalar(self.var, self.msq, self.eps, None, ALU.add)
        else:
            last = nc.vector.tensor_scalar(self.var, self.mv[:, :, 1], self.eps, None, ALU.add)
        last.then_inc(k.sem("norm_var" + self.tag), 1)
        dve.wait_ge(k.sem("norm_rstd" + self.tag), 1)
        for t in range(T):
            if self.rms:
                ins = nc.vector.tensor_scalar(k.n[:, t, :], self.x[:, t, :], self.rstd[:, t:t + 1], None, ALU.mult)
            else:
                ins = nc.vector.tensor_scalar(k.n[:, t, :], self.x[:, t, :], self.mv[:, t, 0:1],
                                              self.rstd[:, t:t + 1], ALU.subtract, ALU.mult)
            ins.then_inc(k.sem("norm_n" + self.tag), 1)

    def gpsimd(self, pool):
        k, nc = self.k, self.k.nc
        pool.wait_ge(k.sem("norm_var" + self.tag), 1)
        nc.gpsimd.tensor_tensor(self.rstd, self.var, k.row("minus_half", 0, T), ALU.pow)\
            .then_inc(k.sem("norm_rstd" + self.tag), 1)

    def tensor(self, pe, bank):
        k, nc = self.k, self.k.nc
        for t in range(T):
            pe.wait_ge(k.sem("norm_n" + self.tag), t + 1)
            ins = nc.tensor.transpose(bank[:, t * P:(t + 1) * P], k.n[:, t, :], k.w("ident"))
        ins.then_inc(k.sem("norm_turned" + self.tag), 1)

    def scalar(self, act, bank):
        k, nc = self.k, self.k.nc
        act.wait_ge(k.sem("norm_turned" + self.tag), 1)
        nc.scalar.copy(k.nT[:, :], bank[:, :]).then_inc(k.sem("nT" + self.tag), 1)


class Mlp:

    def __init__(self, kit, mem, src, units, per, kind, func, first, down, second=None, bias1=None, bias2=None,
                 use=None, extra=None, tag=""):
        self.k, self.src, self.U, self.per, self.kind, self.func = kit, src, units, per, kind, func
        self.first, self.second, self.down = first, second, down
        self.bias1, self.bias2, self.use, self.extra, self.tag = bias1, bias2, use, extra, tag
        self.a = [mem(GT) for _ in range(2)]
        self.h = [mem(GT) for _ in range(2)]
        self.E = units // per

    def s(self, name):
        return self.k.sem(name + self.tag)

    def y(self, e):
        return self.k.bank[4 + e % 2]

    def tensor(self, pe):
        k, nc = self.k, self.k.nc

        def up(u):
            if u >= 2:
                pe.wait_ge(self.s("h_ready"), u - 1)
            ins = nc.tensor.matmul(k.bank[u % 2][:, :], self.first(u), self.src[:, :], start=True, stop=True)
            if self.kind == "gated":
                ins = nc.tensor.matmul(k.bank[2 + u % 2][:, :], self.second(u), self.src[:, :], start=True, stop=True)
            ins.then_inc(self.s("up_ready"), 1)

        def down(u):
            e, i = divmod(u, self.per)
            pe.wait_ge(self.s("h_ready"), u + 1)
            if i == 0 and e >= 2:
                pe.wait_ge(self.s("y_used"), e - 1)
            last = i == self.per - 1
            for t in range(T):
                out = self.y(e)[:, t * D:(t + 1) * D]
                ins = nc.tensor.matmul(out, self.h[u % 2][:, t * P:(t + 1) * P], self.down(u),
                                       start=(i == 0 and t == 0), stop=last and not self.extra,
                                       skip_group_check=True)
                if last and self.extra:
                    ins = nc.tensor.matmul(out, self.extra[0], self.extra[1], start=False, stop=True,
                                           skip_group_check=True)
            ins.then_inc(self.s("down_done"), 1)

        up(0)
        for u in range(self.U):
            if u + 1 < self.U:
                up(u + 1)
            down(u)

    def scalar(self, act):
        k, nc = self.k, self.k.nc
        for u in range(self.U):
            act.wait_ge(self.s("up_ready"), u + 1)
            kw = {"bias": self.bias1(u)} if self.bias1 else {}
            if self.kind == "plain":
                if u >= 2:
                    act.wait_ge(self.s("down_done"), u - 1)
                nc.scalar.activation(self.h[u % 2], k.bank[u % 2][:, :], self.func, **kw)\
                    .then_inc(self.s("h_ready"), 1)
            else:
                if u >= 2:
                    act.wait_ge(self.s("h_ready"), u - 1)
                nc.scalar.activation(self.a[u % 2], k.bank[u % 2][:, :], self.func, **kw)\
                    .then_inc(self.s("a_ready"), 1)

    def vector(self, dve):
        k, nc = self.k, self.k.nc
        for u in range(self.U):
            if self.kind != "plain":
                dve.wait_ge(self.s("a_ready"), u + 1)
                if u >= 2:
                    dve.wait_ge(self.s("down_done"), u - 1)
                if self.kind == "square":
                    ins = nc.vector.tensor_tensor(self.h[u % 2], self.a[u % 2], self.a[u % 2], ALU.mult)
                elif self.bias2:
                    ins = nc.vector.scalar_tensor_tensor(self.h[u % 2], k.bank[2 + u % 2][:, :], self.bias2(u),
                                                         self.a[u % 2], ALU.add, ALU.mult)
                else:
                    ins = nc.vector.tensor_tensor(self.h[u % 2], k.bank[2 + u % 2][:, :], self.a[u % 2], ALU.mult)
                ins.then_inc(self.s("h_ready"), 1)
            e, i = divmod(u, self.per)
            if i == 1 and e >= 1:
                self.take(dve, e - 1)
        self.take(dve, self.E - 1)

    def take(self, dve, e):
        dve.wait_ge(self.s("down_done"), self.per * (e + 1))
        self.use(e, self.y(e)).then_inc(self.s("y_used"), 1)


class Router:

    def __init__(self, kit, mem, srcT, prefix, top2, half):
        self.k, self.srcT, self.pre, self.top2, self.half = kit, srcT, prefix, top2, half
        self.E = 8
        self.z = mem(T, self.E)
        self.mx = mem(T)
        self.sum = mem(T)
        self.rec = mem(T)
        self.p = mem(T, self.E)
        self.probs = mem(T, self.E)
        self.m8 = mem(T, 8)
        self.i8 = mem(T * 8)
        self.i2 = mem(T, 2)
        self.m = [mem(T, self.E) for _ in range(3)]
        self.pT = mem(GT, rows=self.E)

    def tensor(self, pe):
        k, nc, E = self.k, self.k.nc, self.E
        lg, tr, bi = k.bank[6], k.bank[7], k.bank[6]
        for t in range(T):
            ins = nc.tensor.matmul(lg[:, t * E:(t + 1) * E], self.srcT[:, t * P:(t + 1) * P],
                                   k.w(self.pre + "router"), start=True, stop=True)
        ins.then_inc(k.sem("logits"), 1)

    def tensor_bias(self, pe):
        k, nc, E = self.k, self.k.nc, self.E
        tr, bi = k.bank[7], k.bank[6]
        pe.wait_ge(k.sem("probs"), 1)
        for t in range(T):
            ins = nc.tensor.transpose(tr[0:E, t * P:(t + 1) * P], self.probs[:, t, :], k.w("ident"))
        ins.then_inc(k.sem("probs_turned"), 1)
        pe.wait_ge(k.sem("probsT"), 1)
        for t in range(T):
            ins = nc.tensor.matmul(bi[:, t * D:(t + 1) * D], self.pT[:, t * P:(t + 1) * P],
                                   k.w(self.pre + "down_b"), start=True, stop=True)
        ins.then_inc(k.sem("down_bias"), 1)

    def scalar(self, act):
        k, nc = self.k, self.k.nc
        act.wait_ge(k.sem("logits_shifted"), 1)
        nc.scalar.activation(self.p, self.z, ACT.Exp).then_inc(k.sem("router_exp"), 1)

    def scalar_turn(self, act):
        k, nc = self.k, self.k.nc
        act.wait_ge(k.sem("probs_turned"), 1)
        nc.scalar.copy(self.pT, k.bank[7][0:self.E, :]).then_inc(k.sem("probsT"), 1)

    def vector(self, dve):
        k, nc, E, own = self.k, self.k.nc, self.E, self.k.own["dve"]
        lg = k.bank[6][:, 0:T * E].rearrange("p (t e) -> p t e", t=T)
        dve.wait_ge(k.sem("logits"), 1)
        if self.pre == "L3f_":
            own.step(nc.vector.tensor_tensor(self.z, lg, k.w("L3f_bg").unsqueeze(1).to_broadcast([P, T, E]), ALU.add))
            lg = self.z
        own.step(nc.vector.tensor_reduce(self.mx, lg, AX.X, ALU.max))
        nc.vector.tensor_tensor(self.z, lg, over(self.mx, P, T, E), ALU.subtract)\
            .then_inc(k.sem("logits_shifted"), 1)
        dve.wait_ge(k.sem("router_exp"), 1)
        own.step(nc.vector.tensor_reduce(self.sum, self.p, AX.X, ALU.add))
        own.step(nc.vector.reciprocal(self.rec, self.sum))
        if self.top2:
            own.step(nc.vector.tensor_tensor(self.p, self.p, over(self.rec, P, T, E), ALU.mult))
            for t in range(T):
                own.did(nc.vector.max(self.m8[:, t, :], self.p[:, t, :]))
            own.wait()
            i8 = self.i8.bitcast(U32).rearrange("p (t e) -> p t e", t=T)
            for t in range(T):
                own.did(nc.vector.max_index(i8[:, t, :], self.m8[:, t, :], self.p[:, t, :]))
            own.wait()
            own.step(nc.vector.tensor_copy(self.i2, i8[:, :, 0:2]))
            iota = k.w("iota8").unsqueeze(1).to_broadcast([P, T, E])
            for j in range(2):
                own.did(nc.vector.tensor_tensor(self.m[j], iota, self.i2[:, :, j:j + 1].to_broadcast([P, T, E]),
                                                ALU.is_equal))
            own.wait()
            own.step(nc.vector.tensor_tensor(self.m[2], self.m[0], self.m[1], ALU.add))
            own.step(nc.vector.tensor_tensor(self.p, self.p, self.m[2], ALU.mult))
            own.step(nc.vector.tensor_reduce(self.sum, self.p, AX.X, ALU.add))
            own.step(nc.vector.tensor_scalar(self.sum, self.sum, 1e-9, None, ALU.add))
            own.step(nc.vector.reciprocal(self.rec, self.sum))
        own.step(nc.vector.tensor_scalar(self.rec, self.rec, self.half, None, ALU.mult))
        nc.vector.tensor_tensor(self.probs, self.p, over(self.rec, P, T, E), ALU.mult).then_inc(k.sem("probs"), 1)

    def vector_bias(self, dve):
        k, nc = self.k, self.k.nc
        dve.wait_ge(k.sem("down_bias"), 1)
        own = self.k.own["dve"]
        own.step(nc.vector.tensor_tensor(k.x[:, :, :], k.x[:, :, :],
                                         k.bank[6][:, :].rearrange("p (t d) -> p t d", t=T), ALU.add))

    def use(self, e, y):
        k, nc = self.k, self.k.nc
        if e:
            k.nc.vector.wait_ge(k.sem("y_used"), e)
        for t in range(T):
            ins = nc.vector.scalar_tensor_tensor(k.x[:, t, :], y[:, t * D:(t + 1) * D], self.probs[:, t, e:e + 1],
                                                 k.x[:, t, :], ALU.mult, ALU.add)
        return ins


class L1Ffn:

    def __init__(self, kit):
        self.k = kit
        mem = Arena(kit)
        self.norm = Norm(kit, mem, kit.x, 1e-5)
        self.router = Router(kit, mem, kit.nT, "L1f_", True, 0.5)
        self.mlp = Mlp(kit, mem, kit.nT, 16, 2, "gated", ACT.Silu,
                       first=lambda u: kit.row("L1f_gate", u * P, (u + 1) * P),
                       second=lambda u: kit.row("L1f_up", u * P, (u + 1) * P),
                       down=lambda u: kit.row("L1f_down", u * D, (u + 1) * D),
                       bias1=lambda u: kit.row("L1f_gate_b", u, u + 1),
                       bias2=lambda u: kit.row("L1f_up_b", u, u + 1), use=self.router.use)

    def tensor(self, pe):
        self.norm.tensor(pe, self.k.bank[7])
        pe.wait_ge(self.k.sem("nT"), 1)
        self.router.tensor(pe)
        self.router.tensor_bias(pe)
        self.mlp.tensor(pe)

    def scalar(self, act):
        self.norm.scalar(act, self.k.bank[7])
        self.router.scalar(act)
        self.router.scalar_turn(act)
        self.mlp.scalar(act)

    def vector(self, dve):
        self.norm.vector(dve)
        self.router.vector(dve)
        self.router.vector_bias(dve)
        self.mlp.vector(dve)

    def gpsimd(self, pool):
        self.norm.gpsimd(pool)

    def sync(self, sp):
        pass


class Binarise:

    def __init__(self, kit):
        self.k = kit
        mem = Arena(kit)
        self.sgn = mem(2, 4, D)
        self.alpha = mem(8)
        self.q = mem(2, 4, D)
        self.bw1T = kit.ctx.enter_context(kit.nc.sbuf_tensor("bw1T", [P, 512], F32))
        self.bw2T = kit.ctx.enter_context(kit.nc.sbuf_tensor("bw2T", [P, 512], F32))

    def scalar(self, act):
        k, nc = self.k, self.k.nc
        for i, name in enumerate(("L2f_w1", "L2f_w2")):
            nc.scalar.activation(self.sgn[:, i], k.w(name).rearrange("p (a b) -> p a b", a=4), ACT.Sign)\
                .then_inc(k.sem("sign"), 1)
        for i, dst in enumerate((self.bw1T, self.bw2T)):
            act.wait_ge(k.sem("bw_turned"), i + 1)
            nc.scalar.copy(dst[:, :], k.bank[i][:, :]).then_inc(k.sem("bw_kept"), 1)
        act.wait_ge(k.sem("bw_kept"), 2)

    def vector(self, dve):
        k, nc, own = self.k, self.k.nc, self.k.own["dve"]
        w1 = k.w("L2f_w1").rearrange("p (a b) -> p a b", a=4)
        w2 = k.w("L2f_w2").rearrange("p (a b) -> p a b", a=4)
        dve.wait_ge(k.sem("sign"), 2)
        own.did(nc.vector.tensor_reduce(self.alpha[:, 0:4], w1, AX.X, ALU.add, apply_absolute_value=True))
        own.did(nc.vector.tensor_reduce(self.alpha[:, 4:5], w2, AX.XY, ALU.add, apply_absolute_value=True))
        own.wait()
        own.did(nc.vector.tensor_scalar(self.alpha[:, 0:4], self.alpha[:, 0:4], 1.0 / 128, None, ALU.mult))
        own.did(nc.vector.tensor_scalar(self.alpha[:, 4:5], self.alpha[:, 4:5], 1.0 / 512, None, ALU.mult))
        own.wait()
        for i, w in enumerate((w1, w2)):
            a = over(self.alpha[:, 0:4], P, 4, D) if i == 0 else over(self.alpha[:, 4:5], P, 4, D)
            q = self.q[:, i]
            own.step(nc.vector.tensor_tensor(q, self.sgn[:, i], a, ALU.mult))
            own.step(nc.vector.tensor_tensor(q, q, w, ALU.subtract))
            nc.vector.tensor_tensor(q, q, w, ALU.add).then_inc(k.sem("binary"), 1)

    def tensor(self, pe):
        k, nc = self.k, self.k.nc
        for i in range(2):
            pe.wait_ge(k.sem("binary"), i + 1)
            for j in range(4):
                ins = nc.tensor.transpose(k.bank[i][:, j * P:(j + 1) * P], self.q[:, i, j, :], k.w("ident"))
            ins.then_inc(k.sem("bw_turned"), 1)

    def gpsimd(self, pool):
        pass

    def sync(self, sp):
        pass


class L2Ffn:

    def __init__(self, kit, binary):
        self.k = kit
        mem = Arena(kit)
        self.norm = Norm(kit, mem, kit.x, 1e-5)
        self.mlp = Mlp(kit, mem, kit.nT, 4, 4, "plain", ACT.Gelu,
                       first=lambda u: binary.bw1T[:, u * P:(u + 1) * P],
                       down=lambda u: binary.bw2T[:, u * P:(u + 1) * P],
                       bias1=lambda u: kit.row("L2f_b1", u, u + 1),
                       extra=(kit.row("ones", 0, P, hi=1), kit.w("L2f_b2")), use=self.use)

    def use(self, e, y):
        k = self.k
        return k.nc.vector.scalar_tensor_tensor(k.x[:, :, :], y[:, :].rearrange("p (t d) -> p t d", t=T), 0.5,
                                                k.x[:, :, :], ALU.mult, ALU.add)

    def tensor(self, pe):
        self.norm.tensor(pe, self.k.bank[7])
        pe.wait_ge(self.k.sem("nT"), 1)
        self.mlp.tensor(pe)

    def scalar(self, act):
        self.norm.scalar(act, self.k.bank[7])
        self.mlp.scalar(act)

    def vector(self, dve):
        self.norm.vector(dve)
        self.mlp.vector(dve)

    def gpsimd(self, pool):
        self.norm.gpsimd(pool)

    def sync(self, sp):
        pass


class L3Ffn:

    def __init__(self, kit):
        self.k = kit
        mem = Arena(kit)
        self.norm = Norm(kit, mem, kit.x, 1e-5)
        self.qT, self.kT, self.aT = mem(GT), mem(GT), mem(GT)
        self.v = mem(T, D)
        self.mx, self.sum, self.rec = mem(T), mem(T), mem(T)
        self.p = mem(NB, 2, SEQ)
        self.pT = mem(NB, 2, SEQ)
        self.router = Router(kit, mem, kit.nT, "L3f_", False, 0.5)
        self.mlp = Mlp(kit, mem, kit.nT, 32, 4, "plain", ACT.Relu,
                       first=lambda u: kit.row("L3f_W1", u * P, (u + 1) * P),
                       down=lambda u: kit.row("L3f_W2", u * D, (u + 1) * D),
                       bias1=lambda u: kit.row("L3f_b1", u, u + 1), use=self.router.use)

    SCALE = float(np.float32(1.0 / np.sqrt(128)))

    def tensor(self, pe):
        k, nc, b = self.k, self.k.nc, self.k.bank
        ones = k.row("ones", 0, P, hi=1)
        self.norm.tensor(pe, b[7])
        pe.wait_ge(k.sem("nT"), 1)
        nc.tensor.matmul(b[0][:, :], k.w("L3f_Wq"), k.nT[:, :], start=True, stop=True).then_inc(k.sem("q_made"), 1)
        nc.tensor.matmul(b[1][:, :], k.w("L3f_Wk"), k.nT[:, :], start=True, stop=True).then_inc(k.sem("k_made"), 1)
        for t in range(T):
            o = b[2][:, t * D:(t + 1) * D]
            nc.tensor.matmul(o, k.nT[:, t * P:(t + 1) * P], k.w("L3f_Wv"), start=True, stop=False)
            ins = nc.tensor.matmul(o, ones, k.w("L3f_bv"), start=False, stop=True)
        ins.then_inc(k.sem("v_made"), 1)
        pe.wait_ge(k.sem("qk_kept"), 2)
        for s in range(NB):
            for i in range(2):
                ins = nc.tensor.matmul(b[3 + s][:, i * SEQ:(i + 1) * SEQ],
                                       self.qT[:, s * SEQ + i * P:s * SEQ + (i + 1) * P],
                                       self.kT[:, s * SEQ:(s + 1) * SEQ], start=True, stop=True)
            ins.then_inc(k.sem("scores"), 1)
        for s in range(NB):
            pe.wait_ge(k.sem("p_normal"), s + 1)
            for j in range(2):
                for i in range(2):
                    ins = nc.tensor.transpose(b[5 + s][:, j * SEQ + i * P:j * SEQ + (i + 1) * P],
                                              self.p[:, s, i, j * P:(j + 1) * P], k.w("ident"))
            ins.then_inc(k.sem("p_turned"), 1)
        pe.wait_ge(k.sem("v_kept"), 1)
        for s in range(NB):
            pe.wait_ge(k.sem("pT"), s + 1)
            for j in range(2):
                ins = nc.tensor.matmul(b[0][:, s * SEQ:(s + 1) * SEQ], self.v[:, 2 * s + j, :], self.pT[:, s, j, :],
                                       start=(j == 0), stop=(j == 1))
        ins.then_inc(k.sem("a_made"), 1)
        pe.wait_ge(k.sem("aT"), 1)
        for t in range(T):
            o = b[1][:, t * D:(t + 1) * D]
            nc.tensor.matmul(o, self.aT[:, t * P:(t + 1) * P], k.w("L3f_Wo"), start=True, stop=False)
            ins = nc.tensor.matmul(o, ones, k.w("L3f_bo"), start=False, stop=True)
        ins.then_inc(k.sem("attn_out"), 1)
        pe.wait_ge(k.sem("x1"), 1)
        for t in range(T):
            ins = nc.tensor.transpose(b[7][:, t * P:(t + 1) * P], k.n[:, t, :], k.w("ident"))
        ins.then_inc(k.sem("x1_turned"), 1)
        pe.wait_ge(k.sem("x1T"), 1)
        self.router.tensor(pe)
        self.router.tensor_bias(pe)
        self.mlp.tensor(pe)

    def scalar(self, act):
        k, nc, b = self.k, self.k.nc, self.k.bank
        self.norm.scalar(act, b[7])
        act.wait_ge(k.sem("q_made"), 1)
        nc.scalar.activation(self.qT, b[0][:, :], ACT.Identity, bias=k.w("L3f_bq")).then_inc(k.sem("qk_kept"), 1)
        for s in range(NB):
            act.wait_ge(k.sem("neg_max"), s + 1)
            for i in range(2):
                c = 2 * s + i
                ins = nc.scalar.activation(self.p[:, s, i, :], b[3 + s][:, i * SEQ:(i + 1) * SEQ], ACT.Exp,
                                           bias=self.mx[:, c:c + 1], scale=self.SCALE,
                                           accum_out=self.sum[:, c:c + 1])
            ins.then_inc(k.sem("p_exp"), 1)
        for s in range(NB):
            act.wait_ge(k.sem("p_turned"), s + 1)
            nc.scalar.copy(self.pT[:, s, :, :], b[5 + s][:, :].rearrange("p (j q) -> p j q", j=2))\
                .then_inc(k.sem("pT"), 1)
        act.wait_ge(k.sem("a_made"), 1)
        nc.scalar.copy(self.aT, b[0][:, :]).then_inc(k.sem("aT"), 1)
        act.wait_ge(k.sem("x1_turned"), 1)
        nc.scalar.copy(k.nT[:, :], b[7][:, :]).then_inc(k.sem("x1T"), 1)
        self.router.scalar(act)
        self.router.scalar_turn(act)
        self.mlp.scalar(act)

    def vector(self, dve):
        k, nc, b, own = self.k, self.k.nc, self.k.bank, self.k.own["dve"]
        self.norm.vector(dve)
        dve.wait_ge(k.sem("k_made"), 1)
        nc.vector.tensor_scalar(self.kT, b[1][:, :], k.w("L3f_bk"), None, ALU.add).then_inc(k.sem("qk_kept"), 1)
        dve.wait_ge(k.sem("v_made"), 1)
        nc.vector.tensor_copy(self.v, b[2][:, :].rearrange("p (t d) -> p t d", t=T)).then_inc(k.sem("v_kept"), 1)
        for s in range(NB):
            m = self.mx[:, 2 * s:2 * s + 2]
            dve.wait_ge(k.sem("scores"), s + 1)
            own.step(nc.vector.tensor_reduce(m, b[3 + s][:, :].rearrange("p (i q) -> p i q", i=2), AX.X, ALU.max))
            nc.vector.tensor_scalar(m, m, -self.SCALE, None, ALU.mult).then_inc(k.sem("neg_max"), 1)
        for s in range(NB):
            dve.wait_ge(k.sem("p_exp"), s + 1)
            own.step(nc.vector.reciprocal(self.rec[:, 2 * s:2 * s + 2], self.sum[:, 2 * s:2 * s + 2]))
            nc.vector.tensor_tensor(self.p[:, s], self.p[:, s], over(self.rec[:, 2 * s:2 * s + 2], P, 2, SEQ),
                                    ALU.mult).then_inc(k.sem("p_normal"), 1)
        dve.wait_ge(k.sem("attn_out"), 1)
        nc.vector.tensor_tensor(k.n[:, :, :], k.n[:, :, :], b[1][:, :].rearrange("p (t d) -> p t d", t=T), ALU.add)\
            .then_inc(k.sem("x1"), 1)
        dve.wait_ge(k.sem("x1"), 1)
        own.step(nc.vector.scalar_tensor_tensor(k.x[:, :, :], k.n[:, :, :], 0.5, k.x[:, :, :], ALU.mult, ALU.add))
        self.router.vector(dve)
        self.router.vector_bias(dve)
        self.mlp.vector(dve)

    def gpsimd(self, pool):
        self.norm.gpsimd(pool)

    def sync(self, sp):
        pass


def l3ffn_weights(i, tiles, spread):
    f = {n: i["L3_ffn_" + n] for n in ("Wq", "bq", "Wk", "bk", "Wv", "bv", "Wo", "bo", "Wg", "bg", "W1", "b1", "W2", "b2")}
    return {
        "L3f_Wq": f["Wq"], "L3f_Wk": f["Wk"], "L3f_Wv": f["Wv"], "L3f_Wo": f["Wo"],
        "L3f_bq": f["bq"].reshape(P, 1), "L3f_bk": f["bk"].reshape(P, 1),
        "L3f_bv": f["bv"].reshape(1, D), "L3f_bo": f["bo"].reshape(1, D),
        "L3f_router": f["Wg"], "L3f_bg": spread(f["bg"]),
        "L3f_W1": f["W1"].transpose(1, 0, 2).reshape(P, -1),
        "L3f_b1": f["b1"].reshape(-1, P).T,
        "L3f_W2": tiles(f["W2"].reshape(-1, D), D),
        "L3f_down_b": f["b2"],
    }


MORE_WEIGHTS = [l3ffn_weights]


class PrepL1:

    def __init__(self, kit):
        self.k = kit

        def keep(name):
            return kit.ctx.enter_context(kit.nc.sbuf_tensor(name, [P, 16], F32))
        self.e, self.A, self.small, self.rest, self.den, self.inv = [
            keep("l1_" + n) for n in ("exp_alog", "A", "small", "rest", "den", "inv")]

    def scalar(self, act):
        self.k.nc.scalar.activation(self.e[:, :], self.k.w("L1a_A_log"), ACT.Exp).then_inc(self.k.sem("exp_alog"), 1)

    def vector(self, dve):
        nc, own = self.k.nc, self.k.own["dve"]
        dve.wait_ge(self.k.sem("exp_alog"), 1)
        own.step(nc.vector.tensor_scalar(self.A[:, :], self.e[:, :], -1.0, None, ALU.mult))
        own.step(nc.vector.tensor_scalar(self.small[:, :], self.A[:, :], -1e-5, None, ALU.is_gt))
        own.did(nc.vector.tensor_scalar(self.rest[:, :], self.small[:, :], -1.0, 1.0, ALU.mult, ALU.add))
        own.step(nc.vector.tensor_scalar(self.den[:, :], self.A[:, :], 1e-10, None, ALU.add))
        own.step(nc.vector.tensor_tensor(self.den[:, :], self.den[:, :], self.rest[:, :], ALU.mult))
        own.step(nc.vector.tensor_tensor(self.den[:, :], self.den[:, :], self.small[:, :], ALU.add))
        own.step(nc.vector.reciprocal(self.inv[:, :], self.den[:, :]))

    def tensor(self, pe):
        pass

    gpsimd = sync = tensor


class L1Attn:

    N = 16

    def __init__(self, kit, prep):
        self.k, self.prep = kit, prep
        mem = Arena(kit)
        self.norm = Norm(kit, mem, kit.x, 1e-5)
        self.pad = mem(NB, 3 + SEQ)
        self.dtu = mem(GT, rows=64)
        self.C = mem(GT, rows=16)
        self.xb, self.ab, self.e, self.lnw, self.w, self.q, self.dt = [mem(GT) for _ in range(7)]
        self.conv = [mem(NB, SEQ) for _ in range(2)]
        self.u, self.zs, self.dtxu, self.g = [mem(GT) for _ in range(4)]
        self.a = [mem(NB, SEQ + 1) for _ in range(3)]
        self.v = [mem(NB, SEQ + 1) for _ in range(3)]
        self.u_rest = [mem(GT) for _ in range(2)]
        self.u_small = [mem(GT) for _ in range(2)]
        self.h = [mem(NB, SEQ + 1) for _ in range(2)]
        self.hc = [mem(GT) for _ in range(2)]

    @staticmethod
    def two(v):
        return v.rearrange("p (b s) -> p b s", b=NB)

    def tensor(self, pe):
        k, nc, b = self.k, self.k.nc, self.k.bank
        self.norm.tensor(pe, b[7])
        pe.wait_ge(k.sem("nT"), 1)
        nc.tensor.matmul(b[1][0:64, :], k.w("L1a_Wdtu"), k.nT[:, :], start=True, stop=True).then_inc(k.sem("dtu_made"), 1)
        nc.tensor.matmul(b[2][0:16, :], k.w("L1a_WC"), k.nT[:, :], start=True, stop=True).then_inc(k.sem("C_made"), 1)
        nc.tensor.matmul(b[0][:, :], k.w("L1a_Wz"), k.nT[:, :], start=True, stop=True).then_inc(k.sem("z_made"), 1)
        pe.wait_ge(k.sem("dtu"), 1)
        nc.tensor.matmul(b[3][:, :], k.w("L1a_Wdt"), self.dtu, start=True, stop=True).then_inc(k.sem("dt_made"), 1)
        pe.wait_ge(k.sem("C"), 1)
        for n in range(self.N + 1):
            if n < self.N:
                if n >= 2:
                    pe.wait_ge(k.sem("hc"), n - 1)
                nc.tensor.matmul(b[5 + n % 2][:, :], k.row("sel16", n * P, (n + 1) * P), self.C,
                                 start=True, stop=True).then_inc(k.sem("C_row"), 1)
            if n >= 1:
                pe.wait_ge(k.sem("hc"), n)
                nc.tensor.matmul(b[4][:, :], k.w("ident"), self.hc[(n - 1) % 2], start=(n == 1), stop=(n == self.N),
                                 skip_group_check=True).then_inc(k.sem("y_sum"), 1)
        pe.wait_ge(k.sem("gated"), 1)
        for t in range(T):
            ins = nc.tensor.matmul(b[0][:, t * D:(t + 1) * D], self.g[:, t * P:(t + 1) * P], k.w("L1a_Wout"),
                                   start=True, stop=True)
        ins.then_inc(k.sem("out_made"), 1)

    def scalar(self, act):
        k, nc, b = self.k, self.k.nc, self.k.bank
        self.norm.scalar(act, b[7])
        act.wait_ge(k.sem("dtu_made"), 1)
        nc.scalar.copy(self.dtu, b[1][0:64, :]).then_inc(k.sem("dtu"), 1)
        act.wait_ge(k.sem("z_made"), 1)
        nc.scalar.activation(self.zs, b[0][:, :], ACT.Silu).then_inc(k.sem("z_silu"), 1)
        act.wait_ge(k.sem("conv"), 4)
        nc.scalar.activation(self.two(self.u), self.conv[1], ACT.Silu).then_inc(k.sem("u"), 1)
        act.wait_ge(k.sem("dt_x"), 1)
        nc.scalar.activation(self.ab, self.xb, ACT.Abs).then_inc(k.sem("dt_abs"), 1)
        act.wait_ge(k.sem("dt_abs"), 1)
        nc.scalar.activation(self.e, self.ab, ACT.Exp, scale=-1.0).then_inc(k.sem("dt_exp"), 1)
        act.wait_ge(k.sem("dt"), 1)
        act.wait_ge(k.sem("pads"), 1)
        act.wait_ge(k.sem("dt_u"), 1)
        for n in range(self.N):
            if n >= 3:
                act.wait_ge(k.sem("scan"), n - 2)
            nc.scalar.activation(self.a[n % 3][:, :, 1:], self.two(self.dt), ACT.Exp,
                                 scale=self.prep.A[:, n:n + 1]).then_inc(k.sem("decay"), 1)
            if n >= 2:
                act.wait_ge(k.sem("drive"), n - 1)
            nc.scalar.activation(self.u_rest[n % 2], self.u, ACT.Copy, scale=self.prep.rest[:, n:n + 1])\
                .then_inc(k.sem("u_rest"), 1)
            if n >= 2:
                act.wait_ge(k.sem("drive_full"), n - 1)
            nc.scalar.activation(self.u_small[n % 2], self.dtxu, ACT.Copy, scale=self.prep.small[:, n:n + 1])\
                .then_inc(k.sem("u_small"), 1)

    def vector(self, dve):
        k, nc, b, own = self.k, self.k.nc, self.k.bank, self.k.own["dve"]
        nc.vector.memset(self.pad[:, :, 0:3], 0.0)
        for i in range(3):
            ins = nc.vector.memset(self.a[i][:, :, 0:1], 0.0)
        ins.then_inc(k.sem("pads"), 1)
        self.norm.vector(dve)
        dve.wait_ge(k.sem("C_made"), 1)
        nc.vector.tensor_copy(self.C, b[2][0:16, :]).then_inc(k.sem("C"), 1)
        dve.wait_ge(k.sem("nT"), 1)
        own.step(nc.vector.tensor_copy(self.pad[:, :, 3:], self.two(k.nT[:, :])))
        for j in range(4):
            src = self.pad[:, :, j:j + SEQ]
            w = k.row("L1a_conv", j, j + 1)
            dst = self.conv[j % 2]
            if j == 0:
                ins = nc.vector.tensor_scalar(dst, src, w, None, ALU.mult)
            else:
                dve.wait_ge(k.sem("conv"), j)
                ins = nc.vector.scalar_tensor_tensor(dst, src, w, self.conv[(j + 1) % 2], ALU.mult, ALU.add)
            ins.then_inc(k.sem("conv"), 1)
        dve.wait_ge(k.sem("dt_made"), 1)
        nc.vector.tensor_scalar(self.xb, b[3][:, :], k.w("L1a_b_dt"), None, ALU.add).then_inc(k.sem("dt_x"), 1)
        dve.wait_ge(k.sem("dt_exp"), 1)
        softplus(k, self.dt, self.xb, self.e, self.w, self.q).then_inc(k.sem("dt"), 1)
        dve.wait_ge(k.sem("dt"), 1)
        dve.wait_ge(k.sem("u"), 1)
        nc.vector.tensor_tensor(self.dtxu, self.dt, self.u, ALU.mult).then_inc(k.sem("dt_u"), 1)

        def drive(n):
            dve.wait_ge(k.sem("decay"), n + 1)
            dve.wait_ge(k.sem("u_rest"), n + 1)
            if n >= 3:
                dve.wait_ge(k.sem("scan"), n - 2)
            nc.vector.scalar_tensor_tensor(self.v[n % 3][:, :, 1:], self.a[n % 3][:, :, 1:], -1.0,
                                           self.two(self.u_rest[n % 2]), ALU.add, ALU.mult)\
                .then_inc(k.sem("drive"), 1)

        drive(0)
        drive(1)
        for n in range(self.N):
            dve.wait_ge(k.sem("drive_full"), n + 1)
            if n >= 2:
                dve.wait_ge(k.sem("hc"), n - 1)
            nc.vector.tensor_tensor_scan(self.h[n % 2].rearrange("p b s -> p (b s)"),
                                         self.a[n % 3].rearrange("p b s -> p (b s)"),
                                         self.v[n % 3].rearrange("p b s -> p (b s)"), 0.0,
                                         ALU.mult, ALU.add).then_inc(k.sem("scan"), 1)
            if n + 2 < self.N:
                drive(n + 2)
            dve.wait_ge(k.sem("scan"), n + 1)
            dve.wait_ge(k.sem("C_row"), n + 1)
            if n >= 2:
                dve.wait_ge(k.sem("y_sum"), n - 1)
            nc.vector.scalar_tensor_tensor(self.two(self.hc[n % 2]), self.h[n % 2][:, :, 0:SEQ], self.prep.inv[:, n:n + 1],
                                           self.two(b[5 + n % 2][:, :]), ALU.mult, ALU.mult)\
                .then_inc(k.sem("hc"), 1)
        dve.wait_ge(k.sem("y_sum"), self.N)
        own.step(nc.vector.scalar_tensor_tensor(self.xb, self.u, k.w("L1a_D"), b[4][:, :], ALU.mult, ALU.add))
        dve.wait_ge(k.sem("z_silu"), 1)
        nc.vector.tensor_tensor(self.g, self.xb, self.zs, ALU.mult).then_inc(k.sem("gated"), 1)
        dve.wait_ge(k.sem("out_made"), 1)
        nc.vector.tensor_tensor(k.x[:, :, :], k.x[:, :, :], b[0][:, :].rearrange("p (t d) -> p t d", t=T), ALU.add)

    def gpsimd(self, pool):
        k, nc = self.k, self.k.nc
        self.norm.gpsimd(pool)
        for n in range(self.N):
            v = self.v[n % 3]
            pool.wait_ge(k.sem("drive"), n + 1)
            pool.wait_ge(k.sem("u_small"), n + 1)
            nc.gpsimd.tensor_tensor(v[:, :, 1:], v[:, :, 1:], self.two(self.u_small[n % 2]), ALU.add)\
                .then_inc(k.sem("drive_sum"), 1)
            pool.wait_ge(k.sem("drive_sum"), n + 1)
            nc.gpsimd.tensor_copy(v[:, :, 0:1], v[:, :, 1:2]).then_inc(k.sem("drive_full"), 1)

    def sync(self, sp):
        pass


def l1attn_weights(i, tiles, spread):
    wp = i["L1_attn_W_params"]
    return {
        "sel16": np.repeat(np.eye(16, dtype=np.float32), P, 1),
        "L1a_Wz": i["L1_attn_W_z"].T, "L1a_Wdtu": wp[0:64].T, "L1a_WC": wp[80:96].T,
        "L1a_Wdt": i["L1_attn_W_dt"].T, "L1a_b_dt": i["L1_attn_b_dt"].reshape(P, 1),
        "L1a_conv": i["L1_attn_conv_w"].reshape(P, 4), "L1a_A_log": i["L1_attn_A_log"],
        "L1a_D": i["L1_attn_D"].reshape(P, 1), "L1a_Wout": i["L1_attn_W_out"].T,
    }


MORE_WEIGHTS += [l1attn_weights]


class Heads:

    def __init__(self, kit, mem, kvh, prefix, normed, deliver):
        self.k, self.kvh, self.pre, self.normed, self.deliver = kit, kvh, prefix, normed, deliver
        self.nqk = 16 + kvh
        self.wide = (16 + 2 * kvh) * 8
        self.kg = kvh // 4
        self.qkv = mem(T, self.wide)
        self.qk = self.qkv[:, :, 0:self.nqk * 8].rearrange("p t (h c) -> p t h c", c=8)
        if normed:
            self.sq = mem(T, self.nqk, 8)
            self.ms = mem(T, self.nqk)
            self.rs = mem(T, self.nqk)
        self.tmp = [mem(T, self.nqk, 4) for _ in range(4)]
        self.pad = mem(T, self.nqk, 32)
        self.qT = mem(4, GT)
        self.kT = mem(self.kg, GT)
        self.vaug = mem(T, kvh, 9)
        self.neg = mem(4, 2)
        self.p = [mem(3 * P) for _ in range(2)]
        self.pT = [mem(3 * P) for _ in range(2)]
        self.rden = mem(NB, 2, 16)
        self.ctx = mem(T, D)
        self.ctxT = mem(GT)
        self.units = [(s, g, slot) for s in range(NB) for g in range(4) for slot in range(4)]

    def turns(self):
        return [(self.qT[:, g], g, False) for g in range(4)] + [(self.kT[:, g], 4 + g, True) for g in range(self.kg)]

    def tensor(self, pe):
        k, nc, b = self.k, self.k.nc, self.k.bank
        for t in range(T):
            ins = nc.tensor.matmul(b[t][:, 0:self.wide], k.nT[:, t * P:(t + 1) * P], k.w(self.pre + "Wqkv"),
                                   start=True, stop=True)
            ins.then_inc(k.sem("qkv_made"), 1)
        pe.wait_ge(k.sem("padded"), 2)
        for i, (_, g, _) in enumerate(self.turns()):
            if i >= 4:
                pe.wait_ge(k.sem("turned_kept"), i - 3)
            for t in range(T):
                ins = nc.tensor.transpose(b[4 + i % 4][:, t * P:(t + 1) * P],
                                          self.pad[:, t, 4 * g:4 * g + 4, :].rearrange("p h c -> p (h c)"),
                                          k.w("ident"))
            ins.then_inc(k.sem("turned"), 1)
        pe.wait_ge(k.sem("turned_kept"), len(self.turns()))

        def scores(i):
            s, g, slot = self.units[i]
            if i >= 4:
                pe.wait_ge(k.sem("p_exp"), i - 3)
            rows = slice(32 * slot, 32 * slot + 8)
            q = self.qT[rows, g, s * SEQ:(s + 1) * SEQ]
            kk = self.kT[rows, g % self.kg, s * SEQ:(s + 1) * SEQ]
            o = b[slot]
            kw = dict(skip_group_check=True)
            nc.tensor.matmul(o[:, 0:SEQ], q[:, P:SEQ], kk, start=True, stop=False, **kw)
            nc.tensor.matmul(o[:, SEQ:SEQ + P], q[:, 0:P], kk[:, 0:P], start=False, stop=False, **kw)
            nc.tensor.matmul(o[:, P:SEQ], k.identb[:, :], k.maskb[:, :], start=False, stop=False, **kw)
            nc.tensor.matmul(o[:, SEQ:SEQ + P], k.identb[:, :], k.maskb[:, :], start=False, stop=True, **kw)\
                .then_inc(k.sem("scores"), 1)

        def turn(i):
            pe.wait_ge(k.sem("p_exp"), i + 1)
            if i >= 2:
                pe.wait_ge(k.sem("pT"), i - 1)
            for j in range(3):
                ins = nc.tensor.transpose(b[4 + i % 2][:, j * P:(j + 1) * P], self.p[i % 2][:, j * P:(j + 1) * P],
                                          k.w("ident"))
            ins.then_inc(k.sem("p_turned"), 1)

        def mix(i):
            s, g, slot = self.units[i]
            h = 4 * g + slot
            kh = h if self.kvh == 16 else slot
            pe.wait_ge(k.sem("pT"), i + 1)
            o = b[6 + s]
            pT = self.pT[i % 2]
            nc.tensor.matmul(o[:, (16 + h) * 9:(17 + h) * 9], pT[:, 0:P], self.vaug[:, 2 * s, kh, :],
                             start=True, stop=False)
            nc.tensor.matmul(o[:, (16 + h) * 9:(17 + h) * 9], pT[:, P:2 * P], self.vaug[:, 2 * s + 1, kh, :],
                             start=False, stop=True)
            nc.tensor.matmul(o[:, h * 9:(h + 1) * 9], pT[:, 2 * P:3 * P], self.vaug[:, 2 * s, kh, :],
                             start=True, stop=True).then_inc(k.sem("mixed"), 1)

        n = len(self.units)
        scores(0)
        scores(1)
        for i in range(n + 1):
            if i + 2 < n:
                scores(i + 2)
            if i < n:
                turn(i)
            if i >= 1:
                mix(i - 1)
        pe.wait_ge(k.sem("ctx"), 1)
        for t in range(T):
            ins = nc.tensor.transpose(b[0][:, t * P:(t + 1) * P], self.ctx[:, t, :], k.w("ident"))
        ins.then_inc(k.sem("ctx_turned"), 1)
        pe.wait_ge(k.sem("ctxT"), 1)
        for t in range(T):
            ins = nc.tensor.matmul(b[1][:, t * D:(t + 1) * D], self.ctxT[:, t * P:(t + 1) * P],
                                   k.w(self.pre + "Wo"), start=True, stop=True)
        ins.then_inc(k.sem("attn_out"), 1)

    def scalar(self, act):
        k, nc, b = self.k, self.k.nc, self.k.bank
        for t in range(T):
            act.wait_ge(k.sem("qkv_made"), t + 1)
            nc.scalar.copy(self.qkv[:, t, :], b[t][:, 0:self.wide]).then_inc(k.sem("qkv"), 1)
        if self.normed:
            act.wait_ge(k.sem("qkv"), T)
            nc.scalar.activation(self.sq, self.qk, ACT.Square).then_inc(k.sem("qk_squared"), 1)
        for i, (dst, _, is_key) in enumerate(self.turns()):
            act.wait_ge(k.sem("turned"), i + 1)
            src = b[4 + i % 4][:, :]
            ins = nc.scalar.mul(dst, src, float(np.float32(8 ** -0.5))) if is_key else nc.scalar.copy(dst, src)
            ins.then_inc(k.sem("turned_kept"), 1)
        for i, (s, g, slot) in enumerate(self.units):
            act.wait_ge(k.sem("row_max"), i + 1)
            if i >= 2:
                act.wait_ge(k.sem("p_turned"), i - 1)
            nc.scalar.activation(self.p[i % 2][:, 0:SEQ], b[slot][:, 0:SEQ], ACT.Exp, bias=self.neg[:, slot, 0:1])
            nc.scalar.activation(self.p[i % 2][:, SEQ:], b[slot][:, SEQ:SEQ + P], ACT.Exp,
                                 bias=self.neg[:, slot, 1:2]).then_inc(k.sem("p_exp"), 1)
        act.wait_ge(k.sem("ctx_turned"), 1)
        nc.scalar.copy(self.ctxT, b[0][:, :]).then_inc(k.sem("ctxT"), 1)

    def vector(self, dve):
        k, nc, b, own = self.k, self.k.nc, self.k.bank, self.k.own["dve"]
        dve.wait_ge(k.sem("qkv"), T)
        n4 = self.nqk
        v = self.qkv[:, :, n4 * 8:].rearrange("p t (h c) -> p t h c", c=8)
        own.did(nc.vector.tensor_copy(self.vaug[:, :, :, 0:8], v))
        if self.normed:
            dve.wait_ge(k.sem("qk_squared"), 1)
            own.step(nc.vector.tensor_reduce(self.ms, self.sq, AX.X, ALU.add))
            nc.vector.tensor_scalar(self.ms, self.ms, 0.125, float(np.finfo(np.float32).eps), ALU.mult, ALU.add)\
                .then_inc(k.sem("qk_ms"), 1)
            dve.wait_ge(k.sem("qk_rs"), 1)
            own.step(nc.vector.tensor_tensor(self.rs[:, :, 0:16], self.rs[:, :, 0:16],
                                             k.w(self.pre + "q_gain").unsqueeze(1).to_broadcast([P, T, 16]), ALU.mult))
            own.step(nc.vector.tensor_tensor(self.qk, self.qk, over(self.rs, P, T, n4, 8), ALU.mult))
            x1, x2 = self.qk[:, :, :, 0:4], self.qk[:, :, :, 4:8]
        else:
            x1, x2 = self.qk[:, :, :, 0:8:2], self.qk[:, :, :, 1:8:2]
        cos, sin = [k.w(n).rearrange("p (t c) -> p t c", t=T).unsqueeze(2).to_broadcast([P, T, n4, 4])
                    for n in ("rope_cos", "rope_sin")]
        A, B, C, E = self.tmp
        own.did(nc.vector.tensor_tensor(A, x1, cos, ALU.mult))
        own.did(nc.vector.tensor_tensor(B, x2, sin, ALU.mult))
        own.did(nc.vector.tensor_tensor(C, x1, sin, ALU.mult))
        own.step(nc.vector.tensor_tensor(E, x2, cos, ALU.mult))
        dve.wait_ge(k.sem("pad_clear"), 1)
        lo, hi = self.pad[:, :, :, 0:4], self.pad[:, :, :, 4:8]
        if self.normed:
            i1 = nc.vector.tensor_tensor(lo, A, B, ALU.add)
            i2 = nc.vector.tensor_tensor(hi, E, C, ALU.subtract)
        else:
            i1 = nc.vector.tensor_tensor(lo, A, B, ALU.subtract)
            i2 = nc.vector.tensor_tensor(hi, C, E, ALU.add)
        i1.then_inc(k.sem("padded"), 1)
        i2.then_inc(k.sem("padded"), 1)

        def keep_pT(i):
            dve.wait_ge(k.sem("p_turned"), i + 1)
            if i >= 2:
                dve.wait_ge(k.sem("mixed"), i - 1)
            nc.vector.tensor_copy(self.pT[i % 2], b[4 + i % 2][:, 0:3 * P]).then_inc(k.sem("pT"), 1)

        n = len(self.units)
        for i in range(n + 1):
            if i < n:
                slot = self.units[i][2]
                dve.wait_ge(k.sem("scores"), i + 1)
                if i >= 4:
                    dve.wait_ge(k.sem("p_exp"), i - 3)
                nc.vector.tensor_reduce(self.neg[:, slot, 0:1], b[slot][:, 0:SEQ], AX.X, ALU.max, negate=True)
                nc.vector.tensor_reduce(self.neg[:, slot, 1:2], b[slot][:, SEQ:SEQ + P], AX.X, ALU.max, negate=True)\
                    .then_inc(k.sem("row_max"), 1)
            if i >= 1:
                keep_pT(i - 1)
        dve.wait_ge(k.sem("mixed"), n)
        for s in range(NB):
            o = b[6 + s][:, 0:288].rearrange("p (i h c) -> p i h c", i=2, c=9)
            own.did(nc.vector.reciprocal(self.rden[:, s], o[:, :, :, 8]))
        own.wait()
        for s in range(NB):
            o = b[6 + s][:, 0:288].rearrange("p (i h c) -> p i h c", i=2, c=9)
            c = self.ctx[:, 2 * s:2 * s + 2, :].rearrange("p i (h c) -> p i h c", c=8)
            ins = nc.vector.tensor_tensor(c, o[:, :, :, 0:8], over(self.rden[:, s], P, 2, 16, 8), ALU.mult)
            own.did(ins)
        own.wait()
        nc.vector.sem_inc(k.sem("ctx"), 1)
        dve.wait_ge(k.sem("attn_out"), 1)
        self.deliver(b[1][:, :].rearrange("p (t d) -> p t d", t=T))

    def gpsimd(self, pool):
        k, nc = self.k, self.k.nc
        nc.gpsimd.memset(self.vaug[:, :, :, 8:9], 1.0)
        nc.gpsimd.memset(self.pad[:, :, :, 8:], 0.0).then_inc(k.sem("pad_clear"), 1)
        if self.normed:
            pool.wait_ge(k.sem("qk_ms"), 1)
            half = k.row("minus_half", 0, 1).to_broadcast([P, T * self.nqk])
            nc.gpsimd.tensor_tensor(self.rs.rearrange("p t h -> p (t h)"), self.ms.rearrange("p t h -> p (t h)"),
                                    half, ALU.pow).then_inc(k.sem("qk_rs"), 1)


class L0Attn:

    def __init__(self, kit):
        self.k = kit
        mem = Arena(kit)
        self.norm = Norm(kit, mem, kit.x, 1e-5)
        self.heads = Heads(kit, mem, 16, "L0a_", False, self.deliver)

    def deliver(self, y):
        k = self.k
        k.nc.vector.tensor_tensor(k.x[:, :, :], k.x[:, :, :], y, ALU.add)

    def tensor(self, pe):
        self.norm.tensor(pe, self.k.bank[7])
        pe.wait_ge(self.k.sem("nT"), 1)
        self.heads.tensor(pe)

    def scalar(self, act):
        self.norm.scalar(act, self.k.bank[7])
        self.heads.scalar(act)

    def vector(self, dve):
        self.norm.vector(dve)
        self.heads.vector(dve)

    def gpsimd(self, pool):
        self.norm.gpsimd(pool)
        self.heads.gpsimd(pool)

    def sync(self, sp):
        pass

    def run(self, eng, name, method, src, dst, _):
        with eng.Fori(0, GROUPS) as g:
            if name == "sp":
                load_group(self.k, eng, src, g)
            self.k.end(eng, name)
            method(self)(eng)
            self.k.end(eng, name)
            if name == "sp":
                store_group(self.k, eng, dst, g)
            self.k.end(eng, name)


PLACED = [4 * (p % 4) + p // 4 for p in range(16)]


def heads_weights(i, tiles, spread):
    def heads(w):
        return w.reshape(w.shape[0], 16, 8)[:, PLACED].reshape(w.shape[0], P)

    freq = (1.0 / np.float32(10000.0) ** (np.arange(0, 8, 2, dtype=np.float32) / np.float32(8))).astype(np.float32)
    angle = (np.arange(SEQ, dtype=np.float32)[:, None] * freq[None, :]).astype(np.float32)

    def table(a):
        a = a.reshape(2, P, 4)[[0, 1, 0, 1]]
        return a.transpose(1, 0, 2).reshape(P, T * 4)

    wo3 = i["L3_attn_o_w"].reshape(16, 8, D)[PLACED].reshape(P, D)
    wo0 = i["L0_attn_Wo"].T.reshape(16, 8, D)[PLACED].reshape(P, D)
    return {
        "L0a_Wqkv": np.concatenate([heads(i["L0_attn_Wq"].T), heads(i["L0_attn_Wk"].T), heads(i["L0_attn_Wv"].T)], 1),
        "L0a_Wo": wo0,
        "L3a_Wqkv": np.concatenate([heads(i["L3_attn_q_w"]), i["L3_attn_k_w"], i["L3_attn_v_w"]], 1),
        "L3a_Wo": wo3,
        "L3a_q_gain": spread(i["L3_attn_q_gain"][PLACED]),
        "rope_cos": table(np.cos(angle)), "rope_sin": table(np.sin(angle)),
        "mask_neg": np.triu(np.full((P, P), -1e30, np.float32), 1),
    }


MORE_WEIGHTS += [heads_weights]


NE = 16
CAP = TOKENS * 2 // NE
NT = TOKENS // P
NEXT = D + NE
BATCH = 4
WE = 4 * D * 2 + 4 * D


class RouteShared:

    def __init__(self, kit, keep):
        self.k, self.sc = kit, keep
        mem = Arena(kit)
        self.norm = Norm(kit, mem, kit.x, 1e-5)
        self.z, self.p = mem(T, NE), mem(T, NE)
        self.mx, self.sum, self.rec = mem(T), mem(T), mem(T)
        self.rows = mem(T, NEXT)
        self.mlp = Mlp(kit, mem, kit.nT, 2, 2, "gated", ACT.Gelu,
                       first=lambda u: kit.row("L0f_Sg", u * P, (u + 1) * P),
                       second=lambda u: kit.row("L0f_Su", u * P, (u + 1) * P),
                       down=lambda u: kit.row("L0f_Sd", u * P, (u + 1) * P), use=self.use)

    def use(self, e, y):
        k = self.k
        return k.nc.vector.scalar_tensor_tensor(k.x[:, :, :], y[:, :].rearrange("p (t d) -> p t d", t=T), 0.5,
                                                k.x[:, :, :], ALU.mult, ALU.add)

    def tensor(self, pe, g):
        k, nc = self.k, self.k.nc
        self.norm.tensor(pe, k.bank[7])
        pe.wait_ge(k.sem("nT"), 1)
        for t in range(T):
            ins = nc.tensor.matmul(k.bank[6][:, t * NE:(t + 1) * NE], k.nT[:, t * P:(t + 1) * P], k.w("L0f_gate"),
                                   start=True, stop=True)
        ins.then_inc(k.sem("logits"), 1)
        self.mlp.tensor(pe)

    def scalar(self, act, g):
        k, nc = self.k, self.k.nc
        self.norm.scalar(act, k.bank[7])
        act.wait_ge(k.sem("logits_shifted"), 1)
        nc.scalar.activation(self.p, self.z, ACT.Exp).then_inc(k.sem("router_exp"), 1)
        act.wait_ge(k.sem("norm_n"), T)
        nc.scalar.copy(self.rows[:, :, 0:D], k.n[:, :, :]).then_inc(k.sem("row_n"), 1)
        self.mlp.scalar(act)

    def vector(self, dve, g):
        k, nc, own = self.k, self.k.nc, self.k.own["dve"]
        self.norm.vector(dve)
        lg = k.bank[6][:, 0:T * NE].rearrange("p (t e) -> p t e", t=T)
        dve.wait_ge(k.sem("logits"), 1)
        own.step(nc.vector.tensor_reduce(self.mx, lg, AX.X, ALU.max))
        nc.vector.tensor_tensor(self.z, lg, over(self.mx, P, T, NE), ALU.subtract)\
            .then_inc(k.sem("logits_shifted"), 1)
        dve.wait_ge(k.sem("router_exp"), 1)
        own.step(nc.vector.tensor_reduce(self.sum, self.p, AX.X, ALU.add))
        own.step(nc.vector.reciprocal(self.rec, self.sum))
        nc.vector.tensor_tensor(self.rows[:, :, D:], self.p, over(self.rec, P, T, NE), ALU.mult)\
            .then_inc(k.sem("row_scores"), 1)
        dve.wait_ge(k.sem("row_scores"), 1)
        nc.vector.tensor_copy(self.sc[:, bass.ds(g, 1)].rearrange("p o t e -> p (o t) e"), self.rows[:, :, D:])
        self.mlp.vector(dve)

    def gpsimd(self, pool, g):
        self.norm.gpsimd(pool)

    def sync(self, sp, g, n_ext):
        k = self.k
        sp.wait_ge(k.sem("row_n"), 1)
        sp.wait_ge(k.sem("row_scores"), 1)
        v = n_ext.rearrange("(g t p) d -> p g t d", g=GROUPS, p=P)
        sp.dma_start(v[:, bass.ds(g, 1)].rearrange("p o t d -> p (o t) d"), self.rows).then_inc(k.sem("rows_out"), 16)
        sp.wait_ge(k.sem("rows_out"), 16)


class Choose:

    def __init__(self, kit, keep_scores, keep_place):
        self.k, self.sc4, self.place = kit, keep_scores, keep_place
        mem = Arena(kit)
        self.sc = keep_scores.rearrange("p g t e -> p (g t) e")
        self.low, self.cand, self.hit, self.bit = [mem(NE) for _ in range(4)]
        self.ge = mem(NT, NE)
        self.cnt = mem(NE)
        self.gt, self.fill, self.mask = [mem(NT, NE) for _ in range(3)]
        self.need = mem(NE)
        half = mem(NT * NE // 2)
        self.flag = half.bitcast(BF16).rearrange("p (t e) -> p t e", t=NT)
        self.ones = mem(P // 2).bitcast(BF16)
        self.below = mem(P // 2).bitcast(BF16)

    BITS = 30

    def prefix(self, pe, bank):
        k, nc = self.k, self.k.nc
        nc.tensor.matmul(bank[:, 0:NT * NE], self.below, self.flag.rearrange("p t e -> p (t e)"),
                         start=True, stop=False, skip_group_check=True)
        for t in range(NT - 1):
            later = NT - 1 - t
            src = self.flag[:, t:t + 1, :].to_broadcast([P, later, NE])
            ins = nc.tensor.matmul(bank[:, (t + 1) * NE:NT * NE].rearrange("p (t e) -> p t e", e=NE), self.ones, src,
                                   start=False, stop=(t == NT - 2), skip_group_check=True)
        return ins

    def tensor(self, pe):
        k, nc, b = self.k, self.k.nc, self.k.bank
        for r in range(self.BITS + 1):
            pe.wait_ge(k.sem("counted"), r + 1)
            nc.tensor.matmul(b[r % 2][:, 0:NE], k.w("ones"), self.cnt, start=True, stop=True)\
                .then_inc(k.sem("total"), 1)
        pe.wait_ge(k.sem("flags"), 1)
        self.prefix(pe, b[2]).then_inc(k.sem("prefixes"), 1)
        pe.wait_ge(k.sem("flags"), 2)
        self.prefix(pe, b[3]).then_inc(k.sem("prefixes"), 1)

    def vector(self, dve):
        k, nc, b, own = self.k, self.k.nc, self.k.bank, self.k.own["dve"]
        own.did(nc.vector.tensor_copy(self.ones, k.w("ones")))
        own.did(nc.vector.tensor_copy(self.below, k.w("below_")))
        own.did(nc.vector.memset(self.low, 0.0))
        own.step(nc.vector.memset(self.bit.bitcast(I32), 1 << (self.BITS - 1)))
        low, cand, hit, bit = [v.bitcast(I32) for v in (self.low, self.cand, self.hit, self.bit)]
        turned = self.ge.rearrange("p t e -> p e t")
        for r in range(self.BITS):
            own.step(nc.vector.tensor_tensor(cand, low, bit, ALU.bitwise_or))
            own.did(nc.vector.tensor_tensor(self.ge, self.sc, self.cand.unsqueeze(1).to_broadcast([P, NT, NE]),
                                            ALU.is_ge))
            own.wait()
            nc.vector.tensor_reduce(self.cnt, turned, AX.X, ALU.add).then_inc(k.sem("counted"), 1)
            own.did(nc.vector.tensor_scalar(bit, bit, 1, None, ALU.logical_shift_right))
            dve.wait_ge(k.sem("total"), r + 1)
            own.step(nc.vector.tensor_scalar(hit, b[r % 2][:, 0:NE], float(CAP), None, ALU.is_ge))
            own.step(nc.vector.copy_predicated(low, hit, cand))
        own.step(nc.vector.tensor_tensor(self.gt, self.sc, self.low.unsqueeze(1).to_broadcast([P, NT, NE]), ALU.is_gt))
        nc.vector.tensor_reduce(self.cnt, self.gt.rearrange("p t e -> p e t"), AX.X, ALU.add)\
            .then_inc(k.sem("counted"), 1)
        nc.vector.tensor_tensor(self.flag, self.sc, self.low.unsqueeze(1).to_broadcast([P, NT, NE]), ALU.is_equal)\
            .then_inc(k.sem("flags"), 1)
        dve.wait_ge(k.sem("total"), self.BITS + 1)
        own.step(nc.vector.tensor_scalar(self.need, b[self.BITS % 2][:, 0:NE], -1.0, float(CAP), ALU.mult, ALU.add))
        dve.wait_ge(k.sem("prefixes"), 1)
        pre = b[2][:, 0:NT * NE].rearrange("p (t e) -> p t e", t=NT)
        own.step(nc.vector.tensor_tensor(self.fill, pre, self.need.unsqueeze(1).to_broadcast([P, NT, NE]), ALU.is_lt))
        own.step(nc.vector.tensor_tensor(self.fill, self.fill, self.flag, ALU.mult))
        own.step(nc.vector.tensor_tensor(self.mask, self.fill, self.gt, ALU.add))
        nc.vector.tensor_copy(self.flag, self.mask).then_inc(k.sem("flags"), 1)
        own.step(nc.vector.tensor_scalar(self.mask, self.mask, -4096.0, 4096.0, ALU.mult, ALU.add))
        dve.wait_ge(k.sem("prefixes"), 2)
        nc.vector.tensor_tensor(self.place[:, :, :].rearrange("p e t -> p t e"), self.mask,
                                b[3][:, 0:NT * NE].rearrange("p (t e) -> p t e", t=NT), ALU.add)

    def scalar(self, eng):
        pass

    gpsimd = sync = scalar


class Lists:

    def __init__(self, kit, place, index):
        self.k, self.place, self.index = kit, place, index
        mem = Arena(kit)
        self.at = mem(BATCH, NT)
        self.sel = [mem(NT * CAP // 2).bitcast(BF16).rearrange("p (t c) -> p t c", t=NT) for _ in range(2)]
        self.iota = mem(CAP // 2).bitcast(BF16)
        self.tok = mem(NT).bitcast(BF16).rearrange("p (t c) -> p t c", c=2)
        self.num = mem(BATCH * 2)
        self.half = mem(BATCH * 2)

    def vector(self, dve, i):
        k, nc, own = self.k, self.k.nc, self.k.own["dve"]
        own.did(nc.vector.tensor_copy(self.iota, k.w("iota256")))
        own.did(nc.vector.tensor_copy(self.tok, k.w("token_parts").rearrange("p (t c) -> p t c", c=2)))
        own.step(nc.vector.tensor_copy(self.at, self.place[:, bass.ds(i * BATCH, BATCH), :]))
        for j in range(BATCH):
            if j >= 2:
                dve.wait_ge(k.sem("listed"), j - 1)
            for t in range(NT):
                ins = nc.vector.tensor_scalar(self.sel[j % 2][:, t, :], self.iota, self.at[:, j, t:t + 1], None,
                                              ALU.is_equal)
            ins.then_inc(k.sem("selected"), 1)
        dve.wait_ge(k.sem("listed"), BATCH)
        v = k.bank[0][:, 0:BATCH * 4].rearrange("p (a c) -> p a c", c=2)
        own.step(nc.vector.tensor_copy(self.half, v[:, :, 1]))
        own.step(nc.vector.scalar_tensor_tensor(self.num, v[:, :, 0], float(P), self.half, ALU.mult, ALU.add))
        nc.vector.tensor_copy(self.index[:, bass.ds(i * 2 * BATCH, 2 * BATCH)], self.num)

    def tensor(self, pe, i):
        k, nc = self.k, self.k.nc
        for j in range(BATCH):
            pe.wait_ge(k.sem("selected"), j + 1)
            for t in range(NT):
                for h in range(2):
                    c = (2 * j + h) * 2
                    ins = nc.tensor.matmul(k.bank[0][:, c:c + 2], self.sel[j % 2][:, t, h * P:(h + 1) * P],
                                           self.tok[:, t, :], start=(t == 0 and h == 0), stop=(t == NT - 1),
                                           skip_group_check=True)
            ins.then_inc(k.sem("listed"), 1)


class Experts:

    def __init__(self, kit, index):
        self.k, self.index = kit, index
        mem = Arena(kit)
        self.idx = mem(2 * BATCH).bitcast(U32)
        self.rows = mem(BATCH, 2, NEXT)
        self.w = [mem(WE) for _ in range(2)]
        self.nT = [mem(CAP) for _ in range(2)]
        self.a = [mem(CAP) for _ in range(2)]
        self.h = [mem(CAP) for _ in range(2)]
        self.score = mem(BATCH, 2)
        self.out = mem(BATCH, 2, D)

    UNITS = [(j, u) for j in range(BATCH) for u in range(4)]

    def sync(self, sp, i, weights):
        k = self.k
        for j in range(BATCH):
            if j >= 2:
                sp.wait_ge(k.sem("down_done"), 4 * (j - 1))
            sp.dma_start(self.w[j % 2], weights[bass.ds(i * BATCH + j, 1)].rearrange("o p n -> p (o n)"))\
                .then_inc(k.sem(f"expert_w{j % 2}"), 16)

    def gpsimd(self, pool, i, n_ext, dst):
        k, nc = self.k, self.k.nc
        pool.wait_ge(k.sem("idx"), 1)
        for j in range(BATCH):
            for h in range(2):
                c = 2 * j + h
                nc.gpsimd.indirect_dma_start(self.rows[:, j, h, :], None, n_ext,
                                             bass.IndirectOffsetOnAxis(ap=self.idx[:, c:c + 1], axis=0))\
                    .then_inc(k.sem(f"gathered{j}"), 16)
        n = 0
        for j in range(BATCH):
            pool.wait_ge(k.sem("expert_out"), j + 1)
            for h in range(2):
                c = 2 * j + h
                if n:
                    pool.wait_ge(k.sem("added"), 16 * n)
                nc.gpsimd.indirect_dma_start(dst, bass.IndirectOffsetOnAxis(ap=self.idx[:, c:c + 1], axis=0),
                                             self.out[:, j, h, :], None, compute_op=ALU.add)\
                    .then_inc(k.sem("added"), 16)
                n += 1
        pool.wait_ge(k.sem("added"), 16 * n)
        pool.drain()
        pool.dma_reset(range(k.first, k.last + 1))

    def tensor(self, pe, i):
        k, nc, b = self.k, self.k.nc, self.k.bank

        def turn(j):
            pe.wait_ge(k.sem(f"gathered{j}"), 32)
            if j >= 2:
                pe.wait_ge(k.sem("expert_nT"), j - 1)
            for h in range(2):
                ins = nc.tensor.transpose(b[6 + j % 2][:, h * P:(h + 1) * P], self.rows[:, j, h, 0:D], k.w("ident"))
            ins.then_inc(k.sem("rows_turned"), 1)

        def up(n):
            j, u = self.UNITS[n]
            if u == 0:
                pe.wait_ge(k.sem("expert_nT"), j + 1)
                pe.wait_ge(k.sem(f"expert_w{j % 2}"), 16 * (j // 2 + 1))
            if n >= 2:
                pe.wait_ge(k.sem("h_ready"), n - 1)
            o = b[n % 2]
            w = self.w[j % 2]
            nc.tensor.matmul(o[:, 0:CAP], w[:, u * P:(u + 1) * P], self.nT[j % 2], start=True, stop=True)
            nc.tensor.matmul(o[:, CAP:2 * CAP], w[:, 512 + u * P:512 + (u + 1) * P], self.nT[j % 2],
                             start=True, stop=True).then_inc(k.sem("up_ready"), 1)

        def down(n):
            j, u = self.UNITS[n]
            pe.wait_ge(k.sem("h_ready"), n + 1)
            if u == 0 and j >= 2:
                pe.wait_ge(k.sem("expert_out"), j - 1)
            for h in range(2):
                ins = nc.tensor.matmul(b[4 + j % 2][:, h * D:(h + 1) * D], self.h[n % 2][:, h * P:(h + 1) * P],
                                       self.w[j % 2][:, 1024 + u * D:1024 + (u + 1) * D],
                                       start=(u == 0 and h == 0), stop=(u == 3), skip_group_check=True)
            ins.then_inc(k.sem("down_done"), 1)

        turn(0)
        up(0)
        for n in range(len(self.UNITS)):
            j, u = self.UNITS[n]
            if u == 1 and j + 1 < BATCH:
                turn(j + 1)
            if n + 1 < len(self.UNITS):
                up(n + 1)
            down(n)

    def scalar(self, act, i):
        k, nc, b = self.k, self.k.nc, self.k.bank

        def keep(j):
            act.wait_ge(k.sem("rows_turned"), j + 1)
            if j >= 2:
                act.wait_ge(k.sem("up_ready"), 4 * (j - 1))
            nc.scalar.copy(self.nT[j % 2], b[6 + j % 2][:, 0:CAP]).then_inc(k.sem("expert_nT"), 1)

        keep(0)
        for n, (j, u) in enumerate(self.UNITS):
            if u == 2 and j + 1 < BATCH:
                keep(j + 1)
            act.wait_ge(k.sem("up_ready"), n + 1)
            if n >= 2:
                act.wait_ge(k.sem("h_ready"), n - 1)
            nc.scalar.activation(self.a[n % 2], b[n % 2][:, 0:CAP], ACT.Gelu).then_inc(k.sem("a_ready"), 1)

    def vector(self, dve, i):
        k, nc, b, own = self.k, self.k.nc, self.k.bank, self.k.own["dve"]
        nc.vector.tensor_copy(self.idx, self.index[:, bass.ds(i * 2 * BATCH, 2 * BATCH)]).then_inc(k.sem("idx"), 1)

        def finish(j):
            dve.wait_ge(k.sem("down_done"), 4 * (j + 1))
            for h in range(2):
                ins = nc.vector.tensor_scalar(self.out[:, j, h, :], b[4 + j % 2][:, h * D:(h + 1) * D],
                                              self.score[:, j, h:h + 1], 0.5, ALU.mult, ALU.mult)
            ins.then_inc(k.sem("expert_out"), 1)

        for n, (j, u) in enumerate(self.UNITS):
            if u == 0:
                dve.wait_ge(k.sem(f"gathered{j}"), 32)
                own.step(nc.vector.tensor_copy(
                    self.score[:, j, :], self.rows[:, j, :, D:][:, :, bass.ds(i * BATCH + j, 1)]
                    .rearrange("p h o -> p (h o)")))
            dve.wait_ge(k.sem("a_ready"), n + 1)
            if n >= 2:
                dve.wait_ge(k.sem("down_done"), n - 1)
            nc.vector.tensor_tensor(self.h[n % 2], self.a[n % 2], b[n % 2][:, CAP:2 * CAP], ALU.mult)\
                .then_inc(k.sem("h_ready"), 1)
            if u == 1 and j >= 1:
                finish(j - 1)
        finish(BATCH - 1)


class L0Ffn:

    def __init__(self, kit, dram):
        self.k, self.dram = kit, dram
        nc, ctx = kit.nc, kit.ctx
        self.sc = ctx.enter_context(nc.sbuf_tensor("route_scores", [P, GROUPS, T, NE], F32))
        self.place = ctx.enter_context(nc.sbuf_tensor("route_place", [P, NE, NT], F32))
        self.index = ctx.enter_context(nc.sbuf_tensor("route_index", [P, 2 * NE], U32))
        self.route = RouteShared(kit, self.sc)
        self.choose = Choose(kit, self.sc[:, :, :, :], self.place)
        self.lists = Lists(kit, self.place, self.index)
        self.experts = Experts(kit, self.index)

    def run(self, eng, name, method, src, dst, n_ext):
        k = self.k
        with eng.Fori(0, GROUPS) as g:
            if name == "sp":
                load_group(k, eng, src, g)
            k.end(eng, name)
            if name == "sp":
                self.route.sync(eng, g, n_ext)
            else:
                method(self.route)(eng, g)
            k.end(eng, name)
            if name == "sp":
                store_group(k, eng, dst, g)
            k.end(eng, name)
        method(self.choose)(eng)
        k.end(eng, name)
        with eng.Fori(0, NE // BATCH) as i:
            if name in ("pe", "dve"):
                method(self.lists)(eng, i)
            k.end(eng, name)
        with eng.Fori(0, NE // BATCH) as i:
            if name == "sp":
                self.experts.sync(eng, i, self.dram["L0_experts"])
            elif name == "pool":
                self.experts.gpsimd(eng, i, n_ext, dst)
            else:
                method(self.experts)(eng, i)
            k.end(eng, name)


def l0ffn_weights(i, tiles, spread):
    token = np.arange(TOKENS).reshape(NT, P)
    return {
        "L0f_gate": i["L0_ffn_gate_w"].T, "L0f_Sg": i["L0_ffn_Sg"].T, "L0f_Su": i["L0_ffn_Su"].T,
        "L0f_Sd": tiles(i["L0_ffn_Sd"].T, D),
        "below_": np.triu(np.ones((P, P), np.float32), 1),
        "iota256": spread(np.arange(CAP, dtype=np.float32)),
        "token_parts": np.stack([token // P, token % P], -1).transpose(1, 0, 2).reshape(P, -1).astype(np.float32),
    }


def extra_inputs(i):
    down = i["L0_ffn_Wd"].transpose(0, 2, 1).reshape(NE, 4, P, D).transpose(0, 2, 1, 3).reshape(NE, P, 4 * D)
    return {"L0_experts": np.ascontiguousarray(np.concatenate(
        [i["L0_ffn_Wg"].transpose(0, 2, 1), i["L0_ffn_Wu"].transpose(0, 2, 1), down], 2))}


MORE_WEIGHTS += [l0ffn_weights]


H2 = 4
FIR = 64
PE_TAPS = 32


class PrepL2:

    def __init__(self, kit):
        self.k = kit

        def keep(name, n):
            return kit.ctx.enter_context(kit.nc.sbuf_tensor("l2_" + name, [P, n], F32))
        self.diag, self.bias, self.rtemp, self.share = keep("diag", PE_TAPS * P), keep("bias", 16), keep("rtemp", 4), keep("share", 4)
        self.t = [keep(f"t{i}", 4) for i in range(6)]

    def scalar(self, act):
        k, nc, t = self.k, self.k.nc, self.t
        nc.scalar.activation(t[0][:, :], k.w("L2a_log_temp"), ACT.Abs).then_inc(k.sem("temp_abs"), 1)
        act.wait_ge(k.sem("temp_abs"), 1)
        nc.scalar.activation(t[1][:, :], t[0][:, :], ACT.Exp, scale=-1.0).then_inc(k.sem("temp_e"), 1)
        nc.scalar.activation(self.share[:, :], k.w("L2a_residual_logit"), ACT.Sigmoid).then_inc(k.sem("share"), 1)

    def vector(self, dve):
        k, nc, own, t = self.k, self.k.nc, self.k.own["dve"], self.t
        for j in range(PE_TAPS):
            own.did(nc.vector.tensor_scalar(self.diag[:, j * P:(j + 1) * P], k.w("ident"),
                                            k.row("L2a_fir_long", j, j + 1), None, ALU.mult))
        own.step(nc.vector.tensor_tensor(self.bias[:, :], k.w("L2a_b2"), k.w("L2a_base_bias"), ALU.add))
        dve.wait_ge(k.sem("temp_e"), 1)
        own.step(softplus(k, t[4][:, :], k.w("L2a_log_temp"), t[1][:, :], t[2][:, :], t[3][:, :]))
        own.step(nc.vector.tensor_scalar(t[4][:, :], t[4][:, :], 1e-4, None, ALU.add))
        own.step(nc.vector.reciprocal(self.rtemp[:, :], t[4][:, :]))
        dve.wait_ge(k.sem("share"), 1)
        nc.vector.tensor_scalar(self.share[:, :], self.share[:, :], 0.5, None, ALU.mult)

    def tensor(self, pe):
        pass

    gpsimd = sync = tensor


class L2State:

    def __init__(self, kit, prep):
        self.prep, self.mem = prep, Arena(kit)
        mem = self.mem
        self.qT, self.kT = mem(GT), mem(GT)
        self.F = mem(T, 4, D)
        self.ktok = mem(T, D)
        self.vk = mem(T, H2, 64)
        self.beta, self.nbeta = mem(T, H2), mem(T, H2)
        self.after = self.mem.at


class L2Project:

    def __init__(self, kit, st):
        self.k, self.st = kit, st
        mem = st.mem
        mem.at = st.after
        self.norm = Norm(kit, mem, kit.x, 1e-5)
        self.pre = [mem(NB, 3 + SEQ) for _ in range(3)]
        self.c = [[mem(NB, SEQ) for _ in range(2)] for _ in range(3)]
        self.act_ = [mem(GT) for _ in range(2)]
        self.sq = [mem(GT) for _ in range(2)]
        self.ss = [mem(GT) for _ in range(2)]
        self.vf = mem(NB, FIR - 1 + SEQ)
        self.vcopy = mem(GT)
        self.fs = [mem(NB, SEQ) for _ in range(2)]
        self.fl = mem(GT)
        self.part = [mem(NB, SEQ) for _ in range(2)]

    @staticmethod
    def two(v):
        return v.rearrange("p (b s) -> p b s", b=NB)

    def tensor(self, pe):
        k, nc, b = self.k, self.k.nc, self.k.bank
        self.norm.tensor(pe, b[7])
        pe.wait_ge(k.sem("nT"), 1)
        for i, w in ((2, "Wv"), (0, "Wq"), (1, "Wk")):
            nc.tensor.matmul(b[i][:, :], k.w("L2a_" + w), k.nT[:, :], start=True, stop=True)\
                .then_inc(k.sem("projected"), 1)
        for t in range(T):
            ins = nc.tensor.matmul(b[3][:, t * H2:(t + 1) * H2], k.nT[:, t * P:(t + 1) * P], k.w("L2a_Wb"),
                                   start=True, stop=True)
        ins.then_inc(k.sem("beta_made"), 1)
        pe.wait_ge(k.sem("v_act"), 1)
        for j in range(PE_TAPS):
            ins = nc.tensor.matmul(self.two(b[6][:, :]), self.st.prep.diag[:, j * P:(j + 1) * P],
                                   self.vf[:, :, j:j + SEQ], start=(j == 0), stop=(j == PE_TAPS - 1))
            if j == 15:
                for i in range(2):
                    pe.wait_ge(k.sem("squared"), i + 1)
                    nc.tensor.matmul(b[4 + i][:, :], k.w("blocks32"), self.sq[i], start=True, stop=True)\
                        .then_inc(k.sem("sumsq"), 1)
        ins.then_inc(k.sem("long_made"), 1)
        for i, (name, src) in enumerate(self.turned()):
            pe.wait_ge(k.sem(name), 1)
            if i >= 2:
                pe.wait_ge(k.sem("token_kept"), i - 1)
            for t in range(T):
                ins = nc.tensor.transpose(b[i % 2][:, t * P:(t + 1) * P], src[:, t * P:(t + 1) * P], k.w("ident"))
            ins.then_inc(k.sem("token_turned"), 1)

    def turned(self):
        return [("vcopy", self.vcopy), ("k_normal", self.st.kT), ("short", self.fs[0].rearrange("p b s -> p (b s)")),
                ("long", self.fl)]

    def scalar(self, act):
        k, nc, b = self.k, self.k.nc, self.k.bank
        self.norm.scalar(act, b[7])
        for n, i in enumerate((2, 0, 1)):
            act.wait_ge(k.sem("projected"), n + 1)
            nc.scalar.copy(self.pre[i][:, :, 3:], self.two(b[i][:, :])).then_inc(k.sem("pre"), 1)
        act.wait_ge(k.sem("conv2"), 4)
        act.wait_ge(k.sem("pads"), 1)
        nc.scalar.activation(self.c[2][0], self.c[2][1], ACT.Sigmoid).then_inc(k.sem("sigmoid"), 1)
        for i in range(2):
            act.wait_ge(k.sem(f"conv{i}"), 4)
            nc.scalar.activation(self.c[i][0], self.c[i][1], ACT.Sigmoid).then_inc(k.sem("sigmoid"), 1)
        for i in range(2):
            act.wait_ge(k.sem("qk_act"), i + 1)
            nc.scalar.activation(self.sq[i], self.act_[i], ACT.Square).then_inc(k.sem("squared"), 1)
        act.wait_ge(k.sem("beta_made"), 1)
        nc.scalar.activation(self.st.beta, b[3][:, 0:T * H2].rearrange("p (t h) -> p t h", t=T), ACT.Sigmoid)\
            .then_inc(k.sem("beta"), 1)
        for i in range(2):
            act.wait_ge(k.sem("sumsq_eps"), i + 1)
            nc.scalar.activation(self.sq[i], self.ss[i], ACT.Ln).then_inc(k.sem("log_ss"), 1)
            act.wait_ge(k.sem("log_ss"), i + 1)
            nc.scalar.activation(self.ss[i], self.sq[i], ACT.Exp, scale=-0.5).then_inc(k.sem("rnorm"), 1)

    def vector(self, dve):
        k, nc, b, own, st = self.k, self.k.nc, self.k.bank, self.k.own["dve"], self.st
        for i in range(3):
            own.did(nc.vector.memset(self.pre[i][:, :, 0:3], 0.0))
        nc.vector.memset(self.vf[:, :, 0:FIR - 1], 0.0).then_inc(k.sem("pads"), 1)
        self.norm.vector(dve)
        for n, (i, w) in enumerate(((2, "conv_v"), (0, "conv_q"), (1, "conv_k"))):
            dve.wait_ge(k.sem("pre"), n + 1)
            self.taps(dve, self.c[i], self.pre[i], 0, "L2a_" + w, 4, f"conv{i}")
        for n, (dst, i) in enumerate(((self.vf[:, :, FIR - 1:], 2), (self.two(self.act_[0]), 0),
                                      (self.two(self.act_[1]), 1))):
            dve.wait_ge(k.sem("sigmoid"), n + 1)
            nc.vector.tensor_tensor(dst, self.c[i][0], self.c[i][1], ALU.mult)\
                .then_inc(k.sem("v_act" if i == 2 else "qk_act"), 1)
        dve.wait_ge(k.sem("v_act"), 1)
        nc.vector.tensor_copy(self.two(self.vcopy), self.vf[:, :, FIR - 1:]).then_inc(k.sem("vcopy"), 1)
        self.taps(dve, self.fs, self.vf, FIR - 5, "L2a_fir_short", 5, "short_taps")
        dve.wait_ge(k.sem("short_taps"), 5)
        nc.vector.sem_inc(k.sem("short"), 1)
        self.taps(dve, self.part, self.vf, PE_TAPS, "L2a_fir_long_rest", FIR - PE_TAPS, "long_taps")
        for i in range(2):
            dve.wait_ge(k.sem("sumsq"), i + 1)
            nc.vector.tensor_scalar(self.ss[i], b[4 + i][:, :], 1e-6, None, ALU.add).then_inc(k.sem("sumsq_eps"), 1)
        for i, dst in enumerate((st.qT, st.kT)):
            dve.wait_ge(k.sem("rnorm"), i + 1)
            ins = nc.vector.tensor_tensor(dst, self.act_[i], self.ss[i], ALU.mult)
        ins.then_inc(k.sem("k_normal"), 1)
        dve.wait_ge(k.sem("beta"), 1)
        own.step(nc.vector.tensor_scalar(st.nbeta, st.beta, -1.0, None, ALU.mult))

        def heads(v):
            return v.rearrange("p t (h c) -> p t h c", h=H2)
        beta = over(st.beta, P, T, H2, 32)
        dve.wait_ge(k.sem("token_turned"), 1)
        tok = b[0][:, :].rearrange("p (t d) -> p t d", t=T)
        own.did(nc.vector.tensor_tensor(st.vk[:, :, :, 0:32], heads(tok), beta, ALU.mult))
        nc.vector.tensor_copy(st.F[:, :, 3, :], tok).then_inc(k.sem("token_kept"), 1)
        dve.wait_ge(k.sem("token_turned"), 2)
        tok = b[1][:, :].rearrange("p (t d) -> p t d", t=T)
        own.did(nc.vector.tensor_tensor(st.vk[:, :, :, 32:64], heads(tok), beta, ALU.mult))
        nc.vector.tensor_copy(st.ktok, tok).then_inc(k.sem("token_kept"), 1)
        dve.wait_ge(k.sem("long_taps"), FIR - PE_TAPS)
        dve.wait_ge(k.sem("long_made"), 1)
        nc.vector.tensor_tensor(self.two(self.fl), self.part[1], self.two(b[6][:, :]), ALU.add)\
            .then_inc(k.sem("long"), 1)
        for i in (2, 3):
            dve.wait_ge(k.sem("token_turned"), i + 1)
            nc.vector.tensor_copy(st.F[:, :, i - 2, :], b[i % 2][:, :].rearrange("p (t d) -> p t d", t=T))\
                .then_inc(k.sem("token_kept"), 1)

    def taps(self, dve, dst, src, off, name, n, sem):
        k, nc = self.k, self.k.nc
        for j in range(n):
            s = src[:, :, off + j:off + j + SEQ]
            w = k.row(name, j, j + 1)
            if j == 0:
                ins = nc.vector.tensor_scalar(dst[0], s, w, None, ALU.mult)
            else:
                dve.wait_ge(k.sem(sem), j)
                ins = nc.vector.scalar_tensor_tensor(dst[j % 2], s, w, dst[(j + 1) % 2], ALU.mult, ALU.add)
            ins.then_inc(k.sem(sem), 1)

    def gpsimd(self, pool):
        self.norm.gpsimd(pool)

    def sync(self, sp):
        pass


class L2Delta:

    def __init__(self, kit, st):
        self.k, self.st = kit, st
        mem = st.mem
        mem.at = st.after
        self.MT = [mem(GT) for _ in range(H2)]
        self.LT = [mem(GT) for _ in range(2)]
        self.X = [mem(GT) for _ in range(H2)]
        self.R = [mem(GT) for _ in range(H2)]
        self.Y = [mem(GT) for _ in range(H2)]
        self.U = mem(T, D)
        self.wtok = mem(T, D)
        self.wT = mem(GT)
        self.ut = mem(T, D)
        self.S = [mem(D) for _ in range(NB)]

    def rows(self, h):
        return slice(32 * h, 32 * h + 32)

    def tensor(self, pe):
        k, nc, b, st = self.k, self.k.nc, self.k.bank, self.st
        tile = lambda v, t: v[:, t * P:(t + 1) * P]
        for h in range(H2):
            for t in range(T):
                kk = st.kT[self.rows(h), t * P:(t + 1) * P]
                ins = nc.tensor.matmul(tile(b[h], t), kk, kk, start=True, stop=True)
            ins.then_inc(k.sem("gram"), 1)
        for h in range(H2):
            pe.wait_ge(k.sem("M0"), h + 1)
            for t in range(T):
                ins = nc.tensor.transpose(tile(b[4 + h], t), tile(self.Y[h], t), k.w("ident"))
            ins.then_inc(k.sem("M0_turned"), 1)
        pe.wait_ge(k.sem("M0"), H2)
        pe.wait_ge(k.sem("MT0"), H2)
        for m in range(17):
            h = m % 4
            if m < 16:
                pe.wait_ge(k.sem("LT"), m + 1)
                pe.wait_ge(k.sem("X"), m + 1)
                if m >= 2:
                    pe.wait_ge(k.sem("Y"), m - 1)
                for t in range(T):
                    ins = nc.tensor.matmul(tile(b[m % 2], t), tile(self.LT[m % 2], t), tile(self.X[h], t),
                                           start=True, stop=True)
                ins.then_inc(k.sem("Y_made"), 1)
            if m >= 1:
                self.grow(pe, m - 1)
        for t in range(T):
            for h in range(H2):
                if t == 0:
                    pe.wait_ge(k.sem("R"), 4 * 4 + h + 1)
                ins = nc.tensor.matmul(b[t // 2][:, (t % 2) * 256 + h * 64:(t % 2) * 256 + (h + 1) * 64],
                                       tile(self.R[h], t), st.vk[:, t, h, :], start=True, stop=True)
            if t % 2 == 1:
                ins.then_inc(k.sem("UW"), 1)
        for h in range(H2):
            bank = b[2 + h]
            for t in range(T):
                ins = nc.tensor.matmul(tile(bank, t), st.kT[self.rows(h), t * P:(t + 1) * P],
                                       st.qT[self.rows(h), t * P:(t + 1) * P], start=True, stop=True)
            ins.then_inc(k.sem("local"), 1)
        pe.wait_ge(k.sem("w_kept"), 1)
        for t in range(T):
            ins = nc.tensor.transpose(tile(b[6], t), self.wtok[:, t, :], k.w("ident"))
        ins.then_inc(k.sem("w_turned"), 1)
        pe.wait_ge(k.sem("wT"), 1)
        pe.wait_ge(k.sem("local_kept"), H2)
        for j in range(8):
            for s in range(NB):
                t, r = 2 * s + j // 4, j % 4
                rows = self.rows(r)
                cols = slice(t * P + 32 * r, t * P + 32 * r + 32)
                pe.wait_ge(k.sem(f"state{s}"), j + 1)
                nc.tensor.matmul(b[s][rows, 0:D], self.wT[:, cols], self.S[s], start=True, stop=True)\
                    .then_inc(k.sem(f"wS{s}"), 1)
                nc.tensor.matmul(b[4 + t][rows, 0:D], st.qT[:, cols], self.S[s], start=True, stop=False,
                                 skip_group_check=True)
            for s in range(NB):
                t, r = 2 * s + j // 4, j % 4
                rows = self.rows(r)
                pe.wait_ge(k.sem(f"u{s}"), j + 1)
                nc.tensor.matmul(b[2 + s][:, 0:D], st.ktok[rows, t, :], self.ut[rows, t, :], start=(j == 0),
                                 stop=True, skip_group_check=True).then_inc(k.sem(f"kTu{s}"), 1)
                if j % 4 == 3:
                    for h in range(H2):
                        ins = nc.tensor.matmul(b[4 + t][:, 32 * h:32 * h + 32], tile(self.X[h], t),
                                               self.ut[:, t, 32 * h:32 * h + 32], start=False, stop=True,
                                               skip_group_check=True)
                    ins.then_inc(k.sem("delta_made"), 1)

    def grow(self, pe, m):
        k, nc, b = self.k, self.k.nc, self.k.bank
        h = m % 4
        tile = lambda v, t: v[:, t * P:(t + 1) * P]
        pe.wait_ge(k.sem("Y"), m + 1)
        pe.wait_ge(k.sem("R"), m + 1)
        if m >= 2:
            pe.wait_ge(k.sem("R"), m + 3)
            if m < 12:
                pe.wait_ge(k.sem("X"), m + 3)
        for t in range(T):
            ins = nc.tensor.matmul(tile(b[4 + m % 2], t), tile(self.Y[h], t), tile(self.R[h], t), start=True, stop=True)
        if m < 12:
            for t in range(T):
                ins = nc.tensor.matmul(tile(b[2 + m % 2], t), tile(self.R[h], t), tile(self.Y[h], t),
                                       start=True, stop=True)
        ins.then_inc(k.sem("grown"), 1)

    def scalar(self, act):
        k, nc, b = self.k, self.k.nc, self.k.bank
        for h in range(H2):
            act.wait_ge(k.sem("M0_turned"), h + 1)
            nc.scalar.copy(self.MT[h], b[4 + h][:, :]).then_inc(k.sem("MT0"), 1)
        for m in range(16):
            act.wait_ge(k.sem("Y_made"), m + 1)
            if m < 4:
                act.wait_ge(k.sem("X"), m + 1)
            else:
                act.wait_ge(k.sem("grown"), m - 3)
            nc.scalar.copy(self.Y[m % 4], b[m % 2][:, :]).then_inc(k.sem("Y"), 1)
        act.wait_ge(k.sem("w_turned"), 1)
        nc.scalar.copy(self.wT, b[6][:, :]).then_inc(k.sem("wT"), 1)
        for n, (s, half) in enumerate(((0, 0), (1, 0), (0, 1), (1, 1))):
            t = 2 * s + half
            act.wait_ge(k.sem("delta_made"), n + 1)
            nc.scalar.copy(self.st.F[:, t, 2, :], b[4 + t][:, 0:D])

    def vector(self, dve):
        k, nc, b, own, st = self.k, self.k.nc, self.k.bank, self.k.own["dve"], self.st
        tiles = lambda v: v.rearrange("p (t c) -> p t c", t=T)
        every = lambda name: k.w(name).unsqueeze(1).to_broadcast([P, T, P])
        for h in range(H2):
            dve.wait_ge(k.sem("gram"), h + 1)
            for t in range(T):
                ins = nc.vector.scalar_tensor_tensor(self.Y[h][:, t * P:(t + 1) * P], b[h][:, t * P:(t + 1) * P],
                                                     st.nbeta[:, t, h:h + 1], k.w("chunk_lower"), ALU.mult, ALU.mult)
            ins.then_inc(k.sem("M0"), 1)
        for h in range(H2):
            dve.wait_ge(k.sem("M0"), h + 1)
            own.step(nc.vector.tensor_tensor(tiles(self.X[h]), tiles(self.Y[h]), every("below1"), ALU.mult))
            nc.vector.tensor_tensor(tiles(self.X[h]), tiles(self.X[h]), every("ident"), ALU.add)\
                .then_inc(k.sem("X"), 1)
        for h in range(H2):
            dve.wait_ge(k.sem("MT0"), h + 1)
            own.step(nc.vector.tensor_tensor(tiles(self.R[h]), tiles(self.MT[h]), every("above1"), ALU.mult))
            nc.vector.tensor_tensor(tiles(self.R[h]), tiles(self.R[h]), every("ident"), ALU.add)\
                .then_inc(k.sem("R"), 1)
        for m in range(16):
            h = m % 4
            dve.wait_ge(k.sem("grown"), m + 1)
            if m < 12:
                nc.vector.tensor_tensor(self.X[h], self.X[h], b[2 + m % 2][:, :], ALU.add).then_inc(k.sem("X"), 1)
            nc.vector.tensor_tensor(self.R[h], self.R[h], b[4 + m % 2][:, :], ALU.add).then_inc(k.sem("R"), 1)
        for i in range(2):
            dve.wait_ge(k.sem("UW"), i + 1)
            v = b[i][:, :].rearrange("p (t h c) -> p t h c", t=2, h=H2)
            own.did(nc.vector.tensor_copy(self.U[:, 2 * i:2 * i + 2, :].rearrange("p t (h c) -> p t h c", h=H2),
                                          v[:, :, :, 0:32]))
            own.did(nc.vector.tensor_copy(self.wtok[:, 2 * i:2 * i + 2, :].rearrange("p t (h c) -> p t h c", h=H2),
                                          v[:, :, :, 32:64]))
        own.wait()
        nc.vector.sem_inc(k.sem("w_kept"), 1)
        upper = k.w("chunk_upper").unsqueeze(1).to_broadcast([P, T, P])
        for h in range(H2):
            dve.wait_ge(k.sem("local"), h + 1)
            nc.vector.tensor_tensor(self.X[h].rearrange("p (t c) -> p t c", t=T),
                                    b[2 + h][:, :].rearrange("p (t c) -> p t c", t=T), upper, ALU.mult)\
                .then_inc(k.sem("local_kept"), 1)
        for s in range(NB):
            nc.vector.memset(self.S[s], 0.0).then_inc(k.sem(f"state{s}"), 1)
        for j in range(8):
            for s in range(NB):
                t, rows = 2 * s + j // 4, self.rows(j % 4)
                dve.wait_ge(k.sem(f"wS{s}"), j + 1)
                nc.vector.tensor_tensor(self.ut[rows, t, :], self.U[rows, t, :], b[s][rows, 0:D], ALU.subtract)\
                    .then_inc(k.sem(f"u{s}"), 1)
            for s in range(NB):
                if j < 7:
                    dve.wait_ge(k.sem(f"kTu{s}"), j + 1)
                    nc.vector.tensor_tensor(self.S[s], b[2 + s][:, 0:D], k.w("blocks32"), ALU.mult)\
                        .then_inc(k.sem(f"state{s}"), 1)

    def gpsimd(self, pool):
        k, nc = self.k, self.k.nc
        for m in range(16):
            h = m % 4
            if m < 4:
                pool.wait_ge(k.sem("MT0"), h + 1)
            if m >= 2:
                pool.wait_ge(k.sem("Y_made"), m - 1)
            mask = k.w(f"above{2 << (m // 4)}").unsqueeze(1).to_broadcast([P, T, P])
            nc.gpsimd.tensor_tensor(self.LT[m % 2].rearrange("p (t c) -> p t c", t=T),
                                    self.MT[h].rearrange("p (t c) -> p t c", t=T), mask, ALU.mult)\
                .then_inc(k.sem("LT"), 1)

    def sync(self, sp):
        pass


class L2Mix:

    def __init__(self, kit, st):
        self.k, self.st = kit, st
        mem = st.mem
        mem.at = st.after
        self.sq = mem(T * 16, 32)
        self.sum, self.abs, self.ss = [mem(T * 16) for _ in range(3)]
        self.msq = mem(T * 16)
        self.stats = mem(T, H2, 4, 4)
        self.l2 = mem(T * 16)
        self.stT = mem(GT, rows=64)
        self.h1 = [mem(GT) for _ in range(2)]
        self.z, self.p = mem(T * H2, 4), mem(T * H2, 4)
        self.mx, self.tot, self.rec = mem(T * H2), mem(T * H2), mem(T * H2)
        self.prod = mem(T, 4, D)
        self.o = mem(T, D)
        self.osq = mem(T, D)
        self.oss, self.ors = mem(T * H2), mem(T * H2)
        self.oT = mem(GT)

    def tensor(self, pe):
        k, nc, b = self.k, self.k.nc, self.k.bank
        pe.wait_ge(k.sem("stats"), 1)
        for t in range(T):
            ins = nc.tensor.transpose(b[0][0:64, t * P:(t + 1) * P], self.stats[:, t].rearrange("p h s c -> p (h s c)"),
                                      k.w("ident"))
        ins.then_inc(k.sem("stats_turned"), 1)
        pe.wait_ge(k.sem("stT"), 1)
        for h in range(H2 + 1):
            if h < H2:
                if h >= 2:
                    pe.wait_ge(k.sem("h1"), h - 1)
                nc.tensor.matmul(b[1 + h % 2][:, :], k.w("L2a_W1x"), k.nT[:, :], start=True, stop=False)
                nc.tensor.matmul(b[1 + h % 2][:, :], k.row("L2a_W1s", h * P, (h + 1) * P, hi=64), self.stT,
                                 start=False, stop=True).then_inc(k.sem("h1_made"), 1)
            if h >= 1:
                g = h - 1
                pe.wait_ge(k.sem("h1"), g + 1)
                for t in range(T):
                    c = (t * H2 + g) * 4
                    ins = nc.tensor.matmul(b[3][:, c:c + 4], self.h1[g % 2][:, t * P:(t + 1) * P], k.w("L2a_W2"),
                                           start=True, stop=True)
                ins.then_inc(k.sem("logits"), 1)
        pe.wait_ge(k.sem("o_normal"), 1)
        for t in range(T):
            ins = nc.tensor.transpose(b[4][:, t * P:(t + 1) * P], self.osq[:, t, :], k.w("ident"))
        ins.then_inc(k.sem("o_turned"), 1)
        pe.wait_ge(k.sem("oT"), 1)
        for t in range(T):
            ins = nc.tensor.matmul(b[5][:, t * D:(t + 1) * D], self.oT[:, t * P:(t + 1) * P], k.w("L2a_Wo"),
                                   start=True, stop=True)
        ins.then_inc(k.sem("out_made"), 1)

    def scalar(self, act):
        k, nc, b = self.k, self.k.nc, self.k.bank
        F = self.st.F.rearrange("p t s (h c) -> p (t s h) c", h=H2)
        nc.scalar.activation(self.sq, F, ACT.Square).then_inc(k.sem("F_squared"), 1)
        act.wait_ge(k.sem("stats_turned"), 1)
        nc.scalar.copy(self.stT, b[0][0:64, :]).then_inc(k.sem("stT"), 1)
        for h in range(H2):
            act.wait_ge(k.sem("h1_made"), h + 1)
            if h >= 2:
                act.wait_ge(k.sem("logits"), h - 1)
            nc.scalar.activation(self.h1[h % 2], b[1 + h % 2][:, :], ACT.Gelu, bias=k.w("L2a_b1"))\
                .then_inc(k.sem("h1"), 1)
        act.wait_ge(k.sem("z_shifted"), 1)
        nc.scalar.activation(self.p, self.z, ACT.Exp).then_inc(k.sem("p_exp"), 1)
        act.wait_ge(k.sem("mixed"), 1)
        nc.scalar.activation(self.osq, self.o, ACT.Square).then_inc(k.sem("o_squared"), 1)
        act.wait_ge(k.sem("o_turned"), 1)
        nc.scalar.copy(self.oT, b[4][:, :]).then_inc(k.sem("oT"), 1)

    def vector(self, dve):
        k, nc, b, own, st = self.k, self.k.nc, self.k.bank, self.k.own["dve"], self.st
        F = st.F.rearrange("p t s (h c) -> p (t s h) c", h=H2)
        own.did(nc.vector.tensor_reduce(self.sum, F, AX.X, ALU.add))
        own.did(nc.vector.tensor_reduce(self.abs, F, AX.X, ALU.add, apply_absolute_value=True))
        dve.wait_ge(k.sem("F_squared"), 1)
        nc.vector.tensor_reduce(self.ss, self.sq, AX.X, ALU.add).then_inc(k.sem("ss"), 1)

        def stat(i):
            return self.stats[:, :, :, :, i].rearrange("p t h s -> p t s h")

        def tsh(v):
            return v.rearrange("p (t s h) -> p t s h", t=T, s=4)
        own.wait()
        own.step(nc.vector.tensor_scalar(self.sum, self.sum, 1.0 / 32, None, ALU.mult))
        own.did(nc.vector.tensor_copy(stat(0), tsh(self.sum)))
        own.did(nc.vector.tensor_scalar(stat(2), tsh(self.abs), 1.0 / 32, None, ALU.mult))
        own.did(nc.vector.tensor_tensor(self.msq, self.sum, self.sum, ALU.mult))
        dve.wait_ge(k.sem("ss"), 1)
        own.wait()
        own.step(nc.vector.scalar_tensor_tensor(self.msq, self.ss, 1.0 / 32, self.msq, ALU.mult, ALU.subtract))
        own.did(nc.vector.tensor_copy(stat(1), tsh(self.msq)))
        dve.wait_ge(k.sem("l2"), 1)
        own.step(nc.vector.tensor_copy(stat(3), tsh(self.l2)))
        nc.vector.sem_inc(k.sem("stats"), 1)
        dve.wait_ge(k.sem("logits"), H2)
        z3 = self.z.rearrange("p (t h) c -> p t h c", t=T)
        z2 = self.z.rearrange("p (t h) c -> p t (h c)", t=T)
        lg = b[3][:, 0:T * 16].rearrange("p (t c) -> p t c", t=T)
        own.step(nc.vector.tensor_tensor(z2, lg, st.prep.bias[:, :].unsqueeze(1).to_broadcast([P, T, 16]), ALU.add))
        for t in range(T):
            own.did(nc.vector.tensor_tensor(z3[:, t], z3[:, t], over(st.prep.rtemp[:, :], P, H2, 4), ALU.mult))
        own.wait()
        own.step(nc.vector.tensor_reduce(self.mx, self.z, AX.X, ALU.max))
        nc.vector.tensor_tensor(self.z, self.z, over(self.mx, P, T * H2, 4), ALU.subtract)\
            .then_inc(k.sem("z_shifted"), 1)
        dve.wait_ge(k.sem("p_exp"), 1)
        for floor in (True, False):
            own.step(nc.vector.tensor_reduce(self.tot, self.p, AX.X, ALU.add))
            own.step(nc.vector.reciprocal(self.rec, self.tot))
            own.step(nc.vector.tensor_tensor(self.p, self.p, over(self.rec, P, T * H2, 4), ALU.mult))
            if floor:
                own.step(nc.vector.tensor_scalar(self.p[:, :, 0:2], self.p[:, :, 0:2], 0.05, None, ALU.max))
        p4 = self.p.rearrange("p (t h) s -> p t h s", t=T)
        own.step(nc.vector.tensor_tensor(p4[:, :, :, 0], p4[:, :, :, 0],
                                         st.prep.share[:, :].unsqueeze(1).to_broadcast([P, T, H2]), ALU.add))
        for t in range(T):
            own.did(nc.vector.tensor_tensor(self.prod[:, t].rearrange("p s (h c) -> p s h c", h=H2),
                                            st.F[:, t].rearrange("p s (h c) -> p s h c", h=H2),
                                            over(p4[:, t].rearrange("p h s -> p s h"), P, 4, H2, 32), ALU.mult))
        own.wait()
        for t in range(T):
            ins = nc.vector.tensor_reduce(self.o[:, t, :], self.prod[:, t].rearrange("p s d -> p d s"), AX.X, ALU.add)
        ins.then_inc(k.sem("mixed"), 1)
        dve.wait_ge(k.sem("o_squared"), 1)
        heads = lambda v: v.rearrange("p t (h c) -> p (t h) c", h=H2)
        own.step(nc.vector.tensor_reduce(self.oss, heads(self.osq), AX.X, ALU.add))
        nc.vector.tensor_scalar(self.oss, self.oss, 1.0 / 32, 1e-5, ALU.mult, ALU.add).then_inc(k.sem("o_ms"), 1)
        dve.wait_ge(k.sem("o_rs"), 1)
        own.step(nc.vector.tensor_tensor(heads(self.o), heads(self.o), over(self.ors, P, T * H2, 32), ALU.mult))
        nc.vector.tensor_tensor(heads(self.osq), heads(self.o),
                                k.w("L2a_rms_w").unsqueeze(1).to_broadcast([P, T * H2, 32]), ALU.mult)\
            .then_inc(k.sem("o_normal"), 1)
        dve.wait_ge(k.sem("out_made"), 1)
        nc.vector.tensor_tensor(k.x[:, :, :], k.x[:, :, :], b[5][:, :].rearrange("p (t d) -> p t d", t=T), ALU.add)

    def gpsimd(self, pool):
        k, nc = self.k, self.k.nc
        pool.wait_ge(k.sem("ss"), 1)
        nc.gpsimd.tensor_tensor(self.l2, self.ss, k.row("half", 0, 1).to_broadcast([P, T * 16]), ALU.pow)\
            .then_inc(k.sem("l2"), 1)
        pool.wait_ge(k.sem("o_ms"), 1)
        nc.gpsimd.tensor_tensor(self.ors, self.oss, k.row("minus_half", 0, 1).to_broadcast([P, T * H2]), ALU.pow)\
            .then_inc(k.sem("o_rs"), 1)

    def sync(self, sp):
        pass


def l2attn_weights(i, tiles, spread):
    a = {n: i["L2_attn_" + n] for n in ("Wq", "Wk", "Wv", "Wb", "conv_q", "conv_k", "conv_v", "W2", "Wo", "W1")}
    stats = np.zeros((64, H2, P), np.float32)
    for h in range(H2):
        stats[16 * h:16 * h + 16, h] = a["W1"][D:]
    chunk = np.kron(np.eye(4, dtype=np.float32), np.ones((32, 32), np.float32))
    w = {"L2a_" + n: v for n, v in a.items() if n != "W1"}
    w.update({
        "L2a_W1x": a["W1"][:D], "L2a_W1s": stats.reshape(64, H2 * P),
        "L2a_fir_long": i["L2_attn_fir_long"].reshape(P, FIR)[:, :PE_TAPS],
        "L2a_fir_long_rest": i["L2_attn_fir_long"].reshape(P, FIR)[:, PE_TAPS:], "L2a_fir_short": i["L2_attn_fir_short"].reshape(P, 5),
        "L2a_b1": i["L2_attn_b1"].reshape(P, 1),
        "L2a_b2": spread(np.concatenate([i["L2_attn_b2"]] * H2)), "L2a_base_bias": spread(i["L2_attn_base_bias"]),
        "L2a_log_temp": spread(i["L2_attn_log_temp"]), "L2a_residual_logit": spread(i["L2_attn_conv_residual_logit"]),
        "L2a_rms_w": spread(i["L2_attn_rms_w"]),
        "half": np.full((P, 1), 0.5, np.float32),
        "blocks32": chunk, "chunk_lower": np.tril(chunk, -1), "chunk_upper": np.triu(chunk),
    })
    r = np.arange(P)
    for size in (1, 2, 4, 8, 16):
        low = ((r[:, None] // (2 * size) == r[None, :] // (2 * size)) & (r[:, None] // size % 2 == 1)
               & (r[None, :] // size % 2 == 0)).astype(np.float32)
        w[f"above{size}"] = low.T
        if size == 1:
            w["below1"] = low
    return w


MORE_WEIGHTS += [l2attn_weights]


H3 = 16


class PrepL3:

    def __init__(self, kit):
        self.k = kit

        def keep(name, n):
            return kit.ctx.enter_context(kit.nc.sbuf_tensor("l3_" + name, [P, n], F32))
        self.L = keep("decay", H3 * 2 * P)
        self.ad, self.dt = keep("A_dt", H3), keep("dt", H3)
        self.t = [keep(f"t{i}", H3) for i in range(7)]

    def scalar(self, act):
        k, nc, t = self.k, self.k.nc, self.t
        nc.scalar.activation(t[0][:, :], k.w("L3a_dt_bias"), ACT.Abs).then_inc(k.sem("dt_abs"), 1)
        act.wait_ge(k.sem("dt_abs"), 1)
        nc.scalar.activation(t[1][:, :], t[0][:, :], ACT.Exp, scale=-1.0).then_inc(k.sem("dt_exp"), 1)
        nc.scalar.activation(t[6][:, :], k.w("L3a_A_log"), ACT.Exp).then_inc(k.sem("A_exp"), 1)
        act.wait_ge(k.sem("A_dt"), 1)
        for h in range(H3):
            nc.scalar.activation(self.L[:, h * 256:(h + 1) * 256], k.w("L3a_diff"), ACT.Exp,
                                 scale=self.ad[:, h:h + 1]).then_inc(k.sem("decay"), 1)

    def vector(self, dve):
        k, nc, own, t = self.k, self.k.nc, self.k.own["dve"], self.t
        dve.wait_ge(k.sem("dt_exp"), 1)
        own.step(softplus(k, self.dt[:, :], k.w("L3a_dt_bias"), t[1][:, :], t[2][:, :], t[3][:, :]))
        dve.wait_ge(k.sem("A_exp"), 1)
        own.step(nc.vector.scalar_tensor_tensor(t[4][:, :], t[6][:, :], -1.0, self.dt[:, :], ALU.mult, ALU.mult))
        nc.vector.tensor_scalar(self.ad[:, :], t[4][:, :], -1e30, None, ALU.max).then_inc(k.sem("A_dt"), 1)
        for h in range(H3):
            dve.wait_ge(k.sem("decay"), h + 1)
            v = self.L[:, h * 256:(h + 1) * 256]
            nc.vector.scalar_tensor_tensor(v, v, self.dt[:, h:h + 1], k.w("L3a_reach"), ALU.mult, ALU.mult)

    def tensor(self, pe):
        pass

    gpsimd = sync = tensor


class L3State:

    def __init__(self, kit, prep):
        self.prep, self.mem = prep, Arena(kit)
        self.x0, self.xm, self.t = self.mem(T, D), self.mem(T, D), self.mem(T, D)
        self.after = self.mem.at


def rows_of(kit, name, shape):
    return kit.w(name).unsqueeze(1).to_broadcast(shape)


def remix(kit, st, src, name):
    nc, own, sh = kit.nc, kit.own["dve"], [P, T, D]
    own.did(nc.vector.tensor_tensor(st.t, st.x0, rows_of(kit, name + "1", sh), ALU.mult))
    own.step(nc.vector.tensor_tensor(st.xm, src, rows_of(kit, name + "0", sh), ALU.mult))
    own.step(nc.vector.tensor_tensor(st.xm, st.xm, st.t, ALU.add))


def add_scaled(kit, st, y, name):
    nc, own, sh = kit.nc, kit.own["dve"], [P, T, D]
    own.step(nc.vector.tensor_tensor(st.t, y, rows_of(kit, name, sh), ALU.mult))
    ins = nc.vector.tensor_tensor(st.xm, st.xm, st.t, ALU.add)
    return ins


RMS_EPS = float(np.finfo(np.float32).eps)


class L3Mamba:

    def __init__(self, kit, st):
        self.k, self.st = kit, st
        mem = st.mem
        mem.at = st.after
        self.norm0 = Norm(kit, mem, kit.x, 1e-5)
        self.norm = Norm(kit, mem, st.xm, RMS_EPS, rms=True, tag="_m")
        self.xT = mem(GT)
        self.pad = [mem(NB, 3 + SEQ) for _ in range(2)]
        self.c = [[mem(NB, SEQ) for _ in range(2)] for _ in range(2)]
        self.val = [mem(GT) for _ in range(2)]
        self.v = mem(T, 256)
        self.sg = mem(T, 256)
        self.gate = mem(T, 256)
        self.B = [mem(GT) for _ in range(2)]
        self.C = [mem(GT) for _ in range(2)]
        self.S = [mem(3 * P) for _ in range(4)]
        self.yv = mem(T, 256)
        self.yT = [mem(GT) for _ in range(2)]
        self.units = [(j, s, hh) for j in range(8) for s in range(NB) for hh in range(2)]

    def tensor(self, pe):
        k, nc, b = self.k, self.k.nc, self.k.bank
        for t in range(T):
            pe.wait_ge(k.sem("xm_mixed"), 1)
            ins = nc.tensor.transpose(b[6][:, t * P:(t + 1) * P], self.st.xm[:, t, :], k.w("ident"))
        ins.then_inc(k.sem("xm_turned"), 1)
        self.norm.tensor(pe, b[7])
        pe.wait_ge(k.sem("nT_m"), 1)
        for i in range(2):
            nc.tensor.matmul(b[i][:, :], k.row("L3a_in", i * P, (i + 1) * P), k.nT[:, :], start=True, stop=True)\
                .then_inc(k.sem("value_made"), 1)
        for t in range(T):
            ins = nc.tensor.matmul(b[2 + t // 2][:, (t % 2) * 256:(t % 2) * 256 + 256], k.nT[:, t * P:(t + 1) * P],
                                   k.row("L3a_in", 256, 512), start=True, stop=True)
            if t % 2 == 1:
                ins.then_inc(k.sem("gate_made"), 1)
        for i in range(2):
            pe.wait_ge(k.sem("value"), i + 1)
            for t in range(T):
                ins = nc.tensor.transpose(b[4 + i][:, t * P:(t + 1) * P], self.val[i][:, t * P:(t + 1) * P],
                                          k.w("ident"))
            ins.then_inc(k.sem("value_turned"), 1)

        def bc(j):
            if j >= 1:
                pe.wait_ge(k.sem("B"), j)
                pe.wait_ge(k.sem("C"), j)
            nc.tensor.matmul(b[0][:, :], k.row("L3a_B", j * P, (j + 1) * P), self.xT, start=True, stop=True)\
                .then_inc(k.sem("B_made"), 1)
            nc.tensor.matmul(b[1][:, :], k.row("L3a_C", j * P, (j + 1) * P), self.xT, start=True, stop=True)\
                .then_inc(k.sem("C_made"), 1)

        def gram(n):
            j, s, hh = self.units[n]
            pe.wait_ge(k.sem("B"), j + 1)
            pe.wait_ge(k.sem("C"), j + 1)
            if n >= 4:
                pe.wait_ge(k.sem("S"), n - 3)
            rows = slice(64 * hh, 64 * hh + 64)
            B, C, at = self.B[j % 2], self.C[j % 2], s * SEQ
            o = b[2 + n % 4]
            nc.tensor.matmul(o[:, 0:SEQ], B[rows, at:at + P], C[rows, at:at + SEQ], start=True, stop=True)
            nc.tensor.matmul(o[:, SEQ:SEQ + P], B[rows, at + P:at + SEQ], C[rows, at + P:at + SEQ],
                             start=True, stop=True).then_inc(k.sem("gram"), 1)

        def scan(n):
            j, s, hh = self.units[n]
            pe.wait_ge(k.sem("S"), n + 1)
            h = 2 * j + hh
            S = self.S[n % 4]
            o = b[6 + s]
            c = slice(h * 16, h * 16 + 16)
            nc.tensor.matmul(o[:, c], S[:, 0:P], self.v[:, 2 * s, c], start=True, stop=True)
            o1 = o[:, 256 + h * 16:256 + h * 16 + 16]
            nc.tensor.matmul(o1, S[:, P:2 * P], self.v[:, 2 * s, c], start=True, stop=False)
            nc.tensor.matmul(o1, S[:, 2 * P:3 * P], self.v[:, 2 * s + 1, c], start=False, stop=True)\
                .then_inc(k.sem("scanned"), 1)

        pe.wait_ge(k.sem("padded"), 2)
        pe.wait_ge(k.sem("xT"), 1)
        bc(0)
        pe.wait_ge(k.sem("gate"), 2)
        pe.wait_ge(k.sem("v_tok"), 2)
        n_units = len(self.units)
        for n in range(n_units + 2):
            if n < n_units:
                if n % 4 == 0 and n // 4 + 1 < 8:
                    if n // 4 + 1 >= 2:
                        pass
                    bc(n // 4 + 1)
                gram(n)
            if n >= 2:
                scan(n - 2)
        pe.wait_ge(k.sem("y_gated"), 1)
        for i in range(2):
            for t in range(T):
                ins = nc.tensor.transpose(b[i][:, t * P:(t + 1) * P], self.yv[:, t, i * P:(i + 1) * P], k.w("ident"))
            ins.then_inc(k.sem("y_turned"), 1)
        pe.wait_ge(k.sem("yT"), 2)
        for t in range(T):
            for i in range(2):
                ins = nc.tensor.matmul(b[2][:, t * D:(t + 1) * D], self.yT[i][:, t * P:(t + 1) * P],
                                       k.row("L3a_out", i * D, (i + 1) * D), start=(i == 0), stop=(i == 1))
        ins.then_inc(k.sem("out_made"), 1)

    def scalar(self, act):
        k, nc, b = self.k, self.k.nc, self.k.bank
        act.wait_ge(k.sem("xm_turned"), 1)
        nc.scalar.copy(self.xT, b[6][:, :]).then_inc(k.sem("xT"), 1)
        self.norm.scalar(act, b[7])
        for i in range(2):
            act.wait_ge(k.sem("value_made"), i + 1)
            nc.scalar.copy(self.pad[i][:, :, 3:], b[i][:, :].rearrange("p (b s) -> p b s", b=NB))\
                .then_inc(k.sem("padded"), 1)
        for i in range(2):
            act.wait_ge(k.sem("gate_made"), i + 1)
            nc.scalar.activation(self.sg[:, 2 * i:2 * i + 2, :], b[2 + i][:, :].rearrange("p (t c) -> p t c", t=2),
                                 ACT.Sigmoid).then_inc(k.sem("gate_sigmoid"), 1)
        for i in range(2):
            act.wait_ge(k.sem(f"conv{i}"), 4)
            nc.scalar.activation(self.c[i][0], self.c[i][1], ACT.Sigmoid).then_inc(k.sem("value_sigmoid"), 1)
        for j in range(8):
            act.wait_ge(k.sem("B_made"), j + 1)
            if j >= 2:
                act.wait_ge(k.sem("gram"), 4 * (j - 1))
            nc.scalar.copy(self.B[j % 2], b[0][:, :]).then_inc(k.sem("B"), 1)
            act.wait_ge(k.sem("C_made"), j + 1)
            nc.scalar.copy(self.C[j % 2], b[1][:, :]).then_inc(k.sem("C"), 1)
        for i in range(2):
            act.wait_ge(k.sem("y_turned"), i + 1)
            nc.scalar.copy(self.yT[i], b[i][:, :]).then_inc(k.sem("yT"), 1)

    def vector(self, dve):
        k, nc, b, own, st = self.k, self.k.nc, self.k.bank, self.k.own["dve"], self.st
        for i in range(2):
            own.did(nc.vector.memset(self.pad[i][:, :, 0:3], 0.0))
        self.norm0.vector(dve)
        dve.wait_ge(k.sem("norm_n"), T)
        own.step(nc.vector.tensor_copy(st.x0, k.n[:, :, :]))
        remix(k, st, st.x0, "L3a_mix_m")
        nc.vector.sem_inc(k.sem("xm_mixed"), 1)
        self.norm.vector(dve)
        for i in range(2):
            dve.wait_ge(k.sem("padded"), i + 1)
            for j in range(4):
                s = self.pad[i][:, :, j:j + SEQ]
                w = k.row("L3a_conv", 4 * i + j, 4 * i + j + 1)
                if j == 0:
                    ins = nc.vector.tensor_scalar(self.c[i][0], s, w, k.row("L3a_conv_b", i, i + 1), ALU.mult, ALU.add)
                else:
                    dve.wait_ge(k.sem(f"conv{i}"), j)
                    ins = nc.vector.scalar_tensor_tensor(self.c[i][j % 2], s, w, self.c[i][(j + 1) % 2],
                                                         ALU.mult, ALU.add)
                ins.then_inc(k.sem(f"conv{i}"), 1)
        for i in range(2):
            dve.wait_ge(k.sem("gate_sigmoid"), i + 1)
            nc.vector.tensor_tensor(self.gate[:, 2 * i:2 * i + 2, :], self.sg[:, 2 * i:2 * i + 2, :],
                                    b[2 + i][:, :].rearrange("p (t c) -> p t c", t=2), ALU.mult)\
                .then_inc(k.sem("gate"), 1)
        for i in range(2):
            dve.wait_ge(k.sem("value_sigmoid"), i + 1)
            nc.vector.tensor_tensor(self.val[i].rearrange("p (b s) -> p b s", b=NB), self.c[i][0], self.c[i][1],
                                    ALU.mult).then_inc(k.sem("value"), 1)
        for i in range(2):
            dve.wait_ge(k.sem("value_turned"), i + 1)
            nc.vector.tensor_copy(self.v[:, :, i * P:(i + 1) * P], b[4 + i][:, :].rearrange("p (t c) -> p t c", t=T))\
                .then_inc(k.sem("v_tok"), 1)
        for n, (j, s, hh) in enumerate(self.units):
            h = 2 * j + hh
            L = st.prep.L[:, h * 256:(h + 1) * 256]
            dve.wait_ge(k.sem("gram"), n + 1)
            if n >= 4:
                dve.wait_ge(k.sem("scanned"), n - 3)
            o = b[2 + n % 4]
            nc.vector.tensor_tensor(self.S[n % 4][:, 0:SEQ], o[:, 0:SEQ], L, ALU.mult)
            nc.vector.tensor_tensor(self.S[n % 4][:, SEQ:], o[:, SEQ:3 * P], L[:, 0:P], ALU.mult)\
                .then_inc(k.sem("S"), 1)
        dve.wait_ge(k.sem("v_tok"), 2)
        own.step(nc.vector.tensor_tensor(self.yv, self.v, k.w("L3a_D").unsqueeze(1).to_broadcast([P, T, 256]), ALU.mult))
        dve.wait_ge(k.sem("scanned"), len(self.units))
        for s in range(NB):
            own.did(nc.vector.tensor_tensor(self.yv[:, 2 * s:2 * s + 2, :], self.yv[:, 2 * s:2 * s + 2, :],
                                            b[6 + s][:, :].rearrange("p (t c) -> p t c", t=2), ALU.add))
        own.wait()
        nc.vector.tensor_tensor(self.yv, self.yv, self.gate, ALU.mult).then_inc(k.sem("y_gated"), 1)
        dve.wait_ge(k.sem("out_made"), 1)
        add_scaled(k, st, b[2][:, :].rearrange("p (t d) -> p t d", t=T), "L3a_mamba_scale")

    def gpsimd(self, pool):
        self.norm0.gpsimd(pool)
        self.norm.gpsimd(pool)

    def sync(self, sp):
        pass


class L3Mlp:

    def __init__(self, kit, st, which, last):
        self.k, self.st, self.which, self.last = kit, st, which, last
        mem = st.mem
        mem.at = st.after
        self.norm = Norm(kit, mem, st.xm, RMS_EPS, rms=True)
        self.mlp = Mlp(kit, mem, kit.nT, 4, 4, "square", ACT.Relu,
                       first=lambda u: kit.row(f"L3a_{which}_fc", u * P, (u + 1) * P),
                       down=lambda u: kit.row(f"L3a_{which}_proj", u * P, (u + 1) * P), use=self.use)

    def use(self, e, y):
        k = self.k
        return add_scaled(k, self.st, y[:, :].rearrange("p (t d) -> p t d", t=T), f"L3a_{self.which}_mlp_scale")

    def tensor(self, pe):
        self.norm.tensor(pe, self.k.bank[7])
        pe.wait_ge(self.k.sem("nT"), 1)
        self.mlp.tensor(pe)

    def scalar(self, act):
        self.norm.scalar(act, self.k.bank[7])
        self.mlp.scalar(act)

    def vector(self, dve):
        self.norm.vector(dve)
        self.mlp.vector(dve)
        if self.last:
            dve.wait_ge(self.k.sem("y_used"), 1)
            self.k.nc.vector.tensor_tensor(self.k.x[:, :, :], self.k.x[:, :, :], self.st.xm, ALU.add)

    def gpsimd(self, pool):
        self.norm.gpsimd(pool)

    def sync(self, sp):
        pass


class L3Attention:

    def __init__(self, kit, st):
        self.k, self.st = kit, st
        mem = st.mem
        mem.at = st.after
        self.norm = Norm(kit, mem, st.xm, RMS_EPS, rms=True)
        self.heads = Heads(kit, mem, 4, "L3a_", True, self.deliver)

    def deliver(self, y):
        add_scaled(self.k, self.st, y, "L3a_attn_scale")

    def tensor(self, pe):
        self.norm.tensor(pe, self.k.bank[7])
        pe.wait_ge(self.k.sem("nT"), 1)
        self.heads.tensor(pe)

    def scalar(self, act):
        self.norm.scalar(act, self.k.bank[7])
        self.heads.scalar(act)

    def vector(self, dve):
        remix(self.k, self.st, self.st.xm, "L3a_mix_a")
        self.norm.vector(dve)
        self.heads.vector(dve)

    def gpsimd(self, pool):
        self.norm.gpsimd(pool)
        self.heads.gpsimd(pool)

    def sync(self, sp):
        pass


def l3attn_weights(i, tiles, spread):
    a = lambda n: i["L3_attn_" + n]
    q, kk = np.arange(P)[None, :], np.arange(P)[:, None]
    return {
        "L3a_in": a("in_proj_w"), "L3a_B": a("B_proj_w"), "L3a_C": a("C_proj_w"), "L3a_out": tiles(a("out_proj_w"), D),
        "L3a_conv": tiles(a("conv_w"), 4), "L3a_conv_b": a("conv_b").reshape(2, P).T,
        "L3a_D": spread(np.repeat(a("D_param"), 16)),
        "L3a_dt_bias": spread(a("dt_bias")), "L3a_A_log": spread(a("A_log")),
        "L3a_diff": np.concatenate([np.maximum(q - kk, 0), q - kk + P], 1).astype(np.float32),
        "L3a_reach": np.concatenate([(q >= kk), np.ones((P, P), bool)], 1).astype(np.float32),
        "L3a_mix_m0": spread(a("resid_mix_m")[0]), "L3a_mix_m1": spread(a("resid_mix_m")[1]),
        "L3a_mix_a0": spread(a("resid_mix_a")[0]), "L3a_mix_a1": spread(a("resid_mix_a")[1]),
        "L3a_mamba_scale": spread(a("mamba_scale")), "L3a_attn_scale": spread(a("attn_scale")),
        "L3a_m_mlp_scale": spread(a("m_mlp_scale")), "L3a_a_mlp_scale": spread(a("a_mlp_scale")),
        "L3a_m_fc": a("m_fc_w"), "L3a_m_proj": tiles(a("m_proj_w"), D),
        "L3a_a_fc": a("a_fc_w"), "L3a_a_proj": tiles(a("a_proj_w"), D),
    }


MORE_WEIGHTS += [l3attn_weights]


GROUP_STAGES = ("L1f", "L1a", "L1f", "L2f", "L2a", "L2f", "L3f", "L3a", "L3f")


def make_stage(kit, name, shared):
    if name == "L1f":
        return L1Ffn(kit)
    if name == "L1a":
        return L1Attn(kit, shared["l1"])
    if name == "L2f":
        return L2Ffn(kit, shared["bin"])
    if name == "L2a":
        st = L2State(kit, shared["l2"])
        return [L2Project(kit, st), L2Delta(kit, st), L2Mix(kit, st)]
    if name == "L3f":
        return L3Ffn(kit)
    if name == "L3a":
        st = L3State(kit, shared["l3"])
        return [L3Mamba(kit, st), L3Mlp(kit, st, "m", False), L3Attention(kit, st), L3Mlp(kit, st, "a", True)]
    raise KeyError(name)


def build(nc, dram, out, columns, width, plan=None):
    plan = plan or (True, GROUP_STAGES)
    with ExitStack() as ctx:
        kit = Kit(nc, ctx, columns, width)
        shared = {"const": Constants(kit), "bin": Binarise(kit), "l1": PrepL1(kit), "l2": PrepL2(kit), "l3": PrepL3(kit)}
        kinds = {}
        for s in plan[1]:
            if s not in kinds:
                kinds[s] = make_stage(kit, s, shared)
        stages = []
        for s in plan[1]:
            stages += kinds[s] if isinstance(kinds[s], list) else [kinds[s]]
        if plan[0]:
            y = [nc.dram_tensor(f"between_{i}", [TOKENS, D], F32).ap() for i in range(3)]
            n_ext = nc.dram_tensor("n_and_scores", [TOKENS, NEXT], F32).ap()
            l0 = L0Ffn(kit, dram)
            l0a = L0Attn(kit)
            chain = [(l0, dram["x"], y[0]), (l0a, y[0], y[1]), (l0, y[1], y[2])]
            if plan[0] == 1.5:
                chain = chain[:1]
            src = chain[-1][2]
        else:
            chain, src = [], dram["x"]
        to_l3 = max([n for n, st in enumerate(stages) if isinstance(st, L1Ffn)], default=-1) + 1
        at_l3 = min([n for n, st in enumerate(stages) if isinstance(st, L3Ffn)], default=-1)
        if at_l3 < 0:
            to_l3 = -1
        elif at_l3 == 0:
            dram = dict(dram, weights_L1f=dram["weights_L3f"])
            to_l3, at_l3 = -1, -1
        block = ctx.enter_context(nc.Block())

        def whole(eng, name, method):
            kit.stage = 0
            kit.own = {name: Own(eng, kit.own_sems[name])} if name in kit.own_sems else {}
            if name != "sp":
                eng.wait_ge(kit.weights_in, 16 * WEIGHT_DMAS)
            else:
                page_loaded(kit, eng)
            kit.end(eng, name)
            for stage in shared.values():
                method(stage)(eng)
                kit.end(eng, name)
            for stage, a, b in chain:
                stage.run(eng, name, method, a, b, n_ext if plan[0] else None)
            with eng.Fori(0, GROUPS) as g:
                if name == "sp":
                    load_page(kit, eng, dram["weights_L1f"])
                    load_group(kit, eng, src, g)
                    page_loaded(kit, eng)
                kit.end(eng, name)
                for n, stage in enumerate(stages):
                    if name == "sp" and n == to_l3:
                        load_page(kit, eng, dram["weights_L3f"])
                    method(stage)(eng)
                    if name == "sp" and (n == at_l3 - 1 or (at_l3 == 0 and n == 0)):
                        page_loaded(kit, eng)
                    kit.end(eng, name)
                if name == "sp":
                    store_group(kit, eng, out, g)
                kit.end(eng, name)

        @block.sync
        def _(sp):
            load_page(kit, sp, dram["weights_first"])
            n = width["resident"]
            step = (n + WEIGHT_DMAS - 1) // WEIGHT_DMAS
            for i in range(WEIGHT_DMAS):
                a, b = i * step, min(n, (i + 1) * step)
                sp.dma_start(kit.W["resident"][:, a:b], dram["weights_resident"][:, a:b])\
                    .then_inc(kit.weights_in, 16)
            whole(sp, "sp", lambda s: s.sync)

        @block.scalar
        def _(act):
            whole(act, "act", lambda s: s.scalar)

        @block.vector
        def _(dve):
            whole(dve, "dve", lambda s: s.vector)

        @block.tensor
        def _(pe):
            whole(pe, "pe", lambda s: s.tensor)

        @block.gpsimd
        def _(pool):
            whole(pool, "pool", lambda s: s.gpsimd)


WEIGHT_DMAS = 8


def load_group(kit, sp, src, g):
    v = src.rearrange("(g t p) d -> p g t d", g=GROUPS, p=P)
    sp.dma_start(kit.x[:, :, :], v[:, bass.ds(g, 1)].rearrange("p o t d -> p (o t) d")).then_inc(kit.sem("x_in"), 16)
    sp.wait_ge(kit.sem("x_in"), 16)


def store_group(kit, sp, dst, g):
    v = dst.rearrange("(g t p) d -> p g t d", g=GROUPS, p=P)
    sp.dma_start(v[:, bass.ds(g, 1)].rearrange("p o t d -> p (o t) d"), kit.x[:, :, :]).then_inc(kit.sem("x_out"), 16)
    sp.wait_ge(kit.sem("x_out"), 16)


def pack(i):
    def tiles(a, cols):
        n = a.shape[0] // P
        return a.reshape(n, P, cols).transpose(1, 0, 2).reshape(P, n * cols)

    def spread(a):
        a = a.reshape(1, -1)
        return np.broadcast_to(a, (P, a.shape[1]))

    part = np.arange(P)
    w = {
        "ident": np.eye(P, dtype=np.float32),
        "ones": np.ones((P, P), np.float32),
        "minus_half": np.full((P, 8), -0.5, np.float32),
        "iota8": spread(np.arange(8, dtype=np.float32)),
        "L1f_gate": i["L1_ffn_gate_w"].transpose(1, 0, 2).reshape(P, -1),
        "L1f_up": i["L1_ffn_up_w"].transpose(1, 0, 2).reshape(P, -1),
        "L1f_down": tiles(i["L1_ffn_down_w"].reshape(-1, D), D),
        "L1f_gate_b": i["L1_ffn_gate_b"].reshape(-1, P).T,
        "L1f_up_b": i["L1_ffn_up_b"].reshape(-1, P).T,
        "L1f_down_b": i["L1_ffn_down_b"],
        "L1f_router": i["L1_ffn_router_w"].T,
        "L2f_w1": tiles(i["L2_ffn_w1"], D),
        "L2f_w2": i["L2_ffn_w2"],
        "L2f_b1": i["L2_ffn_b1"].reshape(4, P).T,
        "L2f_b2": i["L2_ffn_b2"].reshape(1, D),
    }
    for more in MORE_WEIGHTS:
        w.update(more(i, tiles, spread))
    columns, arrays = {}, {}
    for page, prefixes in PAGES.items():
        mine = [n for n in w if n.startswith(prefixes)] if prefixes else \
            [n for n in w if not any(p and n.startswith(p) for p in PAGES.values())]
        at, parts = 0, []
        for name in mine:
            a = w[name]
            columns[name] = ("page" if prefixes else "resident", at, a.shape[0], a.shape[1])
            if a.shape[0] < P:
                a = np.concatenate([a, np.zeros((P - a.shape[0], a.shape[1]), np.float32)], 0)
            parts.append(a)
            at += a.shape[1]
        assert not prefixes or at <= PAGE
        arrays["weights_" + page] = np.ascontiguousarray(np.concatenate(parts, 1))
    return columns, arrays


PAGES = {
    "first": ("L0f_", "L0a_", "L2f_w", "L3a_diff", "L3a_reach", "L2a_fir_long_pe", "below_", "token_parts", "iota256",
              "mask_neg"),
    "L1f": ("L1f_gate", "L1f_up", "L1f_down"),
    "L3f": ("L3f_W1", "L3f_W2"),
    "resident": (),
}


def load_page(kit, sp, src, parts=4):
    n = src.shape[1]
    step = (n + parts - 1) // parts
    for i in range(parts):
        a, b = i * step, min(n, (i + 1) * step)
        sp.dma_start(kit.W["page"][:, a:b], src[:, a:b]).then_inc(kit.page_in, 16)


def page_loaded(kit, sp, parts=4):
    sp.wait_ge(kit.page_in, 16 * parts)
    sp.sem_clear(kit.page_in)


def kernel(**inputs):
    from concourse import bacc
    from concourse.bass_utils import run_bass_kernel_spmd

    i = {name: np.asarray(a) for name, a in inputs.items()}
    columns, arrays = pack(i)
    arrays.update(extra_inputs(i))
    arrays["x"] = np.ascontiguousarray(i["L0_attn_x"].reshape(TOKENS, D))
    nc = bacc.Bacc("TRN2", target_bir_lowering=False, num_devices=1)
    dram = {name: nc.dram_tensor(name, a.shape, F32, kind="ExternalInput").ap() for name, a in arrays.items()}
    out = nc.dram_tensor("out", (TOKENS, D), F32, kind="ExternalOutput").ap()
    build(nc, dram, out, columns, {"resident": arrays["weights_resident"].shape[1]})
    r = run_bass_kernel_spmd(nc, [arrays], core_ids=[0])
    return r.results[0]["out"].reshape(i["L0_attn_x"].shape)
```

```python
from contextlib import ExitStack

import numpy as np

import concourse.bass as bass
from concourse import mybir

F32 = mybir.dt.float32
BF16 = mybir.dt.bfloat16
I32 = mybir.dt.int32
U32 = mybir.dt.uint32
ALU = mybir.AluOpType
ACT = mybir.ActivationFunctionType
AX = mybir.AxisListType

P = 128
D = 128
SEQ = 256
TOKENS = 2048
GROUPS = 4
GT = TOKENS // GROUPS
T = GT // P
NB = GT // SEQ
ARENA = 17120
PAGE = 8192
STAGE_SEMS = 72


class Own:

    def __init__(self, eng, sem):
        self.eng, self.sem, self.n = eng, sem, 0

    def did(self, ins):
        self.n += 1
        ins.then_inc(self.sem, 1)

    def wait(self):
        if self.n:
            self.eng.wait_ge(self.sem, self.n)

    def step(self, ins):
        self.did(ins)
        self.wait()


class Kit:

    def __init__(self, nc, ctx, columns, width):
        self.nc, self.ctx, self.columns = nc, ctx, columns
        self.W = {"resident": ctx.enter_context(nc.sbuf_tensor("weights_sb", [P, width["resident"]], F32)),
                  "page": ctx.enter_context(nc.sbuf_tensor("weights_page", [P, PAGE], F32))}
        self.page_in = ctx.enter_context(nc.semaphore("page_in"))
        self.arena = ctx.enter_context(nc.sbuf_tensor("arena", [P, ARENA], F32))
        self.x = ctx.enter_context(nc.sbuf_tensor("x_res", [P, T, D], F32))
        self.n = ctx.enter_context(nc.sbuf_tensor("n_tok", [P, T, D], F32))
        self.nT = ctx.enter_context(nc.sbuf_tensor("nT", [P, GT], F32))
        self.x_next = ctx.enter_context(nc.sbuf_tensor("x_next", [P, T, D], F32))
        self.x_out = ctx.enter_context(nc.sbuf_tensor("x_out", [P, T, D], F32))
        self.next_in = ctx.enter_context(nc.semaphore("x_next_in"))
        self.out_done = ctx.enter_context(nc.semaphore("x_out_done"))
        self.identb = ctx.enter_context(nc.sbuf_tensor("ident_bf16", [P, 2 * P], BF16))
        self.maskb = ctx.enter_context(nc.sbuf_tensor("mask_bf16", [P, 2 * P], BF16))
        self.selb = ctx.enter_context(nc.sbuf_tensor("head_rows_bf16", [P, 16 * P], BF16))
        self.bank = [ctx.enter_context(nc.psum_tensor(f"bank{i}", [P, 512], F32)) for i in range(8)]
        self.arrived = ctx.enter_context(nc.semaphore("stage_arrived"))
        self.go = {e: ctx.enter_context(nc.semaphore(f"stage_go_{e}")) for e in ("pe", "act", "dve", "pool")}
        self.pads_in = ctx.enter_context(nc.semaphore("pads_in"))
        self.base_in = ctx.enter_context(nc.semaphore("base_in"))
        self.weights_in = ctx.enter_context(nc.semaphore("weights_in"))
        self.own_sems = {e: ctx.enter_context(nc.semaphore(f"own_{e}")) for e in ("act", "dve", "pool")}
        self.stage_sems = [ctx.enter_context(nc.semaphore(f"of_stage_{i}")) for i in range(STAGE_SEMS)]
        self.first, self.last = self.own_sems["act"].num, self.stage_sems[-1].num
        self.own = {}
        self.stage, self.names = 0, {}

    def sem(self, name):
        names = self.names.setdefault(self.stage, {})
        if name not in names:
            names[name] = self.stage_sems[len(names)]
        return names[name]

    def w(self, name):
        where, at, rows, n = self.columns[name]
        return self.W[where][0:rows, at:at + n]

    def row(self, name, a, b, lo=0, hi=None):
        where, at, rows, n = self.columns[name]
        return self.W[where][lo:rows if hi is None else hi, at + a:at + b]

    def end(self, eng, name):
        self.stage += 1
        eng.drain()
        if name == "sp":
            eng.wait_ge(self.arrived, 4)
            eng.sem_clear(range(self.arrived.num, self.arrived.num + 1))
            eng.sem_clear(range(self.first, self.last + 1))
            for e in self.go:
                eng.sem_inc(self.go[e], 1)
        else:
            eng.sem_inc(self.arrived, 1)
            eng.wait_ge(self.go[name], 1)
            eng.sem_clear(self.go[name])
            if name in self.own:
                self.own[name].n = 0


class Stream:

    AHEAD = 2

    def __init__(self, kit, src, dst):
        self.k = kit
        self.src, self.dst = [v.rearrange("(g t p) d -> p g t d", t=T, p=P) for v in (src, dst)]

    def load(self, sp, g):
        sp.dma_start(self.k.x_next[:, :, :], self.src[:, bass.ds(g, 1)].rearrange("p o t d -> p (o t) d"))\
            .then_inc(self.k.next_in, 16)

    def begin(self, eng, name):
        k = self.k
        if name == "sp":
            self.load(eng, 0)
            eng.wait_ge(k.next_in, 16)
            eng.sem_clear(range(k.next_in.num, k.next_in.num + 1))
            eng.sem_inc(k.out_done, 16)
            eng.sem_inc(k.sem("next_here"), 1)
        elif name == "dve":
            eng.wait_ge(k.sem("next_here"), 1)
            k.nc.vector.tensor_copy(k.x[:, :, :], k.x_next[:, :, :])
        k.end(eng, name)
        if name == "sp":
            self.load(eng, 1)

    def swap(self, eng, name, g):
        k = self.k
        if name == "sp":
            eng.wait_ge(k.out_done, 16)
            eng.sem_clear(range(k.out_done.num, k.out_done.num + 1))
            eng.sem_inc(k.sem("out_free"), 1)
            eng.wait_ge(k.next_in, 16)
            eng.sem_clear(range(k.next_in.num, k.next_in.num + 1))
            eng.sem_inc(k.sem("next_here"), 1)
        elif name == "dve":
            eng.wait_ge(k.sem("out_free"), 1)
            k.own["dve"].step(k.nc.vector.tensor_copy(k.x_out[:, :, :], k.x[:, :, :]))
            eng.wait_ge(k.sem("next_here"), 1)
            k.nc.vector.tensor_copy(k.x[:, :, :], k.x_next[:, :, :])
        k.end(eng, name)
        if name == "sp":
            eng.dma_start(self.dst[:, bass.ds(g, 1)].rearrange("p o t d -> p (o t) d"), k.x_out[:, :, :])\
                .then_inc(k.out_done, 16)
            self.load(eng, g + 2)

    def finish(self, eng, name):
        k = self.k
        if name == "sp":
            for sem in (k.out_done, k.next_in):
                eng.wait_ge(sem, 16)
                eng.sem_clear(range(sem.num, sem.num + 1))
        k.end(eng, name)


class Arena:

    def __init__(self, kit):
        self.kit, self.at = kit, 0

    def __call__(self, *shape, rows=P):
        n = int(np.prod(shape))
        v = self.kit.arena[0:rows, self.at:self.at + n]
        self.at += n
        assert self.at <= ARENA, self.at
        if len(shape) == 2:
            v = v.rearrange("p (a b) -> p a b", a=shape[0])
        elif len(shape) == 3:
            v = v.rearrange("p (a b c) -> p a b c", a=shape[0], b=shape[1])
        elif len(shape) == 4:
            v = v.rearrange("p (a b c d) -> p a b c d", a=shape[0], b=shape[1], c=shape[2])
        return v


def over(v, *shape):
    while len(v.shape) < len(shape):
        v = v.unsqueeze(len(v.shape))
    return v.to_broadcast(list(shape))


class Constants:

    def __init__(self, kit):
        self.k = kit

    def vector(self, dve):
        k, nc = self.k, self.k.nc
        for i in range(2):
            nc.vector.tensor_copy(k.identb[:, i * P:(i + 1) * P], k.w("ident"))
            nc.vector.tensor_copy(k.maskb[:, i * P:(i + 1) * P], k.w("mask_neg"))
        nc.vector.tensor_copy(k.selb[:, :], k.w("head_rows"))

    def tensor(self, eng):
        pass

    scalar = gpsimd = sync = tensor


def log1p_coefficients(degree=4):
    x = np.cos((np.arange(degree + 1) + 0.5) * np.pi / (degree + 1))
    z = np.sqrt((x + 1) / 18)
    c = np.polynomial.polynomial.polyfit(z * z, 2 * np.arctanh(z) / z, degree)
    return [float(v) for v in c]


LOG1P = log1p_coefficients()


def softplus(kit, dst, x, e, t1, t2):
    nc, own = kit.nc, kit.own["dve"]
    own.step(nc.vector.tensor_scalar(t1, e, 2.0, None, ALU.add))
    own.step(nc.vector.reciprocal(t2, t1))
    own.step(nc.vector.tensor_tensor(e, e, t2, ALU.mult))
    own.step(nc.vector.tensor_tensor(t1, e, e, ALU.mult))
    own.step(nc.vector.tensor_scalar(t2, t1, LOG1P[-1], None, ALU.mult))
    for c in LOG1P[-2:0:-1]:
        own.step(nc.vector.scalar_tensor_tensor(t2, t2, c, t1, ALU.add, ALU.mult))
    own.step(nc.vector.scalar_tensor_tensor(t2, t2, LOG1P[0], e, ALU.add, ALU.mult))
    return nc.vector.scalar_tensor_tensor(dst, x, 0.0, t2, ALU.max, ALU.add)


class Norm:

    def __init__(self, kit, mem, x, eps, rms=False, tag=""):
        self.k, self.x, self.eps, self.rms, self.tag = kit, x, eps, rms, tag
        self.stats = mem(T, 6)
        self.mv = mem(T, 2)
        self.var = mem(T)
        self.msq = mem(T)
        self.rstd = mem(T)

    def vector(self, dve):
        k, nc, own = self.k, self.k.nc, self.k.own["dve"]
        for t in range(T):
            own.did(nc.vector.bn_stats(self.stats[:, t, :], self.x[:, t, :]))
        own.wait()
        for t in range(T):
            own.did(nc.vector.bn_aggr(self.mv[:, t, :], self.stats[:, t, :]))
        own.wait()
        if self.rms:
            own.step(nc.vector.tensor_tensor(self.msq, self.mv[:, :, 0], self.mv[:, :, 0], ALU.mult))
            own.step(nc.vector.tensor_tensor(self.msq, self.msq, self.mv[:, :, 1], ALU.add))
            last = nc.vector.tensor_scalar(self.var, self.msq, self.eps, None, ALU.add)
        else:
            last = nc.vector.tensor_scalar(self.var, self.mv[:, :, 1], self.eps, None, ALU.add)
        last.then_inc(k.sem("norm_var" + self.tag), 1)
        dve.wait_ge(k.sem("norm_rstd" + self.tag), 1)
        for t in range(T):
            if self.rms:
                ins = nc.vector.tensor_scalar(k.n[:, t, :], self.x[:, t, :], self.rstd[:, t:t + 1], None, ALU.mult)
            else:
                ins = nc.vector.tensor_scalar(k.n[:, t, :], self.x[:, t, :], self.mv[:, t, 0:1],
                                              self.rstd[:, t:t + 1], ALU.subtract, ALU.mult)
            ins.then_inc(k.sem("norm_n" + self.tag), 1)

    def gpsimd(self, pool):
        k, nc = self.k, self.k.nc
        pool.wait_ge(k.sem("norm_var" + self.tag), 1)
        nc.gpsimd.tensor_tensor(self.rstd, self.var, k.row("minus_half", 0, T), ALU.pow)\
            .then_inc(k.sem("norm_rstd" + self.tag), 1)

    WARM = 24

    def tensor(self, pe, bank):
        k, nc = self.k, self.k.nc
        for _ in range(self.WARM):
            nc.tensor.matmul(bank[:, 0:2 * P], k.identb[:, 0:P], k.identb[:, :], start=True, stop=True)
        for t in range(T):
            pe.wait_ge(k.sem("norm_n" + self.tag), t + 1)
            ins = nc.tensor.transpose(bank[:, t * P:(t + 1) * P], k.n[:, t, :], k.w("ident"))
        ins.then_inc(k.sem("norm_turned" + self.tag), 1)

    def scalar(self, act, bank):
        k, nc = self.k, self.k.nc
        act.wait_ge(k.sem("norm_turned" + self.tag), 1)
        nc.scalar.copy(k.nT[:, :], bank[:, :]).then_inc(k.sem("nT" + self.tag), 1)


class Mlp:

    def __init__(self, kit, mem, src, units, per, kind, func, first, down, second=None, bias1=None, bias2=None,
                 use=None, extra=None, tag=""):
        self.k, self.src, self.U, self.per, self.kind, self.func = kit, src, units, per, kind, func
        self.first, self.second, self.down = first, second, down
        self.bias1, self.bias2, self.use, self.extra, self.tag = bias1, bias2, use, extra, tag
        self.a = [mem(GT) for _ in range(2)]
        self.h = [mem(GT) for _ in range(2)]
        self.E = units // per

    def s(self, name):
        return self.k.sem(name + self.tag)

    def y(self, e):
        return self.k.bank[4 + e % 2]

    def tensor(self, pe, aside={}):
        k, nc = self.k, self.k.nc

        def up(u):
            if u >= 2:
                pe.wait_ge(self.s("h_ready"), u - 1)
            ins = nc.tensor.matmul(k.bank[u % 2][:, :], self.first(u), self.src[:, :], start=True, stop=True)
            if self.kind == "gated":
                ins = nc.tensor.matmul(k.bank[2 + u % 2][:, :], self.second(u), self.src[:, :], start=True, stop=True)
            ins.then_inc(self.s("up_ready"), 1)

        def down(u):
            e, i = divmod(u, self.per)
            pe.wait_ge(self.s("h_ready"), u + 1)
            if i == 0 and e >= 2:
                pe.wait_ge(self.s("y_used"), e - 1)
            last = i == self.per - 1
            for t in range(T):
                out = self.y(e)[:, t * D:(t + 1) * D]
                ins = nc.tensor.matmul(out, self.h[u % 2][:, t * P:(t + 1) * P], self.down(u),
                                       start=(i == 0 and t == 0), stop=last and not self.extra,
                                       skip_group_check=True)
                if last and self.extra:
                    ins = nc.tensor.matmul(out, self.extra[0], self.extra[1], start=False, stop=True,
                                           skip_group_check=True)
            ins.then_inc(self.s("down_done"), 1)

        up(0)
        for u in range(self.U):
            if u + 1 < self.U:
                up(u + 1)
            down(u)
            if u in aside:
                aside[u](pe)

    def scalar(self, act, aside={}):
        k, nc = self.k, self.k.nc
        for u in range(self.U):
            act.wait_ge(self.s("up_ready"), u + 1)
            kw = {"bias": self.bias1(u)} if self.bias1 else {}
            if self.kind == "plain":
                if u >= 2:
                    act.wait_ge(self.s("down_done"), u - 1)
                nc.scalar.activation(self.h[u % 2], k.bank[u % 2][:, :], self.func, **kw)\
                    .then_inc(self.s("h_ready"), 1)
            else:
                if u >= 2:
                    act.wait_ge(self.s("h_ready"), u - 1)
                nc.scalar.activation(self.a[u % 2], k.bank[u % 2][:, :], self.func, **kw)\
                    .then_inc(self.s("a_ready"), 1)
            if u in aside:
                aside[u](act)

    def vector(self, dve, aside={}):
        k, nc = self.k, self.k.nc
        for u in range(self.U):
            if self.kind != "plain":
                dve.wait_ge(self.s("a_ready"), u + 1)
                if u >= 2:
                    dve.wait_ge(self.s("down_done"), u - 1)
                if self.kind == "square":
                    ins = nc.vector.tensor_tensor(self.h[u % 2], self.a[u % 2], self.a[u % 2], ALU.mult)
                elif self.bias2:
                    ins = nc.vector.scalar_tensor_tensor(self.h[u % 2], k.bank[2 + u % 2][:, :], self.bias2(u),
                                                         self.a[u % 2], ALU.add, ALU.mult)
                else:
                    ins = nc.vector.tensor_tensor(self.h[u % 2], k.bank[2 + u % 2][:, :], self.a[u % 2], ALU.mult)
                ins.then_inc(self.s("h_ready"), 1)
            if u in aside:
                aside[u](dve)
            e, i = divmod(u, self.per)
            if i == 1 and e >= 1:
                self.take(dve, e - 1)
        self.take(dve, self.E - 1)

    def take(self, dve, e):
        dve.wait_ge(self.s("down_done"), self.per * (e + 1))
        self.use(e, self.y(e)).then_inc(self.s("y_used"), 1)


class Router:

    def __init__(self, kit, mem, srcT, prefix, top2, half):
        self.k, self.srcT, self.pre, self.top2, self.half = kit, srcT, prefix, top2, half
        self.E = 8
        self.z = mem(T, self.E)
        self.mx = mem(T)
        self.sum = mem(T)
        self.rec = mem(T)
        self.p = mem(T, self.E)
        self.probs = mem(T, self.E)
        self.m8 = mem(T, 8)
        self.i8 = mem(T * 8)
        self.i2 = mem(T, 2)
        self.m = [mem(T, self.E) for _ in range(3)]
        self.pT = mem(GT, rows=self.E)

    def tensor(self, pe):
        k, nc, E = self.k, self.k.nc, self.E
        lg = k.bank[6]
        for t in range(T):
            ins = nc.tensor.matmul(lg[:, t * E:(t + 1) * E], self.srcT[:, t * P:(t + 1) * P],
                                   k.w(self.pre + "router"), start=True, stop=True)
        ins.then_inc(k.sem("logits"), 1)

    def tensor_bias(self, pe):
        k, nc, E = self.k, self.k.nc, self.E
        tr, bi = k.bank[7], k.bank[6]
        pe.wait_ge(k.sem("probs"), 1)
        for t in range(T):
            ins = nc.tensor.transpose(tr[0:E, t * P:(t + 1) * P], self.probs[:, t, :], k.w("ident"))
        ins.then_inc(k.sem("probs_turned"), 1)
        pe.wait_ge(k.sem("probsT"), 1)
        for t in range(T):
            ins = nc.tensor.matmul(bi[:, t * D:(t + 1) * D], self.pT[:, t * P:(t + 1) * P],
                                   k.w(self.pre + "down_b"), start=True, stop=True)
        ins.then_inc(k.sem("down_bias"), 1)

    def scalar(self, act):
        k, nc = self.k, self.k.nc
        act.wait_ge(k.sem("logits_shifted"), 1)
        nc.scalar.activation(self.p, self.z, ACT.Exp).then_inc(k.sem("router_exp"), 1)

    def scalar_turn(self, act):
        k, nc = self.k, self.k.nc
        act.wait_ge(k.sem("probs_turned"), 1)
        nc.scalar.copy(self.pT, k.bank[7][0:self.E, :]).then_inc(k.sem("probsT"), 1)

    def vector(self, dve):
        k, nc, E, own = self.k, self.k.nc, self.E, self.k.own["dve"]
        lg = k.bank[6][:, 0:T * E].rearrange("p (t e) -> p t e", t=T)
        dve.wait_ge(k.sem("logits"), 1)
        if self.pre == "L3f_":
            own.step(nc.vector.tensor_tensor(self.z, lg, k.w("L3f_bg").unsqueeze(1).to_broadcast([P, T, E]), ALU.add))
            lg = self.z
        own.step(nc.vector.tensor_reduce(self.mx, lg, AX.X, ALU.max))
        nc.vector.tensor_tensor(self.z, lg, over(self.mx, P, T, E), ALU.subtract)\
            .then_inc(k.sem("logits_shifted"), 1)
        dve.wait_ge(k.sem("router_exp"), 1)
        own.step(nc.vector.tensor_reduce(self.sum, self.p, AX.X, ALU.add))
        own.step(nc.vector.reciprocal(self.rec, self.sum))
        if self.top2:
            own.step(nc.vector.tensor_tensor(self.p, self.p, over(self.rec, P, T, E), ALU.mult))
            for t in range(T):
                own.did(nc.vector.max(self.m8[:, t, :], self.p[:, t, :]))
            own.wait()
            i8 = self.i8.bitcast(U32).rearrange("p (t e) -> p t e", t=T)
            for t in range(T):
                own.did(nc.vector.max_index(i8[:, t, :], self.m8[:, t, :], self.p[:, t, :]))
            own.wait()

    def vector_rest(self, dve):
        k, nc, E, own = self.k, self.k.nc, self.E, self.k.own["dve"]
        if self.top2:
            i8 = self.i8.bitcast(U32).rearrange("p (t e) -> p t e", t=T)
            own.step(nc.vector.tensor_copy(self.i2, i8[:, :, 0:2]))
            iota = k.w("iota8").unsqueeze(1).to_broadcast([P, T, E])
            for j in range(2):
                own.did(nc.vector.tensor_tensor(self.m[j], iota, self.i2[:, :, j:j + 1].to_broadcast([P, T, E]),
                                                ALU.is_equal))
            own.wait()
            own.step(nc.vector.tensor_tensor(self.m[2], self.m[0], self.m[1], ALU.add))
            own.step(nc.vector.tensor_tensor(self.p, self.p, self.m[2], ALU.mult))
            own.step(nc.vector.tensor_reduce(self.sum, self.p, AX.X, ALU.add))
            own.step(nc.vector.tensor_scalar(self.sum, self.sum, 1e-9, None, ALU.add))
            own.step(nc.vector.reciprocal(self.rec, self.sum))
        own.step(nc.vector.tensor_scalar(self.rec, self.rec, self.half, None, ALU.mult))
        nc.vector.tensor_tensor(self.probs, self.p, over(self.rec, P, T, E), ALU.mult).then_inc(k.sem("probs"), 1)

    def vector_bias(self, dve):
        k, nc = self.k, self.k.nc
        dve.wait_ge(k.sem("down_bias"), 1)
        own = self.k.own["dve"]
        own.step(nc.vector.tensor_tensor(k.x[:, :, :], k.x[:, :, :],
                                         k.bank[6][:, :].rearrange("p (t d) -> p t d", t=T), ALU.add))

    def use(self, e, y):
        k, nc = self.k, self.k.nc
        if e:
            k.nc.vector.wait_ge(k.sem("y_used"), e)
        for t in range(T):
            ins = nc.vector.scalar_tensor_tensor(k.x[:, t, :], y[:, t * D:(t + 1) * D], self.probs[:, t, e:e + 1],
                                                 k.x[:, t, :], ALU.mult, ALU.add)
        return ins


class L1Ffn:

    def __init__(self, kit):
        self.k = kit
        mem = Arena(kit)
        self.norm = Norm(kit, mem, kit.x, 1e-5)
        self.router = Router(kit, mem, kit.nT, "L1f_", True, 0.5)
        self.mlp = Mlp(kit, mem, kit.nT, 16, 2, "gated", ACT.Silu,
                       first=lambda u: kit.row("L1f_gate", u * P, (u + 1) * P),
                       second=lambda u: kit.row("L1f_up", u * P, (u + 1) * P),
                       down=lambda u: kit.row("L1f_down", u * D, (u + 1) * D),
                       bias1=lambda u: kit.row("L1f_gate_b", u, u + 1),
                       bias2=lambda u: kit.row("L1f_up_b", u, u + 1), use=self.router.use)

    def tensor(self, pe):
        self.norm.tensor(pe, self.k.bank[7])
        pe.wait_ge(self.k.sem("nT"), 1)
        self.router.tensor(pe)
        self.mlp.tensor(pe, {1: self.router.tensor_bias})

    def scalar(self, act):
        self.norm.scalar(act, self.k.bank[7])
        self.router.scalar(act)
        self.mlp.scalar(act, {1: self.router.scalar_turn})

    def vector(self, dve):
        self.norm.vector(dve)
        self.router.vector(dve)
        self.mlp.vector(dve, {0: self.router.vector_rest, 2: self.router.vector_bias})

    def gpsimd(self, pool):
        self.norm.gpsimd(pool)

    def sync(self, sp):
        pass


class Binarise:

    def __init__(self, kit):
        self.k = kit
        mem = Arena(kit)
        self.sgn = mem(2, 4, D)
        self.alpha = mem(8)
        self.q = mem(2, 4, D)
        self.bw1T = kit.ctx.enter_context(kit.nc.sbuf_tensor("bw1T", [P, 512], F32))
        self.bw2T = kit.ctx.enter_context(kit.nc.sbuf_tensor("bw2T", [P, 512], F32))

    def scalar(self, act):
        k, nc = self.k, self.k.nc
        for i, name in enumerate(("L2f_w1", "L2f_w2")):
            nc.scalar.activation(self.sgn[:, i], k.w(name).rearrange("p (a b) -> p a b", a=4), ACT.Sign)\
                .then_inc(k.sem("sign"), 1)
        for i, dst in enumerate((self.bw1T, self.bw2T)):
            act.wait_ge(k.sem("bw_turned"), i + 1)
            nc.scalar.copy(dst[:, :], k.bank[i][:, :]).then_inc(k.sem("bw_kept"), 1)
        act.wait_ge(k.sem("bw_kept"), 2)

    def vector(self, dve):
        k, nc, own = self.k, self.k.nc, self.k.own["dve"]
        w1 = k.w("L2f_w1").rearrange("p (a b) -> p a b", a=4)
        w2 = k.w("L2f_w2").rearrange("p (a b) -> p a b", a=4)
        dve.wait_ge(k.sem("sign"), 2)
        own.did(nc.vector.tensor_reduce(self.alpha[:, 0:4], w1, AX.X, ALU.add, apply_absolute_value=True))
        own.did(nc.vector.tensor_reduce(self.alpha[:, 4:5], w2, AX.XY, ALU.add, apply_absolute_value=True))
        own.wait()
        own.did(nc.vector.tensor_scalar(self.alpha[:, 0:4], self.alpha[:, 0:4], 1.0 / 128, None, ALU.mult))
        own.did(nc.vector.tensor_scalar(self.alpha[:, 4:5], self.alpha[:, 4:5], 1.0 / 512, None, ALU.mult))
        own.wait()
        for i, w in enumerate((w1, w2)):
            a = over(self.alpha[:, 0:4], P, 4, D) if i == 0 else over(self.alpha[:, 4:5], P, 4, D)
            q = self.q[:, i]
            own.step(nc.vector.tensor_tensor(q, self.sgn[:, i], a, ALU.mult))
            own.step(nc.vector.tensor_tensor(q, q, w, ALU.subtract))
            nc.vector.tensor_tensor(q, q, w, ALU.add).then_inc(k.sem("binary"), 1)

    def tensor(self, pe):
        k, nc = self.k, self.k.nc
        for i in range(2):
            pe.wait_ge(k.sem("binary"), i + 1)
            for j in range(4):
                ins = nc.tensor.transpose(k.bank[i][:, j * P:(j + 1) * P], self.q[:, i, j, :], k.w("ident"))
            ins.then_inc(k.sem("bw_turned"), 1)

    def gpsimd(self, pool):
        pass

    def sync(self, sp):
        pass


class L2Ffn:

    def __init__(self, kit, binary):
        self.k = kit
        mem = Arena(kit)
        self.norm = Norm(kit, mem, kit.x, 1e-5)
        self.mlp = Mlp(kit, mem, kit.nT, 4, 4, "plain", ACT.Gelu,
                       first=lambda u: binary.bw1T[:, u * P:(u + 1) * P],
                       down=lambda u: binary.bw2T[:, u * P:(u + 1) * P],
                       bias1=lambda u: kit.row("L2f_b1", u, u + 1),
                       extra=(kit.row("ones", 0, P, hi=1), kit.w("L2f_b2")), use=self.use)

    def use(self, e, y):
        k = self.k
        return k.nc.vector.scalar_tensor_tensor(k.x[:, :, :], y[:, :].rearrange("p (t d) -> p t d", t=T), 0.5,
                                                k.x[:, :, :], ALU.mult, ALU.add)

    def tensor(self, pe):
        self.norm.tensor(pe, self.k.bank[7])
        pe.wait_ge(self.k.sem("nT"), 1)
        self.mlp.tensor(pe)

    def scalar(self, act):
        self.norm.scalar(act, self.k.bank[7])
        self.mlp.scalar(act)

    def vector(self, dve):
        self.norm.vector(dve)
        self.mlp.vector(dve)

    def gpsimd(self, pool):
        self.norm.gpsimd(pool)

    def sync(self, sp):
        pass


class L3Ffn:

    def __init__(self, kit):
        self.k = kit
        mem = Arena(kit)
        self.norm = Norm(kit, mem, kit.x, 1e-5)
        self.qT, self.kT, self.aT = mem(GT), mem(GT), mem(GT)
        self.v = mem(T, D)
        self.mx, self.sum, self.rec = mem(T), mem(T), mem(T)
        self.p = mem(NB, 2, SEQ)
        self.pT = mem(NB, 2, SEQ)
        self.router = Router(kit, mem, kit.nT, "L3f_", False, 0.5)
        self.mlp = Mlp(kit, mem, kit.nT, 32, 4, "plain", ACT.Relu,
                       first=lambda u: kit.row("L3f_tiles", 2 * u * P, (2 * u + 1) * P),
                       down=lambda u: kit.row("L3f_tiles", (2 * u + 1) * P, (2 * u + 2) * P),
                       bias1=lambda u: kit.row("L3f_b1", u, u + 1), use=self.router.use)

    SCALE = float(np.float32(1.0 / np.sqrt(128)))

    def tensor(self, pe):
        k, nc, b = self.k, self.k.nc, self.k.bank
        ones = k.row("ones", 0, P, hi=1)
        self.norm.tensor(pe, b[7])
        pe.wait_ge(k.sem("nT"), 1)
        nc.tensor.matmul(b[0][:, :], k.w("L3f_Wq"), k.nT[:, :], start=True, stop=True).then_inc(k.sem("q_made"), 1)
        nc.tensor.matmul(b[1][:, :], k.w("L3f_Wk"), k.nT[:, :], start=True, stop=True).then_inc(k.sem("k_made"), 1)
        for t in range(T):
            o = b[2][:, t * D:(t + 1) * D]
            nc.tensor.matmul(o, k.nT[:, t * P:(t + 1) * P], k.w("L3f_Wv"), start=True, stop=False)
            ins = nc.tensor.matmul(o, ones, k.w("L3f_bv"), start=False, stop=True)
        ins.then_inc(k.sem("v_made"), 1)
        pe.wait_ge(k.sem("qk_kept"), 2)
        for s in range(NB):
            for i in range(2):
                ins = nc.tensor.matmul(b[3 + s][:, i * SEQ:(i + 1) * SEQ],
                                       self.qT[:, s * SEQ + i * P:s * SEQ + (i + 1) * P],
                                       self.kT[:, s * SEQ:(s + 1) * SEQ], start=True, stop=True)
            ins.then_inc(k.sem("scores"), 1)
        for s in range(NB):
            pe.wait_ge(k.sem("p_normal"), s + 1)
            for j in range(2):
                for i in range(2):
                    ins = nc.tensor.transpose(b[5 + s][:, j * SEQ + i * P:j * SEQ + (i + 1) * P],
                                              self.p[:, s, i, j * P:(j + 1) * P], k.w("ident"))
            ins.then_inc(k.sem("p_turned"), 1)
        pe.wait_ge(k.sem("v_kept"), 1)
        for s in range(NB):
            pe.wait_ge(k.sem("pT"), s + 1)
            for j in range(2):
                ins = nc.tensor.matmul(b[0][:, s * SEQ:(s + 1) * SEQ], self.v[:, 2 * s + j, :], self.pT[:, s, j, :],
                                       start=(j == 0), stop=(j == 1))
        ins.then_inc(k.sem("a_made"), 1)
        pe.wait_ge(k.sem("aT"), 1)
        for t in range(T):
            o = b[1][:, t * D:(t + 1) * D]
            nc.tensor.matmul(o, self.aT[:, t * P:(t + 1) * P], k.w("L3f_Wo"), start=True, stop=False)
            ins = nc.tensor.matmul(o, ones, k.w("L3f_bo"), start=False, stop=True)
        ins.then_inc(k.sem("attn_out"), 1)
        pe.wait_ge(k.sem("x1"), 1)
        for t in range(T):
            ins = nc.tensor.transpose(b[7][:, t * P:(t + 1) * P], k.n[:, t, :], k.w("ident"))
        ins.then_inc(k.sem("x1_turned"), 1)
        pe.wait_ge(k.sem("x1T"), 1)
        self.router.tensor(pe)
        self.mlp.tensor(pe, {1: self.router.tensor_bias})

    def scalar(self, act):
        k, nc, b = self.k, self.k.nc, self.k.bank
        self.norm.scalar(act, b[7])
        act.wait_ge(k.sem("q_made"), 1)
        nc.scalar.activation(self.qT, b[0][:, :], ACT.Identity, bias=k.w("L3f_bq")).then_inc(k.sem("qk_kept"), 1)
        for s in range(NB):
            act.wait_ge(k.sem("neg_max"), s + 1)
            for i in range(2):
                c = 2 * s + i
                ins = nc.scalar.activation(self.p[:, s, i, :], b[3 + s][:, i * SEQ:(i + 1) * SEQ], ACT.Exp,
                                           bias=self.mx[:, c:c + 1], scale=self.SCALE,
                                           accum_out=self.sum[:, c:c + 1])
            ins.then_inc(k.sem("p_exp"), 1)
        for s in range(NB):
            act.wait_ge(k.sem("p_turned"), s + 1)
            nc.scalar.copy(self.pT[:, s, :, :], b[5 + s][:, :].rearrange("p (j q) -> p j q", j=2))\
                .then_inc(k.sem("pT"), 1)
        act.wait_ge(k.sem("a_made"), 1)
        nc.scalar.copy(self.aT, b[0][:, :]).then_inc(k.sem("aT"), 1)
        act.wait_ge(k.sem("x1_turned"), 1)
        nc.scalar.copy(k.nT[:, :], b[7][:, :]).then_inc(k.sem("x1T"), 1)
        self.router.scalar(act)
        self.mlp.scalar(act, {1: self.router.scalar_turn})

    def vector(self, dve):
        k, nc, b, own = self.k, self.k.nc, self.k.bank, self.k.own["dve"]
        self.norm.vector(dve)
        dve.wait_ge(k.sem("k_made"), 1)
        nc.vector.tensor_scalar(self.kT, b[1][:, :], k.w("L3f_bk"), None, ALU.add).then_inc(k.sem("qk_kept"), 1)
        dve.wait_ge(k.sem("v_made"), 1)
        nc.vector.tensor_copy(self.v, b[2][:, :].rearrange("p (t d) -> p t d", t=T)).then_inc(k.sem("v_kept"), 1)
        for s in range(NB):
            m = self.mx[:, 2 * s:2 * s + 2]
            dve.wait_ge(k.sem("scores"), s + 1)
            own.step(nc.vector.tensor_reduce(m, b[3 + s][:, :].rearrange("p (i q) -> p i q", i=2), AX.X, ALU.max))
            nc.vector.tensor_scalar(m, m, -self.SCALE, None, ALU.mult).then_inc(k.sem("neg_max"), 1)
        for s in range(NB):
            dve.wait_ge(k.sem("p_exp"), s + 1)
            own.step(nc.vector.reciprocal(self.rec[:, 2 * s:2 * s + 2], self.sum[:, 2 * s:2 * s + 2]))
            nc.vector.tensor_tensor(self.p[:, s], self.p[:, s], over(self.rec[:, 2 * s:2 * s + 2], P, 2, SEQ),
                                    ALU.mult).then_inc(k.sem("p_normal"), 1)
        dve.wait_ge(k.sem("attn_out"), 1)
        nc.vector.tensor_tensor(k.n[:, :, :], k.n[:, :, :], b[1][:, :].rearrange("p (t d) -> p t d", t=T), ALU.add)\
            .then_inc(k.sem("x1"), 1)
        dve.wait_ge(k.sem("x1"), 1)
        own.step(nc.vector.scalar_tensor_tensor(k.x[:, :, :], k.n[:, :, :], 0.5, k.x[:, :, :], ALU.mult, ALU.add))
        self.router.vector(dve)
        self.mlp.vector(dve, {0: self.router.vector_rest, 2: self.router.vector_bias})

    def gpsimd(self, pool):
        self.norm.gpsimd(pool)

    def sync(self, sp):
        pass


def l3ffn_weights(i, tiles, spread):
    f = {n: i["L3_ffn_" + n] for n in ("Wq", "bq", "Wk", "bk", "Wv", "bv", "Wo", "bo", "Wg", "bg", "W1", "b1", "W2", "b2")}
    return {
        "L3f_Wq": f["Wq"], "L3f_Wk": f["Wk"], "L3f_Wv": f["Wv"], "L3f_Wo": f["Wo"],
        "L3f_bq": f["bq"].reshape(P, 1), "L3f_bk": f["bk"].reshape(P, 1),
        "L3f_bv": f["bv"].reshape(1, D), "L3f_bo": f["bo"].reshape(1, D),
        "L3f_router": f["Wg"], "L3f_bg": spread(f["bg"]),
        "L3f_tiles": np.stack([f["W1"].transpose(1, 0, 2).reshape(P, -1, P),
                           f["W2"].reshape(-1, P, D).transpose(1, 0, 2)], 2).reshape(P, -1),
        "L3f_b1": f["b1"].reshape(-1, P).T,
        "L3f_down_b": f["b2"],
    }


MORE_WEIGHTS = [l3ffn_weights]


class PrepL1:

    def __init__(self, kit):
        self.k = kit

        def keep(name):
            return kit.ctx.enter_context(kit.nc.sbuf_tensor(name, [P, 16], F32))
        self.e, self.A, self.small, self.rest, self.den, self.inv = [
            keep("l1_" + n) for n in ("exp_alog", "A", "small", "rest", "den", "inv")]

    def scalar(self, act):
        self.k.nc.scalar.activation(self.e[:, :], self.k.w("L1a_A_log"), ACT.Exp).then_inc(self.k.sem("exp_alog"), 1)

    def vector(self, dve):
        nc, own = self.k.nc, self.k.own["dve"]
        dve.wait_ge(self.k.sem("exp_alog"), 1)
        own.step(nc.vector.tensor_scalar(self.A[:, :], self.e[:, :], -1.0, None, ALU.mult))
        own.step(nc.vector.tensor_scalar(self.small[:, :], self.A[:, :], -1e-5, None, ALU.is_gt))
        own.did(nc.vector.tensor_scalar(self.rest[:, :], self.small[:, :], -1.0, 1.0, ALU.mult, ALU.add))
        own.step(nc.vector.tensor_scalar(self.den[:, :], self.A[:, :], 1e-10, None, ALU.add))
        own.step(nc.vector.tensor_tensor(self.den[:, :], self.den[:, :], self.rest[:, :], ALU.mult))
        own.step(nc.vector.tensor_tensor(self.den[:, :], self.den[:, :], self.small[:, :], ALU.add))
        own.step(nc.vector.reciprocal(self.inv[:, :], self.den[:, :]))

    def tensor(self, pe):
        pass

    gpsimd = sync = tensor


class L1Attn:

    N = 16

    def __init__(self, kit, prep):
        self.k, self.prep = kit, prep
        mem = Arena(kit)
        self.norm = Norm(kit, mem, kit.x, 1e-5)
        self.pad = mem(NB, 3 + SEQ)
        self.dtu = mem(GT, rows=64)
        self.C = mem(GT, rows=16)
        self.part2 = mem(GT // 2, rows=16).bitcast(BF16)
        self.parts = mem(GT // 2).bitcast(BF16)
        self.xb, self.ab, self.e, self.lnw, self.w, self.q, self.dt = [mem(GT) for _ in range(7)]
        self.conv = [mem(NB, SEQ) for _ in range(2)]
        self.u, self.zs, self.dtxu, self.g = [mem(GT) for _ in range(4)]
        self.a = [mem(NB, SEQ + 1) for _ in range(3)]
        self.v = [mem(NB, SEQ + 1) for _ in range(3)]
        self.u_rest = [mem(GT) for _ in range(2)]
        self.u_small = [mem(GT) for _ in range(2)]
        self.h = [mem(NB, SEQ + 1) for _ in range(2)]
        self.hc = [mem(GT) for _ in range(2)]

    @staticmethod
    def two(v):
        return v.rearrange("p (b s) -> p b s", b=NB)

    def tensor(self, pe):
        k, nc, b = self.k, self.k.nc, self.k.bank
        self.norm.tensor(pe, b[7])
        pe.wait_ge(k.sem("nT"), 1)
        nc.tensor.matmul(b[1][0:64, :], k.w("L1a_Wdtu"), k.nT[:, :], start=True, stop=True).then_inc(k.sem("dtu_made"), 1)
        nc.tensor.matmul(b[2][0:16, :], k.w("L1a_WC"), k.nT[:, :], start=True, stop=True).then_inc(k.sem("C_made"), 1)
        nc.tensor.matmul(b[0][:, :], k.w("L1a_Wz"), k.nT[:, :], start=True, stop=True).then_inc(k.sem("z_made"), 1)
        pe.wait_ge(k.sem("dtu"), 1)
        nc.tensor.matmul(b[3][:, :], k.w("L1a_Wdt"), self.dtu, start=True, stop=True).then_inc(k.sem("dt_made"), 1)
        pe.wait_ge(k.sem("C_parts"), 3)
        for n in range(self.N + 1):
            if n < self.N:
                if n >= 2:
                    pe.wait_ge(k.sem("hc"), n - 1)
                nc.tensor.matmul(b[5 + n % 2][:, :], k.selb[:, n * P:(n + 1) * P], self.parts,
                                 start=True, stop=True).then_inc(k.sem("C_row"), 1)
            if n >= 1:
                pe.wait_ge(k.sem("hc"), n)
                nc.tensor.matmul(b[4][:, :], k.w("ident"), self.hc[(n - 1) % 2], start=(n == 1), stop=(n == self.N),
                                 skip_group_check=True).then_inc(k.sem("y_sum"), 1)
        pe.wait_ge(k.sem("gated"), 1)
        for t in range(T):
            ins = nc.tensor.matmul(b[0][:, t * D:(t + 1) * D], self.g[:, t * P:(t + 1) * P], k.w("L1a_Wout"),
                                   start=True, stop=True)
        ins.then_inc(k.sem("out_made"), 1)

    def scalar(self, act):
        k, nc, b = self.k, self.k.nc, self.k.bank
        self.norm.scalar(act, b[7])
        act.wait_ge(k.sem("dtu_made"), 1)
        nc.scalar.copy(self.dtu, b[1][0:64, :]).then_inc(k.sem("dtu"), 1)
        act.wait_ge(k.sem("z_made"), 1)
        nc.scalar.activation(self.zs, b[0][:, :], ACT.Silu).then_inc(k.sem("z_silu"), 1)
        act.wait_ge(k.sem("dt_x"), 1)
        nc.scalar.activation(self.ab, self.xb, ACT.Abs).then_inc(k.sem("dt_abs"), 1)
        act.wait_ge(k.sem("dt_abs"), 1)
        nc.scalar.activation(self.e, self.ab, ACT.Exp, scale=-1.0).then_inc(k.sem("dt_exp"), 1)
        act.wait_ge(k.sem("conv"), 4)
        nc.scalar.activation(self.two(self.u), self.conv[1], ACT.Silu).then_inc(k.sem("u"), 1)
        act.wait_ge(k.sem("dt"), 1)
        act.wait_ge(k.sem("pads"), 1)
        act.wait_ge(k.sem("dt_u"), 1)
        for n in range(self.N):
            if n >= 3:
                act.wait_ge(k.sem("scan"), n - 2)
            nc.scalar.activation(self.a[n % 3][:, :, 1:], self.two(self.dt), ACT.Exp,
                                 scale=self.prep.A[:, n:n + 1]).then_inc(k.sem("decay"), 1)
            if n >= 2:
                act.wait_ge(k.sem("drive"), n - 1)
            nc.scalar.activation(self.u_rest[n % 2], self.u, ACT.Copy, scale=self.prep.rest[:, n:n + 1])\
                .then_inc(k.sem("u_rest"), 1)
            if n >= 2:
                act.wait_ge(k.sem("drive_full"), n - 1)
            nc.scalar.activation(self.u_small[n % 2], self.dtxu, ACT.Copy, scale=self.prep.small[:, n:n + 1])\
                .then_inc(k.sem("u_small"), 1)

    def vector(self, dve):
        k, nc, b, own = self.k, self.k.nc, self.k.bank, self.k.own["dve"]
        nc.vector.memset(self.pad[:, :, 0:3], 0.0)
        for i in range(3):
            ins = nc.vector.memset(self.a[i][:, :, 0:1], 0.0)
        ins.then_inc(k.sem("pads"), 1)
        self.norm.vector(dve)
        dve.wait_ge(k.sem("C_made"), 1)
        own.step(nc.vector.tensor_copy(self.C, b[2][0:16, :]))
        dve.wait_ge(k.sem("parts_clear"), 1)
        nc.vector.tensor_copy(self.parts[0:16], self.C).then_inc(k.sem("C_parts"), 1)
        dve.wait_ge(k.sem("C_parts"), 1)
        own.step(nc.vector.tensor_tensor(self.C, self.C, self.parts[0:16], ALU.subtract))
        own.step(nc.vector.tensor_copy(self.part2, self.C))
        nc.vector.tensor_copy(self.parts[32:48], self.part2).then_inc(k.sem("C_parts"), 1)
        nc.vector.tensor_tensor(self.parts[64:80], self.C, self.part2, ALU.subtract).then_inc(k.sem("C_parts"), 1)
        dve.wait_ge(k.sem("dt_made"), 1)
        nc.vector.tensor_scalar(self.xb, b[3][:, :], k.w("L1a_b_dt"), None, ALU.add).then_inc(k.sem("dt_x"), 1)
        own.step(nc.vector.tensor_copy(self.pad[:, :, 3:], self.two(k.nT[:, :])))
        for j in range(4):
            src = self.pad[:, :, j:j + SEQ]
            w = k.row("L1a_conv", j, j + 1)
            dst = self.conv[j % 2]
            if j == 0:
                ins = nc.vector.tensor_scalar(dst, src, w, None, ALU.mult)
            else:
                dve.wait_ge(k.sem("conv"), j)
                ins = nc.vector.scalar_tensor_tensor(dst, src, w, self.conv[(j + 1) % 2], ALU.mult, ALU.add)
            ins.then_inc(k.sem("conv"), 1)
        dve.wait_ge(k.sem("dt_exp"), 1)
        softplus(k, self.dt, self.xb, self.e, self.w, self.q).then_inc(k.sem("dt"), 1)
        dve.wait_ge(k.sem("dt"), 1)
        dve.wait_ge(k.sem("u"), 1)
        nc.vector.tensor_tensor(self.dtxu, self.dt, self.u, ALU.mult).then_inc(k.sem("dt_u"), 1)

        def drive(n):
            dve.wait_ge(k.sem("decay"), n + 1)
            dve.wait_ge(k.sem("u_rest"), n + 1)
            if n >= 3:
                dve.wait_ge(k.sem("scan"), n - 2)
            nc.vector.scalar_tensor_tensor(self.v[n % 3][:, :, 1:], self.a[n % 3][:, :, 1:], -1.0,
                                           self.two(self.u_rest[n % 2]), ALU.add, ALU.mult)\
                .then_inc(k.sem("drive"), 1)

        drive(0)
        drive(1)
        for n in range(self.N):
            dve.wait_ge(k.sem("drive_full"), n + 1)
            if n >= 2:
                dve.wait_ge(k.sem("hc"), n - 1)
            nc.vector.tensor_tensor_scan(self.h[n % 2].rearrange("p b s -> p (b s)"),
                                         self.a[n % 3].rearrange("p b s -> p (b s)"),
                                         self.v[n % 3].rearrange("p b s -> p (b s)"), 0.0,
                                         ALU.mult, ALU.add).then_inc(k.sem("scan"), 1)
            if n + 2 < self.N:
                drive(n + 2)
            dve.wait_ge(k.sem("scan"), n + 1)
            dve.wait_ge(k.sem("C_row"), n + 1)
            if n >= 2:
                dve.wait_ge(k.sem("y_sum"), n - 1)
            nc.vector.scalar_tensor_tensor(self.two(self.hc[n % 2]), self.h[n % 2][:, :, 0:SEQ], self.prep.inv[:, n:n + 1],
                                           self.two(b[5 + n % 2][:, :]), ALU.mult, ALU.mult)\
                .then_inc(k.sem("hc"), 1)
        dve.wait_ge(k.sem("y_sum"), self.N)
        own.step(nc.vector.scalar_tensor_tensor(self.xb, self.u, k.w("L1a_D"), b[4][:, :], ALU.mult, ALU.add))
        dve.wait_ge(k.sem("z_silu"), 1)
        nc.vector.tensor_tensor(self.g, self.xb, self.zs, ALU.mult).then_inc(k.sem("gated"), 1)
        dve.wait_ge(k.sem("out_made"), 1)
        nc.vector.tensor_tensor(k.x[:, :, :], k.x[:, :, :], b[0][:, :].rearrange("p (t d) -> p t d", t=T), ALU.add)

    def gpsimd(self, pool):
        k, nc = self.k, self.k.nc
        nc.gpsimd.memset(self.parts, 0.0).then_inc(k.sem("parts_clear"), 1)
        self.norm.gpsimd(pool)
        for n in range(self.N):
            v = self.v[n % 3]
            pool.wait_ge(k.sem("drive"), n + 1)
            pool.wait_ge(k.sem("u_small"), n + 1)
            nc.gpsimd.tensor_tensor(v[:, :, 1:], v[:, :, 1:], self.two(self.u_small[n % 2]), ALU.add)\
                .then_inc(k.sem("drive_sum"), 1)
            pool.wait_ge(k.sem("drive_sum"), n + 1)
            nc.gpsimd.tensor_copy(v[:, :, 0:1], v[:, :, 1:2]).then_inc(k.sem("drive_full"), 1)

    def sync(self, sp):
        pass


def l1attn_weights(i, tiles, spread):
    wp = i["L1_attn_W_params"]
    return {
        "L1a_Wz": i["L1_attn_W_z"].T, "L1a_Wdtu": wp[0:64].T, "L1a_WC": wp[80:96].T,
        "L1a_Wdt": i["L1_attn_W_dt"].T, "L1a_b_dt": i["L1_attn_b_dt"].reshape(P, 1),
        "L1a_conv": i["L1_attn_conv_w"].reshape(P, 4), "L1a_A_log": i["L1_attn_A_log"],
        "L1a_D": i["L1_attn_D"].reshape(P, 1), "L1a_Wout": i["L1_attn_W_out"].T,
    }


MORE_WEIGHTS += [l1attn_weights]


N_HEADS = 16


class Heads:

    AHEAD = 3

    def __init__(self, kit, mem, kvh, prefix, normed, deliver):
        self.k, self.kvh, self.pre, self.normed, self.deliver = kit, kvh, prefix, normed, deliver
        self.nqk = N_HEADS + kvh
        self.wide = (N_HEADS + 2 * kvh) * 8
        qkv_at = mem.at
        self.qkv = mem(T, self.wide)
        self.qk = self.qkv[:, :, 0:self.nqk * 8].rearrange("p t (h c) -> p t h c", c=8)
        if normed:
            self.sq = mem(T, self.nqk, 8)
            self.ms = mem(T, self.nqk)
            self.rs = mem(T, self.nqk)
        r_at = mem.at
        self.r = mem(2, self.nqk, 8)
        self.tmp = [mem(2, self.nqk, 4) for _ in range(4)]

        def half(*shape):
            n = int(np.prod(shape))
            v = mem(n // 2).bitcast(BF16)
            letters = "abcd"[:len(shape)]
            return v.rearrange("p (%s) -> p %s" % (" ".join(letters), " ".join(letters)),
                               **dict(zip(letters[:-1], shape)))
        self.part = [[half(2, self.nqk, 8) for _ in range(3)] for _ in range(NB)]
        stack_at = mem.at
        self.stack = half(T, self.nqk, 64)
        self.qT = half(NB, 8, SEQ)
        self.kT = half(NB, kvh // 2, SEQ)
        self.vaug = mem(T, kvh, 32)
        self.top = mem(NB, N_HEADS, 3)
        self.neg = mem(NB, 2, N_HEADS)
        self.neg_part = [half(2, 8, N_HEADS) for _ in range(NB)]
        self.negT = half(NB, 3 * P)
        self.pT = [mem(3 * P) for _ in range(3)]
        self.mixed = kit.arena[:, stack_at:stack_at + NB * 4 * SEQ].rearrange("p (s g q) -> p s g q", s=NB, g=4)
        self.rden = mem(NB, 2, N_HEADS)
        self.ctx = kit.arena[:, r_at:r_at + T * D].rearrange("p (t d) -> p t d", t=T)
        self.ctxT = kit.arena[:, qkv_at:qkv_at + GT]
        self.groups = 4 + kvh // 4
        self.n = NB * N_HEADS

    def a_item(self, n):
        return n if n < N_HEADS + self.AHEAD else n + 1

    def m_item(self, s):
        return N_HEADS + self.AHEAD if s == 0 else self.n + 1

    def b_bank(self, i):
        return self.k.bank[3 + i % 3]

    def tensor(self, pe):
        k, nc, b = self.k, self.k.nc, self.k.bank
        kw = dict(skip_group_check=True)
        for t in range(T):
            nc.tensor.matmul(b[t][:, 0:self.wide], k.nT[:, t * P:(t + 1) * P], k.w(self.pre + "Wqkv"),
                             start=True, stop=True).then_inc(k.sem("qkv_made"), 1)

        def turn(s, g):
            j = s * self.groups + g
            if g == 0:
                pe.wait_ge(k.sem("q_stack"), 6 * (s + 1))
                pe.wait_ge(k.sem("k1_stack"), 2 * (s + 1))
                pe.wait_ge(k.sem("k23_stack"), 4 * (s + 1))
            if j >= 3:
                pe.wait_ge(k.sem("turned_kept"), j - 2)
            elif j < T - 3:
                pe.wait_ge(k.sem("qkv"), T)
            for pair in range(2):
                for i in range(2):
                    at = pair * SEQ + i * P
                    ins = nc.tensor.matmul(self.b_bank(j)[:, at:at + P],
                                           self.stack[:, 2 * s + i, 4 * g + 2 * pair:4 * g + 2 * pair + 2, :]
                                           .rearrange("p h c -> p (h c)"), k.identb[:, 0:P], start=True, stop=True)
            ins.then_inc(k.sem("turned"), 1)

        def head(n):
            s, h = divmod(n, N_HEADS)
            kh = h if self.kvh == N_HEADS else h % 4
            rows = slice(64 * (h % 2), 64 * (h % 2) + 64)
            return s, h, kh, self.qT[rows, s, h // 2, :], self.kT[rows, s, kh // 2, :]

        def item(m):
            if m >= 3:
                pe.wait_ge(k.sem("a_read"), m - 2)
            return b[m % 3]

        def pass_a(n):
            s, h, kh, q, kk = head(n)
            if h == 0:
                pe.wait_ge(k.sem("turned_kept"), (s + 1) * self.groups)
            o = item(self.a_item(n))
            nc.tensor.matmul(o[:, 0:SEQ], q[:, P:SEQ], kk, start=True, stop=False, **kw)
            nc.tensor.matmul(o[:, SEQ:SEQ + P], q[:, 0:P], kk[:, 0:P], start=False, stop=False, **kw)
            nc.tensor.matmul(o[:, P:3 * P], k.identb[:, 0:P], k.maskb[:, :], start=False, stop=True, **kw)\
                .then_inc(k.sem("a_made"), 1)

        def turn_maxima(s):
            pe.wait_ge(k.sem("neg_parts"), 3 * (s + 1))
            o = item(self.m_item(s))
            for j, i in enumerate((0, 1, 0)):
                ins = nc.tensor.matmul(o[:, j * P:(j + 1) * P],
                                       self.neg_part[s][:, i, :, :].rearrange("p j h -> p (j h)"),
                                       k.identb[:, 0:P], start=True, stop=True)
            ins.then_inc(k.sem("a_made"), 1)

        def pass_b(n):
            s, h, kh, q, kk = head(n)
            if h == 0:
                pe.wait_ge(k.sem("a_read"), self.m_item(s) + 1)
            if n >= 3:
                pe.wait_ge(k.sem("p"), n - 2)
            o = self.b_bank(n)
            nc.tensor.matmul(o[:, P:3 * P], kk[:, 0:P], q, start=True, stop=False, **kw)
            nc.tensor.matmul(o[:, 0:P], kk[:, P:SEQ], q[:, P:SEQ], start=False, stop=False, **kw)
            nc.tensor.matmul(o[:, 0:2 * P], k.maskb[:, 0:P], k.identb[:, :], start=False, stop=False, **kw)
            nc.tensor.matmul(o[:, 0:3 * P], k.selb[:, h * P:(h + 1) * P], self.negT[:, s, :],
                             start=False, stop=True, **kw).then_inc(k.sem("b_made"), 1)

        def mix(n):
            s, h, kh, _, _ = head(n)
            g, slot = divmod(h, 4)
            if n == 0:
                pe.wait_ge(k.sem("v_kept"), 3)
            if s == 1 and h % 8 == 0:
                pe.wait_ge(k.sem("mix_kept"), 1 + h // 8)
            pe.wait_ge(k.sem("p"), n + 1)
            o, p, at = b[6 + g // 2][32 * slot:32 * slot + 32, :], self.pT[n % 3], (g % 2) * SEQ
            nc.tensor.matmul(o[:, at:at + SEQ], self.vaug[:, 2 * s, kh, :], p[:, P:3 * P],
                             start=True, stop=False, tile_position=(0, 32 * slot), **kw)
            nc.tensor.matmul(o[:, at + P:at + SEQ], self.vaug[:, 2 * s + 1, kh, :], p[:, 0:P],
                             start=False, stop=True, tile_position=(0, 32 * slot), **kw).then_inc(k.sem("mixed"), 1)

        def turn_back(s):
            pe.wait_ge(k.sem("mix_kept"), 2 * s + 2)
            pe.wait_ge(k.sem("a_read"), self.m_item(1) + 1)
            if s == 1:
                pe.wait_ge(k.sem("ctx"), 2)
            for i in range(2):
                for g in range(4):
                    ins = nc.tensor.transpose(b[i][:, g * P:(g + 1) * P], self.mixed[:, s, g, i * P:(i + 1) * P],
                                              k.w("ident"))
                ins.then_inc(k.sem("turned_back"), 1)

        for g in range(self.groups):
            turn(0, g)
        for n in range(N_HEADS):
            pass_a(n)
            if n % 2 == 1 and n // 2 < self.groups:
                turn(1, n // 2)
        for n in range(self.AHEAD):
            pass_a(N_HEADS + n)
        turn_maxima(0)
        for n in range(self.n):
            ahead = N_HEADS + self.AHEAD + n
            if ahead < self.n:
                pass_a(ahead)
            if n == N_HEADS - 2:
                turn_maxima(1)
            pass_b(n)
            if n >= 2:
                mix(n - 2)
            if n == N_HEADS + 6:
                turn_back(0)
        mix(self.n - 2)
        mix(self.n - 1)
        turn_back(1)
        for t in range(T):
            pe.wait_ge(k.sem("ctx"), t + 1)
            ins = nc.tensor.transpose(b[2][:, t * P:(t + 1) * P], self.ctx[:, t, :], k.w("ident"))
        ins.then_inc(k.sem("ctx_turned"), 1)
        pe.wait_ge(k.sem("ctxT"), 1)
        for t in range(T):
            ins = nc.tensor.matmul(b[3][:, t * D:(t + 1) * D], self.ctxT[:, t * P:(t + 1) * P],
                                   k.w(self.pre + "Wo"), start=True, stop=True)
        ins.then_inc(k.sem("attn_out"), 1)

    def scalar(self, act):
        k, nc, b = self.k, self.k.nc, self.k.bank
        nq, nk = N_HEADS * 8, self.nqk * 8
        for t in range(T):
            act.wait_ge(k.sem("qkv_made"), t + 1)
            if self.normed:
                nc.scalar.copy(self.qkv[:, t, :], b[t][:, 0:self.wide]).then_inc(k.sem("qkv"), 1)
            else:
                nc.scalar.copy(self.qkv[:, t, 0:nq], b[t][:, 0:nq])
                nc.scalar.mul(self.qkv[:, t, nq:nk], b[t][:, nq:nk], HEAD_SCALE)
                nc.scalar.copy(self.qkv[:, t, nk:], b[t][:, nk:self.wide]).then_inc(k.sem("qkv"), 1)
            if self.normed:
                act.wait_ge(k.sem("qkv"), t + 1)
                nc.scalar.activation(self.sq[:, t], self.qk[:, t], ACT.Square).then_inc(k.sem("qk_squared"), 1)
        if self.normed:
            act.wait_ge(k.sem("qk_rms"), 1)
            nc.scalar.activation(self.rs, self.ms, ACT.Sqrt).then_inc(k.sem("qk_rs"), 1)
        for s in range(NB):
            for part, (a, e) in enumerate(((0, 3), (3, 6), (6, 8))):
                act.wait_ge(k.sem("parts"), 3 * s + part + 1)
                for i in range(2):
                    nc.scalar.copy(self.stack[:, 2 * s + i, 0:N_HEADS, :]
                                   .rearrange("p h (s c) -> p h s c", c=8)[:, :, a:e, :],
                                   self.part[s][part][:, i, 0:N_HEADS, :].unsqueeze(2)
                                   .to_broadcast([P, N_HEADS, e - a, 8])).then_inc(k.sem("q_stack"), 1)
            for g in range(self.groups):
                act.wait_ge(k.sem("turned"), s * self.groups + g + 1)
                dst = self.qT[:, s, 2 * g:2 * g + 2, :] if g < 4 else self.kT[:, s, 2 * g - 8:2 * g - 6, :]
                nc.scalar.copy(dst.rearrange("p a b -> p (a b)"), self.b_bank(s * self.groups + g)[:, :])\
                    .then_inc(k.sem("turned_kept"), 1)
        def keep_mix(j):
            act.wait_ge(k.sem("mixed"), 8 * (j + 1))
            nc.scalar.copy(self.mixed[:, j // 2, 2 * (j % 2):2 * (j % 2) + 2, :].rearrange("p g q -> p (g q)"),
                           b[6 + j % 2][:, :]).then_inc(k.sem("mix_kept"), 1)

        for n in range(self.n):
            if n >= 11 and n % 8 == 3:
                keep_mix(n // 8 - 1)
            act.wait_ge(k.sem("b_made"), n + 1)
            if n >= 3:
                act.wait_ge(k.sem("mixed"), n - 2)
            nc.scalar.activation(self.pT[n % 3], self.b_bank(n)[:, 0:3 * P], ACT.Exp).then_inc(k.sem("p"), 1)
        keep_mix(3)
        act.wait_ge(k.sem("ctx_turned"), 1)
        nc.scalar.copy(self.ctxT, b[2][:, :]).then_inc(k.sem("ctxT"), 1)

    def rotate(self, dve, s):
        k, nc, own = self.k, self.k.nc, self.k.own["dve"]
        n4, tiles = self.nqk, slice(2 * s, 2 * s + 2)
        qk = self.qk[:, tiles]
        dve.wait_ge(k.sem("qkv"), 2 * s + 2)
        if self.normed:
            if s == 0:
                dve.wait_ge(k.sem("qk_squared"), T)
                own.step(nc.vector.tensor_reduce(self.ms, self.sq, AX.X, ALU.add))
                own.step(nc.vector.tensor_scalar(self.ms, self.ms, 0.125, float(np.finfo(np.float32).eps),
                                                 ALU.mult, ALU.add))
                nc.vector.reciprocal(self.ms, self.ms).then_inc(k.sem("qk_rms"), 1)
                dve.wait_ge(k.sem("qk_rs"), 1)
                own.step(nc.vector.tensor_tensor(self.rs, self.rs, k.w(self.pre + "qk_gain").unsqueeze(1)
                                                 .to_broadcast([P, T, n4]), ALU.mult))
            own.step(nc.vector.tensor_tensor(qk, qk, over(self.rs[:, tiles], P, 2, n4, 8), ALU.mult))
            x1, x2 = qk[:, :, :, 0:4], qk[:, :, :, 4:8]
        else:
            x1, x2 = qk[:, :, :, 0:8:2], qk[:, :, :, 1:8:2]
        cos, sin = [k.w(n).rearrange("p (t c) -> p t c", t=T)[:, tiles].unsqueeze(2).to_broadcast([P, 2, n4, 4])
                    for n in ("rope_cos", "rope_sin")]
        A, B, C, E = self.tmp
        own.did(nc.vector.tensor_tensor(A, x1, cos, ALU.mult))
        own.did(nc.vector.tensor_tensor(B, x2, sin, ALU.mult))
        own.did(nc.vector.tensor_tensor(C, x1, sin, ALU.mult))
        own.step(nc.vector.tensor_tensor(E, x2, cos, ALU.mult))
        lo, hi = self.r[:, :, :, 0:4], self.r[:, :, :, 4:8]
        if self.normed:
            own.did(nc.vector.tensor_tensor(lo, A, B, ALU.add))
            own.step(nc.vector.tensor_tensor(hi, E, C, ALU.subtract))
        else:
            own.did(nc.vector.tensor_tensor(lo, A, B, ALU.subtract))
            own.step(nc.vector.tensor_tensor(hi, C, E, ALU.add))
        flat = lambda v: v.rearrange("p t h c -> p (t h c)")
        r, parts, count = flat(self.r), [flat(v) for v in self.part[s]], 3 * s
        nc.vector.tensor_copy(parts[0], r).then_inc(k.sem("parts"), 1)
        dve.wait_ge(k.sem("parts"), count + 1)
        own.step(nc.vector.tensor_tensor(r, r, parts[0], ALU.subtract))
        nc.vector.tensor_copy(parts[1], r).then_inc(k.sem("parts"), 1)
        dve.wait_ge(k.sem("parts"), count + 2)
        nc.vector.tensor_tensor(parts[2], r, parts[1], ALU.subtract).then_inc(k.sem("parts"), 1)
        dve.wait_ge(k.sem("parts"), count + 3)
        for part, n in ((1, 3), (2, 2)):
            for i in range(2):
                nc.vector.tensor_copy(*self.key_blocks(s, part, n, i)).then_inc(k.sem("k23_stack"), 1)

    def key_blocks(self, s, part, n, i):
        return (self.stack[:, 2 * s + i, N_HEADS:, :].rearrange("p h (s c) -> p h s c", c=8)[:, :, part:8:3, :],
                self.part[s][part][:, i, N_HEADS:, :].unsqueeze(2).to_broadcast([P, self.kvh, n, 8]))

    def split_maxima(self, dve, s):
        k, nc, own = self.k, self.k.nc, self.k.own["dve"]
        dve.wait_ge(k.sem("a_read"), self.a_item(N_HEADS * (s + 1) - 1) + 1)
        top, neg, part = self.top[:, s], self.neg[:, s], self.neg_part[s]
        own.did(nc.vector.tensor_tensor(neg[:, 0], top[:, :, 0], top[:, :, 1], ALU.min))
        own.step(nc.vector.tensor_copy(neg[:, 1], top[:, :, 2]))
        dve.wait_ge(k.sem("neg_clear"), s + 1)
        for j in range(3):
            nc.vector.tensor_copy(part[:, :, 2 * j, :], neg).then_inc(k.sem("neg_parts"), 1)
            if j < 2:
                dve.wait_ge(k.sem("neg_parts"), 3 * s + j + 1)
                own.step(nc.vector.tensor_tensor(neg, neg, part[:, :, 2 * j, :], ALU.subtract))

    def vector(self, dve):
        k, nc, b, own = self.k, self.k.nc, self.k.bank, self.k.own["dve"]
        for s in range(NB):
            self.rotate(dve, s)

        def maxima(n):
            s, h = divmod(n, N_HEADS)
            m = self.a_item(n)
            dve.wait_ge(k.sem("a_made"), m + 1)
            nc.vector.tensor_reduce(self.top[:, s, h], b[m % 3][:, 0:3 * P].rearrange("p (j q) -> p j q", j=3),
                                    AX.X, ALU.max, negate=True).then_inc(k.sem("a_read"), 1)

        def keep_maxima(s):
            m = self.m_item(s)
            dve.wait_ge(k.sem("a_made"), m + 1)
            nc.vector.tensor_copy(self.negT[:, s, :], b[m % 3][:, 0:3 * P]).then_inc(k.sem("a_read"), 1)

        for n in range(N_HEADS):
            maxima(n)
        self.split_maxima(dve, 0)
        for n in range(N_HEADS, N_HEADS + self.AHEAD):
            maxima(n)
        keep_maxima(0)
        for n in range(N_HEADS + self.AHEAD, self.n):
            maxima(n)
        self.split_maxima(dve, 1)
        keep_maxima(1)
        for s in range(NB):
            for i in range(2):
                dve.wait_ge(k.sem("turned_back"), 2 * s + i + 1)
                o = b[i][:, :].rearrange("p (h c) -> p h c", c=32)
                own.step(nc.vector.reciprocal(self.rden[:, s, i], o[:, :, 8]))
                nc.vector.tensor_tensor(self.ctx[:, 2 * s + i, :].rearrange("p (h c) -> p h c", c=8), o[:, :, 0:8],
                                        over(self.rden[:, s, i], P, N_HEADS, 8), ALU.mult).then_inc(k.sem("ctx"), 1)
        dve.wait_ge(k.sem("attn_out"), 1)
        self.deliver(b[3][:, :].rearrange("p (t d) -> p t d", t=T))

    def gpsimd(self, pool):
        k, nc = self.k, self.k.nc
        for s in range(NB):
            nc.gpsimd.memset(self.neg_part[s], 0.0).then_inc(k.sem("neg_clear"), 1)
        nc.gpsimd.memset(self.vaug[:, :, :, 9:], 0.0).then_inc(k.sem("v_kept"), 1)
        nc.gpsimd.memset(self.vaug[:, :, :, 8:9], 1.0).then_inc(k.sem("v_kept"), 1)
        for s in range(NB):
            pool.wait_ge(k.sem("parts"), 3 * s + 1)
            for i in range(2):
                nc.gpsimd.tensor_copy(*self.key_blocks(s, 0, 3, i)).then_inc(k.sem("k1_stack"), 1)
        pool.wait_ge(k.sem("qkv"), T)
        nc.gpsimd.tensor_copy(self.vaug[:, :, :, 0:8],
                              self.qkv[:, :, self.nqk * 8:].rearrange("p t (h c) -> p t h c", c=8))\
            .then_inc(k.sem("v_kept"), 1)


HEAD_SCALE = float(np.float32(8 ** -0.5))


class L0Attn:

    def __init__(self, kit):
        self.k = kit
        mem = Arena(kit)
        self.norm = Norm(kit, mem, kit.x, 1e-5)
        self.heads = Heads(kit, mem, 16, "L0a_", False, self.deliver)

    def deliver(self, y):
        k = self.k
        k.nc.vector.tensor_tensor(k.x[:, :, :], k.x[:, :, :], y, ALU.add)

    def tensor(self, pe):
        self.norm.tensor(pe, self.k.bank[7])
        pe.wait_ge(self.k.sem("nT"), 1)
        self.heads.tensor(pe)

    def scalar(self, act):
        self.norm.scalar(act, self.k.bank[7])
        self.heads.scalar(act)

    def vector(self, dve):
        self.norm.vector(dve)
        self.heads.vector(dve)

    def gpsimd(self, pool):
        self.norm.gpsimd(pool)
        self.heads.gpsimd(pool)

    def sync(self, sp):
        pass

    def run(self, eng, name, method, src, dst, *_):
        stream = Stream(self.k, src, dst)
        stream.begin(eng, name)
        with eng.Fori(0, GROUPS) as g:
            method(self)(eng)
            self.k.end(eng, name)
            stream.swap(eng, name, g)
        stream.finish(eng, name)


PLACED = [4 * (p % 4) + p // 4 for p in range(16)]


def heads_weights(i, tiles, spread):
    def heads(w):
        return w.reshape(w.shape[0], 16, 8)[:, PLACED].reshape(w.shape[0], P)

    freq = (1.0 / np.float32(10000.0) ** (np.arange(0, 8, 2, dtype=np.float32) / np.float32(8))).astype(np.float32)
    angle = (np.arange(SEQ, dtype=np.float32)[:, None] * freq[None, :]).astype(np.float32)

    def table(a):
        a = a.reshape(2, P, 4)[[0, 1, 0, 1]]
        return a.transpose(1, 0, 2).reshape(P, T * 4)

    wo3 = i["L3_attn_o_w"].reshape(16, 8, D)[PLACED].reshape(P, D)
    wo0 = i["L0_attn_Wo"].T.reshape(16, 8, D)[PLACED].reshape(P, D)
    return {
        "L0a_Wqkv": np.concatenate([heads(i["L0_attn_Wq"].T), heads(i["L0_attn_Wk"].T), heads(i["L0_attn_Wv"].T)], 1),
        "L0a_Wo": wo0,
        "L3a_Wqkv": np.concatenate([heads(i["L3_attn_q_w"]), i["L3_attn_k_w"], i["L3_attn_v_w"]], 1),
        "L3a_Wo": wo3,
        "L3a_qk_gain": spread(np.concatenate([i["L3_attn_q_gain"][PLACED], np.full(4, HEAD_SCALE, np.float32)])),
        "rope_cos": table(np.cos(angle)), "rope_sin": table(np.sin(angle)),
        "head_rows": np.tile(np.concatenate([np.repeat(np.eye(N_HEADS, dtype=np.float32), P, 1),
                                             np.zeros((16, N_HEADS * P), np.float32)], 0), (4, 1))
        * (np.arange(P)[:, None] < 96).astype(np.float32),
        "mask_neg": np.triu(np.full((P, P), -1e30, np.float32), 1),
    }


MORE_WEIGHTS += [heads_weights]


NE = 16
CAP = TOKENS * 2 // NE
NT = TOKENS // P
NEXT = D + NE
BATCH = 8
WE = 4 * D * 2 + 4 * D


class RouteShared:

    def __init__(self, kit, keep):
        self.k, self.sc = kit, keep
        mem = Arena(kit)
        self.norm = Norm(kit, mem, kit.x, 1e-5)
        self.z, self.p = mem(T, NE), mem(T, NE)
        self.mx, self.sum, self.rec = mem(T), mem(T), mem(T)
        self.rows = mem(T, NEXT)
        self.mlp = Mlp(kit, mem, kit.nT, 2, 2, "gated", ACT.Gelu,
                       first=lambda u: kit.row("L0f_Sg", u * P, (u + 1) * P),
                       second=lambda u: kit.row("L0f_Su", u * P, (u + 1) * P),
                       down=lambda u: kit.row("L0f_Sd", u * P, (u + 1) * P), use=self.use)

    def use(self, e, y):
        k = self.k
        return k.nc.vector.scalar_tensor_tensor(k.x[:, :, :], y[:, :].rearrange("p (t d) -> p t d", t=T), 0.5,
                                                k.x[:, :, :], ALU.mult, ALU.add)

    def tensor(self, pe, g):
        k, nc = self.k, self.k.nc
        self.norm.tensor(pe, k.bank[7])
        pe.wait_ge(k.sem("nT"), 1)
        for t in range(T):
            ins = nc.tensor.matmul(k.bank[6][:, t * NE:(t + 1) * NE], k.nT[:, t * P:(t + 1) * P], k.w("L0f_gate"),
                                   start=True, stop=True)
        ins.then_inc(k.sem("logits"), 1)
        self.mlp.tensor(pe)

    def scalar(self, act, g):
        k, nc = self.k, self.k.nc
        self.norm.scalar(act, k.bank[7])
        act.wait_ge(k.sem("logits_shifted"), 1)
        nc.scalar.activation(self.p, self.z, ACT.Exp).then_inc(k.sem("router_exp"), 1)
        act.wait_ge(k.sem("norm_n"), T)
        nc.scalar.copy(self.rows[:, :, 0:D], k.n[:, :, :]).then_inc(k.sem("row_n"), 1)
        self.mlp.scalar(act)

    def vector(self, dve, g):
        k, nc, own = self.k, self.k.nc, self.k.own["dve"]
        self.norm.vector(dve)
        lg = k.bank[6][:, 0:T * NE].rearrange("p (t e) -> p t e", t=T)
        dve.wait_ge(k.sem("logits"), 1)
        own.step(nc.vector.tensor_reduce(self.mx, lg, AX.X, ALU.max))
        nc.vector.tensor_tensor(self.z, lg, over(self.mx, P, T, NE), ALU.subtract)\
            .then_inc(k.sem("logits_shifted"), 1)
        dve.wait_ge(k.sem("router_exp"), 1)
        own.step(nc.vector.tensor_reduce(self.sum, self.p, AX.X, ALU.add))
        own.step(nc.vector.reciprocal(self.rec, self.sum))
        nc.vector.tensor_tensor(self.rows[:, :, D:], self.p, over(self.rec, P, T, NE), ALU.mult)\
            .then_inc(k.sem("row_scores"), 1)
        dve.wait_ge(k.sem("row_scores"), 1)
        nc.vector.tensor_copy(self.sc[:, bass.ds(g, 1)].rearrange("p o t e -> p (o t) e"), self.rows[:, :, D:])
        self.mlp.vector(dve)

    def gpsimd(self, pool, g):
        self.norm.gpsimd(pool)

    def sync(self, sp, g, n_ext):
        k = self.k
        sp.wait_ge(k.sem("row_n"), 1)
        sp.wait_ge(k.sem("row_scores"), 1)
        v = n_ext.rearrange("(g t p) d -> p g t d", g=GROUPS, p=P)
        sp.dma_start(v[:, bass.ds(g, 1)].rearrange("p o t d -> p (o t) d"), self.rows).then_inc(k.sem("rows_out"), 16)
        sp.wait_ge(k.sem("rows_out"), 16)


class Choose:

    def __init__(self, kit, keep_scores, keep_place):
        self.k, self.sc4, self.place = kit, keep_scores, keep_place
        mem = Arena(kit)
        self.sc = keep_scores.rearrange("p g t e -> p (g t) e")
        self.low = mem(NE)
        self.cand, self.hit, self.bits = [mem(3, NE) for _ in range(3)]
        self.ge = mem(3, NT, NE)
        self.cnt = mem(3, NE)
        self.gt, self.fill, self.mask = [mem(NT, NE) for _ in range(3)]
        self.need = mem(NE)
        half = mem(NT * NE // 2)
        self.flag = half.bitcast(BF16).rearrange("p (t e) -> p t e", t=NT)
        self.ones = mem(P // 2).bitcast(BF16)
        self.below = mem(P // 2).bitcast(BF16)

    ROUNDS = 15

    def prefix(self, pe, bank):
        k, nc = self.k, self.k.nc
        nc.tensor.matmul(bank[:, 0:NT * NE], self.below, self.flag.rearrange("p t e -> p (t e)"),
                         start=True, stop=False, skip_group_check=True)
        for t in range(NT - 1):
            later = NT - 1 - t
            src = self.flag[:, t:t + 1, :].to_broadcast([P, later, NE])
            ins = nc.tensor.matmul(bank[:, (t + 1) * NE:NT * NE].rearrange("p (t e) -> p t e", e=NE), self.ones, src,
                                   start=False, stop=(t == NT - 2), skip_group_check=True)
        return ins

    def tensor(self, pe):
        k, nc, b = self.k, self.k.nc, self.k.bank
        for r in range(self.ROUNDS + 1):
            pe.wait_ge(k.sem("counted"), r + 1)
            nc.tensor.matmul(b[r % 2][:, 0:3 * NE], k.w("ones"), self.cnt.rearrange("p j e -> p (j e)"),
                             start=True, stop=True)\
                .then_inc(k.sem("total"), 1)
        pe.wait_ge(k.sem("flags"), 1)
        self.prefix(pe, b[2]).then_inc(k.sem("prefixes"), 1)
        pe.wait_ge(k.sem("flags"), 2)
        self.prefix(pe, b[3]).then_inc(k.sem("prefixes"), 1)

    def vector(self, dve):
        k, nc, b, own = self.k, self.k.nc, self.k.bank, self.k.own["dve"]
        own.did(nc.vector.tensor_copy(self.ones, k.w("ones")))
        own.did(nc.vector.tensor_copy(self.below, k.w("below_")))
        own.did(nc.vector.memset(self.low, 0.0))
        low, cand, hit, bits = [v.bitcast(I32) for v in (self.low, self.cand, self.hit, self.bits)]
        for j in range(3):
            own.step(nc.vector.memset(bits[:, j], (j + 1) << (2 * self.ROUNDS - 2)))
        turned = self.ge.rearrange("p j t e -> p j e t")
        for r in range(self.ROUNDS):
            own.step(nc.vector.tensor_tensor(cand, bits, low.unsqueeze(1).to_broadcast([P, 3, NE]), ALU.bitwise_or))
            for j in range(3):
                own.did(nc.vector.tensor_tensor(self.ge[:, j], self.sc,
                                                self.cand[:, j].unsqueeze(1).to_broadcast([P, NT, NE]), ALU.is_ge))
            own.wait()
            nc.vector.tensor_reduce(self.cnt, turned, AX.X, ALU.add).then_inc(k.sem("counted"), 1)
            own.did(nc.vector.tensor_scalar(bits, bits, 2, None, ALU.logical_shift_right))
            dve.wait_ge(k.sem("total"), r + 1)
            own.step(nc.vector.tensor_scalar(hit, b[r % 2][:, 0:3 * NE].rearrange("p (j e) -> p j e", j=3),
                                             float(CAP), None, ALU.is_ge))
            for j in range(3):
                own.step(nc.vector.copy_predicated(low, hit[:, j], cand[:, j]))
        own.step(nc.vector.tensor_tensor(self.gt, self.sc, self.low.unsqueeze(1).to_broadcast([P, NT, NE]), ALU.is_gt))
        nc.vector.tensor_reduce(self.cnt[:, 0], self.gt.rearrange("p t e -> p e t"), AX.X, ALU.add)\
            .then_inc(k.sem("counted"), 1)
        nc.vector.tensor_tensor(self.flag, self.sc, self.low.unsqueeze(1).to_broadcast([P, NT, NE]), ALU.is_equal)\
            .then_inc(k.sem("flags"), 1)
        dve.wait_ge(k.sem("total"), self.ROUNDS + 1)
        own.step(nc.vector.tensor_scalar(self.need, b[self.ROUNDS % 2][:, 0:NE], -1.0, float(CAP), ALU.mult, ALU.add))
        dve.wait_ge(k.sem("prefixes"), 1)
        pre = b[2][:, 0:NT * NE].rearrange("p (t e) -> p t e", t=NT)
        own.step(nc.vector.tensor_tensor(self.fill, pre, self.need.unsqueeze(1).to_broadcast([P, NT, NE]), ALU.is_lt))
        own.step(nc.vector.tensor_tensor(self.fill, self.fill, self.flag, ALU.mult))
        own.step(nc.vector.tensor_tensor(self.mask, self.fill, self.gt, ALU.add))
        nc.vector.tensor_copy(self.flag, self.mask).then_inc(k.sem("flags"), 1)
        own.step(nc.vector.tensor_scalar(self.mask, self.mask, -4096.0, 4096.0, ALU.mult, ALU.add))
        dve.wait_ge(k.sem("prefixes"), 2)
        nc.vector.tensor_tensor(self.place[:, :, :].rearrange("p e t -> p t e"), self.mask,
                                b[3][:, 0:NT * NE].rearrange("p (t e) -> p t e", t=NT), ALU.add)

    def scalar(self, eng):
        pass

    gpsimd = sync = scalar


class Lists:

    def __init__(self, kit, place, index):
        self.k, self.place, self.index = kit, place, index
        mem = Arena(kit)
        self.at = mem(BATCH, NT)
        self.sel = [mem(NT * CAP // 2).bitcast(BF16).rearrange("p (t c) -> p t c", t=NT) for _ in range(2)]
        self.iota = mem(CAP // 2).bitcast(BF16)
        self.tok = mem(NT).bitcast(BF16).rearrange("p (t c) -> p t c", c=2)
        self.num = mem(BATCH * 2)
        self.half = mem(BATCH * 2)

    def vector(self, dve, i):
        k, nc, own = self.k, self.k.nc, self.k.own["dve"]
        own.did(nc.vector.tensor_copy(self.iota, k.w("iota256")))
        own.did(nc.vector.tensor_copy(self.tok, k.w("token_parts").rearrange("p (t c) -> p t c", c=2)))
        own.step(nc.vector.tensor_copy(self.at, self.place[:, bass.ds(i * BATCH, BATCH), :]))
        for j in range(BATCH):
            if j >= 2:
                dve.wait_ge(k.sem("listed"), j - 1)
            for t in range(NT):
                ins = nc.vector.tensor_scalar(self.sel[j % 2][:, t, :], self.iota, self.at[:, j, t:t + 1], None,
                                              ALU.is_equal)
            ins.then_inc(k.sem("selected"), 1)
        dve.wait_ge(k.sem("listed"), BATCH)
        v = k.bank[0][:, 0:BATCH * 4].rearrange("p (a c) -> p a c", c=2)
        own.step(nc.vector.tensor_copy(self.half, v[:, :, 1]))
        own.step(nc.vector.scalar_tensor_tensor(self.num, v[:, :, 0], float(P), self.half, ALU.mult, ALU.add))
        nc.vector.tensor_copy(self.index[:, bass.ds(i * 2 * BATCH, 2 * BATCH)], self.num)

    def tensor(self, pe, i):
        k, nc = self.k, self.k.nc
        for j in range(BATCH):
            pe.wait_ge(k.sem("selected"), j + 1)
            for t in range(NT):
                for h in range(2):
                    c = (2 * j + h) * 2
                    ins = nc.tensor.matmul(k.bank[0][:, c:c + 2], self.sel[j % 2][:, t, h * P:(h + 1) * P],
                                           self.tok[:, t, :], start=(t == 0 and h == 0), stop=(t == NT - 1),
                                           skip_group_check=True)
            ins.then_inc(k.sem("listed"), 1)


class Experts:

    def __init__(self, kit, index):
        self.k, self.index = kit, index
        mem = Arena(kit)
        self.idx = mem(2 * BATCH).bitcast(U32)
        self.rows = mem(BATCH, 2, NEXT)
        self.w = [mem(WE) for _ in range(2)]
        self.nT = [mem(CAP) for _ in range(2)]
        self.a = [mem(CAP) for _ in range(2)]
        self.h = [mem(CAP) for _ in range(2)]
        self.score = mem(BATCH, 2)
        self.out = mem(BATCH, 2, D)

    UNITS = [(j, u) for j in range(BATCH) for u in range(4)]

    def sync(self, sp, i, weights):
        k = self.k
        for j in range(BATCH):
            if j >= 2:
                sp.wait_ge(k.sem("down_done"), 4 * (j - 1))
            sp.dma_start(self.w[j % 2], weights[bass.ds(i * BATCH + j, 1)].rearrange("o p n -> p (o n)"))\
                .then_inc(k.sem(f"expert_w{j % 2}"), 16)

    def gpsimd(self, pool, i, n_ext, dst):
        k, nc = self.k, self.k.nc
        pool.wait_ge(k.sem("idx"), 1)
        for j in range(BATCH):
            for h in range(2):
                c = 2 * j + h
                nc.gpsimd.indirect_dma_start(self.rows[:, j, h, :], None, n_ext,
                                             bass.IndirectOffsetOnAxis(ap=self.idx[:, c:c + 1], axis=0))\
                    .then_inc(k.sem(f"gathered{j}"), 16)
        n = 0
        for j in range(BATCH):
            pool.wait_ge(k.sem("expert_out"), j + 1)
            for h in range(2):
                c = 2 * j + h
                if h == 0 and n:
                    pool.wait_ge(k.sem("added"), 16 * n)
                nc.gpsimd.indirect_dma_start(dst, bass.IndirectOffsetOnAxis(ap=self.idx[:, c:c + 1], axis=0),
                                             self.out[:, j, h, :], None, compute_op=ALU.add)\
                    .then_inc(k.sem("added"), 16)
                n += 1
        pool.wait_ge(k.sem("added"), 16 * n)
        pool.drain()
        pool.dma_reset(range(k.first, k.last + 1))

    def tensor(self, pe, i):
        k, nc, b = self.k, self.k.nc, self.k.bank

        def turn(j):
            pe.wait_ge(k.sem(f"gathered{j}"), 32)
            if j >= 2:
                pe.wait_ge(k.sem("expert_nT"), j - 1)
            for h in range(2):
                ins = nc.tensor.transpose(b[6 + j % 2][:, h * P:(h + 1) * P], self.rows[:, j, h, 0:D], k.w("ident"))
            ins.then_inc(k.sem("rows_turned"), 1)

        def up(n):
            j, u = self.UNITS[n]
            if u == 0:
                pe.wait_ge(k.sem("expert_nT"), j + 1)
                pe.wait_ge(k.sem(f"expert_w{j % 2}"), 16 * (j // 2 + 1))
            if n >= 2:
                pe.wait_ge(k.sem("h_ready"), n - 1)
            o = b[n % 2]
            w = self.w[j % 2]
            nc.tensor.matmul(o[:, 0:CAP], w[:, u * P:(u + 1) * P], self.nT[j % 2], start=True, stop=True)
            nc.tensor.matmul(o[:, CAP:2 * CAP], w[:, 512 + u * P:512 + (u + 1) * P], self.nT[j % 2],
                             start=True, stop=True).then_inc(k.sem("up_ready"), 1)

        def down(n):
            j, u = self.UNITS[n]
            pe.wait_ge(k.sem("h_ready"), n + 1)
            if u == 0 and j >= 2:
                pe.wait_ge(k.sem("expert_out"), j - 1)
            for h in range(2):
                ins = nc.tensor.matmul(b[4 + j % 2][:, h * D:(h + 1) * D], self.h[n % 2][:, h * P:(h + 1) * P],
                                       self.w[j % 2][:, 1024 + u * D:1024 + (u + 1) * D],
                                       start=(u == 0 and h == 0), stop=(u == 3), skip_group_check=True)
            ins.then_inc(k.sem("down_done"), 1)

        turn(0)
        up(0)
        for n in range(len(self.UNITS)):
            j, u = self.UNITS[n]
            if u == 1 and j + 1 < BATCH:
                turn(j + 1)
            if n + 1 < len(self.UNITS):
                up(n + 1)
            down(n)

    def scalar(self, act, i):
        k, nc, b = self.k, self.k.nc, self.k.bank

        def keep(j):
            act.wait_ge(k.sem("rows_turned"), j + 1)
            if j >= 2:
                act.wait_ge(k.sem("up_ready"), 4 * (j - 1))
            nc.scalar.copy(self.nT[j % 2], b[6 + j % 2][:, 0:CAP]).then_inc(k.sem("expert_nT"), 1)

        keep(0)
        for n, (j, u) in enumerate(self.UNITS):
            if u == 2 and j + 1 < BATCH:
                keep(j + 1)
            act.wait_ge(k.sem("up_ready"), n + 1)
            if n >= 2:
                act.wait_ge(k.sem("h_ready"), n - 1)
            nc.scalar.activation(self.a[n % 2], b[n % 2][:, 0:CAP], ACT.Gelu).then_inc(k.sem("a_ready"), 1)

    def vector(self, dve, i):
        k, nc, b, own = self.k, self.k.nc, self.k.bank, self.k.own["dve"]
        nc.vector.tensor_copy(self.idx, self.index[:, bass.ds(i * 2 * BATCH, 2 * BATCH)]).then_inc(k.sem("idx"), 1)

        def finish(j):
            dve.wait_ge(k.sem("down_done"), 4 * (j + 1))
            for h in range(2):
                ins = nc.vector.tensor_scalar(self.out[:, j, h, :], b[4 + j % 2][:, h * D:(h + 1) * D],
                                              self.score[:, j, h:h + 1], 0.5, ALU.mult, ALU.mult)
            ins.then_inc(k.sem("expert_out"), 1)

        for n, (j, u) in enumerate(self.UNITS):
            if u == 0:
                dve.wait_ge(k.sem(f"gathered{j}"), 32)
                own.step(nc.vector.tensor_copy(
                    self.score[:, j, :], self.rows[:, j, :, D:][:, :, bass.ds(i * BATCH + j, 1)]
                    .rearrange("p h o -> p (h o)")))
            dve.wait_ge(k.sem("a_ready"), n + 1)
            if n >= 2:
                dve.wait_ge(k.sem("down_done"), n - 1)
            nc.vector.tensor_tensor(self.h[n % 2], self.a[n % 2], b[n % 2][:, CAP:2 * CAP], ALU.mult)\
                .then_inc(k.sem("h_ready"), 1)
            if u == 1 and j >= 1:
                finish(j - 1)
        finish(BATCH - 1)


class L0Ffn:

    def __init__(self, kit, dram):
        self.k, self.dram = kit, dram
        nc, ctx = kit.nc, kit.ctx
        self.sc = ctx.enter_context(nc.sbuf_tensor("route_scores", [P, GROUPS, T, NE], F32))
        self.place = ctx.enter_context(nc.sbuf_tensor("route_place", [P, NE, NT], F32))
        self.index = ctx.enter_context(nc.sbuf_tensor("route_index", [P, 2 * NE], U32))
        self.route = RouteShared(kit, self.sc)
        self.choose = Choose(kit, self.sc[:, :, :, :], self.place)
        self.lists = Lists(kit, self.place, self.index)
        self.experts = Experts(kit, self.index)

    def run(self, eng, name, method, src, dst, n_ext, routed, listed):
        k = self.k
        stream = Stream(k, src, dst)
        stream.begin(eng, name)
        with eng.Fori(0, GROUPS) as g:
            if name == "sp":
                self.route.sync(eng, g, n_ext)
            else:
                method(self.route)(eng, g)
            k.end(eng, name)
            stream.swap(eng, name, g)
        stream.finish(eng, name)
        if routed:
            routed()
        method(self.choose)(eng)
        k.end(eng, name)
        with eng.Fori(0, NE // BATCH) as i:
            if name in ("pe", "dve"):
                method(self.lists)(eng, i)
            k.end(eng, name)
        if listed:
            listed()
        with eng.Fori(0, NE // BATCH) as i:
            if name == "sp":
                self.experts.sync(eng, i, self.dram["L0_experts"])
            elif name == "pool":
                self.experts.gpsimd(eng, i, n_ext, dst)
            else:
                method(self.experts)(eng, i)
            k.end(eng, name)


def l0ffn_weights(i, tiles, spread):
    token = np.arange(TOKENS).reshape(NT, P)
    return {
        "L0f_gate": i["L0_ffn_gate_w"].T, "L0f_Sg": i["L0_ffn_Sg"].T, "L0f_Su": i["L0_ffn_Su"].T,
        "L0f_Sd": tiles(i["L0_ffn_Sd"].T, D),
        "below_": np.triu(np.ones((P, P), np.float32), 1),
        "iota256": spread(np.arange(CAP, dtype=np.float32)),
        "token_parts": np.stack([token // P, token % P], -1).transpose(1, 0, 2).reshape(P, -1).astype(np.float32),
    }


def extra_inputs(i):
    down = i["L0_ffn_Wd"].transpose(0, 2, 1).reshape(NE, 4, P, D).transpose(0, 2, 1, 3).reshape(NE, P, 4 * D)
    return {"L0_experts": np.ascontiguousarray(np.concatenate(
        [i["L0_ffn_Wg"].transpose(0, 2, 1), i["L0_ffn_Wu"].transpose(0, 2, 1), down], 2))}


MORE_WEIGHTS += [l0ffn_weights]


H2 = 4
FIR = 64
PE_TAPS = 32


class PrepL2:

    def __init__(self, kit):
        self.k = kit

        def keep(name, n):
            return kit.ctx.enter_context(kit.nc.sbuf_tensor("l2_" + name, [P, n], F32))
        self.diag, self.bias, self.rtemp, self.share = keep("diag", PE_TAPS * P), keep("bias", 16), keep("rtemp", 4), keep("share", 4)
        self.t = [keep(f"t{i}", 4) for i in range(6)]

    def scalar(self, act):
        k, nc, t = self.k, self.k.nc, self.t
        nc.scalar.activation(t[0][:, :], k.w("L2a_log_temp"), ACT.Abs).then_inc(k.sem("temp_abs"), 1)
        act.wait_ge(k.sem("temp_abs"), 1)
        nc.scalar.activation(t[1][:, :], t[0][:, :], ACT.Exp, scale=-1.0).then_inc(k.sem("temp_e"), 1)
        nc.scalar.activation(self.share[:, :], k.w("L2a_residual_logit"), ACT.Sigmoid).then_inc(k.sem("share"), 1)

    def vector(self, dve):
        k, nc, own, t = self.k, self.k.nc, self.k.own["dve"], self.t
        for j in range(PE_TAPS):
            own.did(nc.vector.tensor_scalar(self.diag[:, j * P:(j + 1) * P], k.w("ident"),
                                            k.row("L2a_fir_long", j, j + 1), None, ALU.mult))
        own.step(nc.vector.tensor_tensor(self.bias[:, :], k.w("L2a_b2"), k.w("L2a_base_bias"), ALU.add))
        dve.wait_ge(k.sem("temp_e"), 1)
        own.step(softplus(k, t[4][:, :], k.w("L2a_log_temp"), t[1][:, :], t[2][:, :], t[3][:, :]))
        own.step(nc.vector.tensor_scalar(t[4][:, :], t[4][:, :], 1e-4, None, ALU.add))
        own.step(nc.vector.reciprocal(self.rtemp[:, :], t[4][:, :]))
        dve.wait_ge(k.sem("share"), 1)
        nc.vector.tensor_scalar(self.share[:, :], self.share[:, :], 0.5, None, ALU.mult)

    def tensor(self, pe):
        pass

    gpsimd = sync = tensor


class L2State:

    def __init__(self, kit, prep):
        self.prep, self.mem = prep, Arena(kit)
        mem = self.mem
        self.qT, self.kT = mem(GT), mem(GT)
        self.F = mem(T, 4, D)
        self.ktok = mem(T, D)
        self.vk = mem(T, H2, 64)
        self.beta, self.nbeta = mem(T, H2), mem(T, H2)
        self.after = self.mem.at


class L2Project:

    def __init__(self, kit, st):
        self.k, self.st = kit, st
        mem = st.mem
        mem.at = st.after
        self.norm = Norm(kit, mem, kit.x, 1e-5)
        self.pre = [mem(NB, 3 + SEQ) for _ in range(3)]
        self.c = [[mem(NB, SEQ) for _ in range(2)] for _ in range(3)]
        self.act_ = [mem(GT) for _ in range(2)]
        self.sq = [mem(GT) for _ in range(2)]
        self.ss = [mem(GT) for _ in range(2)]
        self.vf = mem(NB, FIR - 1 + SEQ)
        self.vcopy = mem(GT)
        self.fs = [mem(NB, SEQ) for _ in range(2)]
        self.fl = mem(GT)
        self.part = [[mem(NB, SEQ) for _ in range(2)] for _ in range(2)]

    @staticmethod
    def two(v):
        return v.rearrange("p (b s) -> p b s", b=NB)

    def tensor(self, pe):
        k, nc, b = self.k, self.k.nc, self.k.bank
        self.norm.tensor(pe, b[7])
        pe.wait_ge(k.sem("nT"), 1)
        for i, w in ((2, "Wv"), (0, "Wq"), (1, "Wk")):
            nc.tensor.matmul(b[i][:, :], k.w("L2a_" + w), k.nT[:, :], start=True, stop=True)\
                .then_inc(k.sem("projected"), 1)
        for t in range(T):
            ins = nc.tensor.matmul(b[3][:, t * H2:(t + 1) * H2], k.nT[:, t * P:(t + 1) * P], k.w("L2a_Wb"),
                                   start=True, stop=True)
        ins.then_inc(k.sem("beta_made"), 1)
        pe.wait_ge(k.sem("v_act"), 1)
        for j in range(PE_TAPS):
            ins = nc.tensor.matmul(self.two(b[6][:, :]), self.st.prep.diag[:, j * P:(j + 1) * P],
                                   self.vf[:, :, j:j + SEQ], start=(j == 0), stop=(j == PE_TAPS - 1))
            if j == 15:
                for i in range(2):
                    pe.wait_ge(k.sem("squared"), i + 1)
                    nc.tensor.matmul(b[4 + i][:, :], k.w("blocks32"), self.sq[i], start=True, stop=True)\
                        .then_inc(k.sem("sumsq"), 1)
        ins.then_inc(k.sem("long_made"), 1)
        for i, (name, count, src) in enumerate(self.turned()):
            pe.wait_ge(k.sem(name), count)
            if i >= 2:
                pe.wait_ge(k.sem("token_kept"), i - 1)
            for t in range(T):
                ins = nc.tensor.transpose(b[i % 2][:, t * P:(t + 1) * P], src[:, t * P:(t + 1) * P], k.w("ident"))
            ins.then_inc(k.sem("token_turned"), 1)

    def turned(self):
        return [("vcopy", 1, self.vcopy), ("k_normal", 1, self.st.kT), ("short_taps", 5, self.fs[0].rearrange("p b s -> p (b s)")),
                ("long", 1, self.fl)]

    def scalar(self, act):
        k, nc, b = self.k, self.k.nc, self.k.bank
        self.norm.scalar(act, b[7])
        for n, i in enumerate((2, 0, 1)):
            act.wait_ge(k.sem("projected"), n + 1)
            nc.scalar.copy(self.pre[i][:, :, 3:], self.two(b[i][:, :])).then_inc(k.sem("pre"), 1)
        act.wait_ge(k.sem("conv2"), 4)
        act.wait_ge(k.sem("pads"), 1)
        nc.scalar.activation(self.c[2][0], self.c[2][1], ACT.Sigmoid).then_inc(k.sem("sigmoid"), 1)
        for i in range(2):
            act.wait_ge(k.sem(f"conv{i}"), 4)
            nc.scalar.activation(self.c[i][0], self.c[i][1], ACT.Sigmoid).then_inc(k.sem("sigmoid"), 1)
        for i in range(2):
            act.wait_ge(k.sem("qk_act"), i + 1)
            nc.scalar.activation(self.sq[i], self.act_[i], ACT.Square).then_inc(k.sem("squared"), 1)
        act.wait_ge(k.sem("beta_made"), 1)
        nc.scalar.activation(self.st.beta, b[3][:, 0:T * H2].rearrange("p (t h) -> p t h", t=T), ACT.Sigmoid)\
            .then_inc(k.sem("beta"), 1)
        for i in range(2):
            act.wait_ge(k.sem("sumsq_eps"), i + 1)
            nc.scalar.activation(self.sq[i], self.ss[i], ACT.Ln).then_inc(k.sem("log_ss"), 1)
            act.wait_ge(k.sem("log_ss"), i + 1)
            nc.scalar.activation(self.ss[i], self.sq[i], ACT.Exp, scale=-0.5).then_inc(k.sem("rnorm"), 1)

    def vector(self, dve):
        k, nc, b, own, st = self.k, self.k.nc, self.k.bank, self.k.own["dve"], self.st
        for i in range(3):
            own.did(nc.vector.memset(self.pre[i][:, :, 0:3], 0.0))
        nc.vector.memset(self.vf[:, :, 0:FIR - 1], 0.0).then_inc(k.sem("pads"), 1)
        self.norm.vector(dve)

        def silu(n, dst, i):
            dve.wait_ge(k.sem("sigmoid"), n + 1)
            nc.vector.tensor_tensor(dst, self.c[i][0], self.c[i][1], ALU.mult)\
                .then_inc(k.sem("v_act" if i == 2 else "qk_act"), 1)

        dve.wait_ge(k.sem("pre"), 1)
        self.taps(dve, (self.c[2], self.pre[2], 0, "L2a_conv_v", 0, 4, "conv2"))
        dve.wait_ge(k.sem("pre"), 2)
        self.taps(dve, (self.c[0], self.pre[0], 0, "L2a_conv_q", 0, 4, "conv0"))
        silu(0, self.vf[:, :, FIR - 1:], 2)
        dve.wait_ge(k.sem("pre"), 3)
        self.taps(dve, (self.c[1], self.pre[1], 0, "L2a_conv_k", 0, 4, "conv1"))
        silu(1, self.two(self.act_[0]), 0)
        silu(2, self.two(self.act_[1]), 1)
        dve.wait_ge(k.sem("v_act"), 1)
        nc.vector.tensor_copy(self.two(self.vcopy), self.vf[:, :, FIR - 1:]).then_inc(k.sem("vcopy"), 1)
        half = (FIR - PE_TAPS) // 2
        self.taps(dve, (self.fs, self.vf, FIR - 5, "L2a_fir_short", 0, 5, "short_taps"),
                  (self.part[0], self.vf, PE_TAPS, "L2a_fir_long_rest", 0, half, "long_taps0"),
                  (self.part[1], self.vf, PE_TAPS + half, "L2a_fir_long_rest", half, half, "long_taps1"))
        for i in range(2):
            dve.wait_ge(k.sem(f"long_taps{i}"), half)
        own.step(nc.vector.tensor_tensor(self.part[0][1], self.part[0][1], self.part[1][1], ALU.add))
        for i in range(2):
            dve.wait_ge(k.sem("sumsq"), i + 1)
            nc.vector.tensor_scalar(self.ss[i], b[4 + i][:, :], 1e-6, None, ALU.add).then_inc(k.sem("sumsq_eps"), 1)
        for i, dst in enumerate((st.qT, st.kT)):
            dve.wait_ge(k.sem("rnorm"), i + 1)
            ins = nc.vector.tensor_tensor(dst, self.act_[i], self.ss[i], ALU.mult)
        ins.then_inc(k.sem("k_normal"), 1)
        dve.wait_ge(k.sem("beta"), 1)
        own.step(nc.vector.tensor_scalar(st.nbeta, st.beta, -1.0, None, ALU.mult))

        def heads(v):
            return v.rearrange("p t (h c) -> p t h c", h=H2)
        beta = over(st.beta, P, T, H2, 32)
        dve.wait_ge(k.sem("token_turned"), 1)
        tok = b[0][:, :].rearrange("p (t d) -> p t d", t=T)
        own.did(nc.vector.tensor_tensor(st.vk[:, :, :, 0:32], heads(tok), beta, ALU.mult))
        nc.vector.tensor_copy(st.F[:, :, 3, :], tok).then_inc(k.sem("token_kept"), 1)
        dve.wait_ge(k.sem("token_turned"), 2)
        tok = b[1][:, :].rearrange("p (t d) -> p t d", t=T)
        own.did(nc.vector.tensor_tensor(st.vk[:, :, :, 32:64], heads(tok), beta, ALU.mult))
        nc.vector.tensor_copy(st.ktok, tok).then_inc(k.sem("token_kept"), 1)
        dve.wait_ge(k.sem("long_made"), 1)
        nc.vector.tensor_tensor(self.two(self.fl), self.part[0][1], self.two(b[6][:, :]), ALU.add)\
            .then_inc(k.sem("long"), 1)
        for i in (2, 3):
            dve.wait_ge(k.sem("token_turned"), i + 1)
            nc.vector.tensor_copy(st.F[:, :, i - 2, :], b[i % 2][:, :].rearrange("p (t d) -> p t d", t=T))\
                .then_inc(k.sem("token_kept"), 1)

    def taps(self, dve, *filters):
        k, nc = self.k, self.k.nc
        for j in range(max(f[5] for f in filters)):
            for dst, src, off, name, first, n, sem in filters:
                if j >= n:
                    continue
                s = src[:, :, off + j:off + j + SEQ]
                w = k.row(name, first + j, first + j + 1)
                if j == 0:
                    ins = nc.vector.tensor_scalar(dst[0], s, w, None, ALU.mult)
                else:
                    dve.wait_ge(k.sem(sem), j)
                    ins = nc.vector.scalar_tensor_tensor(dst[j % 2], s, w, dst[(j + 1) % 2], ALU.mult, ALU.add)
                ins.then_inc(k.sem(sem), 1)

    def gpsimd(self, pool):
        self.norm.gpsimd(pool)

    def sync(self, sp):
        pass


class L2Delta:

    def __init__(self, kit, st):
        self.k, self.st = kit, st
        mem = st.mem
        mem.at = st.after
        self.MT = [mem(GT) for _ in range(H2)]
        self.LT = [mem(GT) for _ in range(2)]
        self.X = [mem(GT) for _ in range(H2)]
        self.R = [mem(GT) for _ in range(H2)]
        self.Y = [mem(GT) for _ in range(H2)]
        self.U = mem(T, D)
        self.wtok = mem(T, D)
        self.wT = mem(GT)
        self.ut = mem(T, D)
        self.S = [mem(D) for _ in range(NB)]

    def rows(self, h):
        return slice(32 * h, 32 * h + 32)

    def tensor(self, pe):
        k, nc, b, st = self.k, self.k.nc, self.k.bank, self.st
        tile = lambda v, t: v[:, t * P:(t + 1) * P]
        for h in range(H2):
            for t in range(T):
                kk = st.kT[self.rows(h), t * P:(t + 1) * P]
                ins = nc.tensor.matmul(tile(b[h], t), kk, kk, start=True, stop=True)
            ins.then_inc(k.sem("gram"), 1)
        for h in range(H2):
            pe.wait_ge(k.sem("M0"), h + 1)
            for t in range(T):
                ins = nc.tensor.transpose(tile(b[4 + h], t), tile(self.Y[h], t), k.w("ident"))
            ins.then_inc(k.sem("M0_turned"), 1)
        pe.wait_ge(k.sem("M0"), H2)
        pe.wait_ge(k.sem("MT0"), H2)
        for m in range(17):
            h = m % 4
            if m < 16:
                pe.wait_ge(k.sem("LT"), m + 1)
                pe.wait_ge(k.sem("X"), m + 1)
                if m >= 2:
                    pe.wait_ge(k.sem("Y"), m - 1)
                for t in range(T):
                    ins = nc.tensor.matmul(tile(b[m % 2], t), tile(self.LT[m % 2], t), tile(self.X[h], t),
                                           start=True, stop=True)
                ins.then_inc(k.sem("Y_made"), 1)
            if m >= 1:
                self.grow(pe, m - 1)
        for t in range(T):
            for h in range(H2):
                if t == 0:
                    pe.wait_ge(k.sem("R"), 4 * 4 + h + 1)
                ins = nc.tensor.matmul(b[t // 2][:, (t % 2) * 256 + h * 64:(t % 2) * 256 + (h + 1) * 64],
                                       tile(self.R[h], t), st.vk[:, t, h, :], start=True, stop=True)
            if t % 2 == 1:
                ins.then_inc(k.sem("UW"), 1)
        for h in range(H2):
            bank = b[2 + h]
            for t in range(T):
                ins = nc.tensor.matmul(tile(bank, t), st.kT[self.rows(h), t * P:(t + 1) * P],
                                       st.qT[self.rows(h), t * P:(t + 1) * P], start=True, stop=True)
            ins.then_inc(k.sem("local"), 1)
        pe.wait_ge(k.sem("w_kept"), 1)
        for t in range(T):
            ins = nc.tensor.transpose(tile(b[6], t), self.wtok[:, t, :], k.w("ident"))
        ins.then_inc(k.sem("w_turned"), 1)
        pe.wait_ge(k.sem("wT"), 1)
        pe.wait_ge(k.sem("local_kept"), H2)
        for j in range(8):
            for s in range(NB):
                t, r = 2 * s + j // 4, j % 4
                rows = self.rows(r)
                cols = slice(t * P + 32 * r, t * P + 32 * r + 32)
                pe.wait_ge(k.sem(f"state{s}"), j + 1)
                nc.tensor.matmul(b[s][rows, 0:D], self.wT[:, cols], self.S[s], start=True, stop=True)\
                    .then_inc(k.sem(f"wS{s}"), 1)
                nc.tensor.matmul(b[4 + t][rows, 0:D], st.qT[:, cols], self.S[s], start=True, stop=False,
                                 skip_group_check=True)
            for s in range(NB):
                t, r = 2 * s + j // 4, j % 4
                rows = self.rows(r)
                pe.wait_ge(k.sem(f"u{s}"), j + 1)
                nc.tensor.matmul(b[2 + s][:, 0:D], st.ktok[rows, t, :], self.ut[rows, t, :], start=(j == 0),
                                 stop=True, skip_group_check=True).then_inc(k.sem(f"kTu{s}"), 1)
                if j % 4 == 3:
                    for h in range(H2):
                        ins = nc.tensor.matmul(b[4 + t][:, 32 * h:32 * h + 32], tile(self.X[h], t),
                                               self.ut[:, t, 32 * h:32 * h + 32], start=False, stop=True,
                                               skip_group_check=True)
                    ins.then_inc(k.sem("delta_made"), 1)

    def grow(self, pe, m):
        k, nc, b = self.k, self.k.nc, self.k.bank
        h = m % 4
        tile = lambda v, t: v[:, t * P:(t + 1) * P]
        pe.wait_ge(k.sem("Y"), m + 1)
        pe.wait_ge(k.sem("R"), m + 1)
        if m >= 2:
            pe.wait_ge(k.sem("R"), m + 3)
            if m < 12:
                pe.wait_ge(k.sem("X"), m + 3)
        for t in range(T):
            ins = nc.tensor.matmul(tile(b[4 + m % 2], t), tile(self.Y[h], t), tile(self.R[h], t), start=True, stop=True)
        if m < 12:
            for t in range(T):
                ins = nc.tensor.matmul(tile(b[2 + m % 2], t), tile(self.R[h], t), tile(self.Y[h], t),
                                       start=True, stop=True)
        ins.then_inc(k.sem("grown"), 1)

    def scalar(self, act):
        k, nc, b = self.k, self.k.nc, self.k.bank
        for h in range(H2):
            for v in (self.X[h], self.R[h]):
                nc.scalar.copy(v.rearrange("p (t c) -> p t c", t=T), k.w("ident").unsqueeze(1).to_broadcast([P, T, P]))\
                    .then_inc(k.sem("identity"), 1)
        for h in range(H2):
            act.wait_ge(k.sem("M0_turned"), h + 1)
            nc.scalar.copy(self.MT[h], b[4 + h][:, :]).then_inc(k.sem("MT0"), 1)
        for m in range(16):
            act.wait_ge(k.sem("Y_made"), m + 1)
            if m < 4:
                act.wait_ge(k.sem("X"), m + 1)
            else:
                act.wait_ge(k.sem("grown"), m - 3)
            nc.scalar.copy(self.Y[m % 4], b[m % 2][:, :]).then_inc(k.sem("Y"), 1)
        act.wait_ge(k.sem("w_turned"), 1)
        nc.scalar.copy(self.wT, b[6][:, :]).then_inc(k.sem("wT"), 1)
        for n, (s, half) in enumerate(((0, 0), (1, 0), (0, 1), (1, 1))):
            t = 2 * s + half
            act.wait_ge(k.sem("delta_made"), n + 1)
            nc.scalar.copy(self.st.F[:, t, 2, :], b[4 + t][:, 0:D])

    def vector(self, dve):
        k, nc, b, own, st = self.k, self.k.nc, self.k.bank, self.k.own["dve"], self.st
        tiles = lambda v: v.rearrange("p (t c) -> p t c", t=T)
        every = lambda name: k.w(name).unsqueeze(1).to_broadcast([P, T, P])
        for h in range(H2):
            dve.wait_ge(k.sem("gram"), h + 1)
            for t in range(T):
                ins = nc.vector.scalar_tensor_tensor(self.Y[h][:, t * P:(t + 1) * P], b[h][:, t * P:(t + 1) * P],
                                                     st.nbeta[:, t, h:h + 1], k.w("chunk_lower"), ALU.mult, ALU.mult)
            ins.then_inc(k.sem("M0"), 1)
        for h in range(H2):
            dve.wait_ge(k.sem("M0"), h + 1)
            dve.wait_ge(k.sem("identity"), 2 * h + 1)
            nc.vector.copy_predicated(tiles(self.X[h]), every("below1").bitcast(I32), tiles(self.Y[h]))\
                .then_inc(k.sem("X"), 1)
        for h in range(H2):
            dve.wait_ge(k.sem("MT0"), h + 1)
            dve.wait_ge(k.sem("identity"), 2 * h + 2)
            nc.vector.copy_predicated(tiles(self.R[h]), every("above1").bitcast(I32), tiles(self.MT[h]))\
                .then_inc(k.sem("R"), 1)
        for m in range(16):
            h = m % 4
            dve.wait_ge(k.sem("grown"), m + 1)
            if m < 12:
                nc.vector.tensor_tensor(self.X[h], self.X[h], b[2 + m % 2][:, :], ALU.add).then_inc(k.sem("X"), 1)
            nc.vector.tensor_tensor(self.R[h], self.R[h], b[4 + m % 2][:, :], ALU.add).then_inc(k.sem("R"), 1)
        for i in range(2):
            dve.wait_ge(k.sem("UW"), i + 1)
            v = b[i][:, :].rearrange("p (t h c) -> p t h c", t=2, h=H2)
            own.did(nc.vector.tensor_copy(self.U[:, 2 * i:2 * i + 2, :].rearrange("p t (h c) -> p t h c", h=H2),
                                          v[:, :, :, 0:32]))
            own.did(nc.vector.tensor_copy(self.wtok[:, 2 * i:2 * i + 2, :].rearrange("p t (h c) -> p t h c", h=H2),
                                          v[:, :, :, 32:64]))
        own.wait()
        nc.vector.sem_inc(k.sem("w_kept"), 1)
        upper = k.w("chunk_upper").unsqueeze(1).to_broadcast([P, T, P])
        for h in range(H2):
            dve.wait_ge(k.sem("local"), h + 1)
            nc.vector.tensor_tensor(self.X[h].rearrange("p (t c) -> p t c", t=T),
                                    b[2 + h][:, :].rearrange("p (t c) -> p t c", t=T), upper, ALU.mult)\
                .then_inc(k.sem("local_kept"), 1)
        for s in range(NB):
            nc.vector.memset(self.S[s], 0.0).then_inc(k.sem(f"state{s}"), 1)
        for j in range(8):
            for s in range(NB):
                t, rows = 2 * s + j // 4, self.rows(j % 4)
                dve.wait_ge(k.sem(f"wS{s}"), j + 1)
                nc.vector.tensor_tensor(self.ut[rows, t, :], self.U[rows, t, :], b[s][rows, 0:D], ALU.subtract)\
                    .then_inc(k.sem(f"u{s}"), 1)
            for s in range(NB):
                if j < 7:
                    dve.wait_ge(k.sem(f"kTu{s}"), j + 1)
                    nc.vector.tensor_tensor(self.S[s], b[2 + s][:, 0:D], k.w("blocks32"), ALU.mult)\
                        .then_inc(k.sem(f"state{s}"), 1)

    def gpsimd(self, pool):
        k, nc = self.k, self.k.nc
        for m in range(16):
            h = m % 4
            if m < 4:
                pool.wait_ge(k.sem("MT0"), h + 1)
            if m >= 2:
                pool.wait_ge(k.sem("Y_made"), m - 1)
            mask = k.w(f"above{2 << (m // 4)}").unsqueeze(1).to_broadcast([P, T, P])
            nc.gpsimd.tensor_tensor(self.LT[m % 2].rearrange("p (t c) -> p t c", t=T),
                                    self.MT[h].rearrange("p (t c) -> p t c", t=T), mask, ALU.mult)\
                .then_inc(k.sem("LT"), 1)

    def sync(self, sp):
        pass


class L2Mix:

    def __init__(self, kit, st):
        self.k, self.st = kit, st
        mem = st.mem
        mem.at = st.after
        self.sq = mem(T * 16, 32)
        self.sum, self.abs, self.ss = [mem(T * 16) for _ in range(3)]
        self.msq = mem(T * 16)
        self.stats = mem(T, H2, 4, 4)
        self.l2 = mem(T * 16)
        self.stT = mem(GT, rows=64)
        self.h1 = [mem(GT) for _ in range(2)]
        self.z, self.p = mem(T * H2, 4), mem(T * H2, 4)
        self.mx, self.tot, self.rec = mem(T * H2), mem(T * H2), mem(T * H2)
        self.prod = mem(T, 4, D)
        self.o = mem(T, D)
        self.osq = mem(T, D)
        self.oss, self.ors = mem(T * H2), mem(T * H2)
        self.oT = mem(GT)

    def tensor(self, pe):
        k, nc, b = self.k, self.k.nc, self.k.bank
        hidden = [b[i] for i in (1, 2, 6, 7)]
        for h in range(H2):
            nc.tensor.matmul(hidden[h][:, :], k.w("L2a_W1x"), k.nT[:, :], start=True, stop=False)
        pe.wait_ge(k.sem("stats"), 1)
        for t in range(T):
            ins = nc.tensor.transpose(b[0][0:64, t * P:(t + 1) * P], self.stats[:, t].rearrange("p h s c -> p (h s c)"),
                                      k.w("ident"))
        ins.then_inc(k.sem("stats_turned"), 1)
        pe.wait_ge(k.sem("stT"), 1)
        for h in range(H2 + 1):
            if h < H2:
                nc.tensor.matmul(hidden[h][:, :], k.row("L2a_W1s", h * P, (h + 1) * P, hi=64), self.stT,
                                 start=False, stop=True).then_inc(k.sem("h1_made"), 1)
            if h >= 1:
                g = h - 1
                pe.wait_ge(k.sem("h1"), g + 1)
                for t in range(T):
                    c = (t * H2 + g) * 4
                    ins = nc.tensor.matmul(b[3][:, c:c + 4], self.h1[g % 2][:, t * P:(t + 1) * P], k.w("L2a_W2"),
                                           start=True, stop=True)
                ins.then_inc(k.sem("logits"), 1)
        pe.wait_ge(k.sem("o_normal"), 1)
        for t in range(T):
            ins = nc.tensor.transpose(b[4][:, t * P:(t + 1) * P], self.osq[:, t, :], k.w("ident"))
        ins.then_inc(k.sem("o_turned"), 1)
        pe.wait_ge(k.sem("oT"), 1)
        for t in range(T):
            ins = nc.tensor.matmul(b[5][:, t * D:(t + 1) * D], self.oT[:, t * P:(t + 1) * P], k.w("L2a_Wo"),
                                   start=True, stop=True)
        ins.then_inc(k.sem("out_made"), 1)

    def scalar(self, act):
        k, nc, b = self.k, self.k.nc, self.k.bank
        F = self.st.F.rearrange("p t s (h c) -> p (t s h) c", h=H2)
        nc.scalar.activation(self.sq, F, ACT.Square).then_inc(k.sem("F_squared"), 1)
        act.wait_ge(k.sem("ss"), 1)
        nc.scalar.activation(self.l2, self.ss, ACT.Sqrt).then_inc(k.sem("l2"), 1)
        act.wait_ge(k.sem("stats_turned"), 1)
        nc.scalar.copy(self.stT, b[0][0:64, :]).then_inc(k.sem("stT"), 1)
        for h in range(H2):
            act.wait_ge(k.sem("h1_made"), h + 1)
            if h >= 2:
                act.wait_ge(k.sem("logits"), h - 1)
            nc.scalar.activation(self.h1[h % 2], b[(1, 2, 6, 7)[h]][:, :], ACT.Gelu, bias=k.w("L2a_b1"))\
                .then_inc(k.sem("h1"), 1)
        act.wait_ge(k.sem("z_shifted"), 1)
        nc.scalar.activation(self.p, self.z, ACT.Exp).then_inc(k.sem("p_exp"), 1)
        act.wait_ge(k.sem("mixed"), 1)
        nc.scalar.activation(self.osq, self.o, ACT.Square).then_inc(k.sem("o_squared"), 1)
        act.wait_ge(k.sem("o_ms"), 1)
        nc.scalar.activation(self.ors, self.oss, ACT.Sqrt).then_inc(k.sem("o_rs"), 1)
        act.wait_ge(k.sem("o_turned"), 1)
        nc.scalar.copy(self.oT, b[4][:, :]).then_inc(k.sem("oT"), 1)

    def vector(self, dve):
        k, nc, b, own, st = self.k, self.k.nc, self.k.bank, self.k.own["dve"], self.st
        F = st.F.rearrange("p t s (h c) -> p (t s h) c", h=H2)
        own.did(nc.vector.tensor_reduce(self.sum, F, AX.X, ALU.add))
        own.did(nc.vector.tensor_reduce(self.abs, F, AX.X, ALU.add, apply_absolute_value=True))
        dve.wait_ge(k.sem("F_squared"), 1)
        nc.vector.tensor_reduce(self.ss, self.sq, AX.X, ALU.add).then_inc(k.sem("ss"), 1)

        def stat(i):
            return self.stats[:, :, :, :, i].rearrange("p t h s -> p t s h")

        def tsh(v):
            return v.rearrange("p (t s h) -> p t s h", t=T, s=4)
        own.wait()
        own.step(nc.vector.tensor_scalar(self.sum, self.sum, 1.0 / 32, None, ALU.mult))
        own.did(nc.vector.tensor_copy(stat(0), tsh(self.sum)))
        own.did(nc.vector.tensor_scalar(stat(2), tsh(self.abs), 1.0 / 32, None, ALU.mult))
        own.did(nc.vector.tensor_tensor(self.msq, self.sum, self.sum, ALU.mult))
        dve.wait_ge(k.sem("ss"), 1)
        own.wait()
        own.step(nc.vector.scalar_tensor_tensor(self.msq, self.ss, 1.0 / 32, self.msq, ALU.mult, ALU.subtract))
        own.did(nc.vector.tensor_copy(stat(1), tsh(self.msq)))
        dve.wait_ge(k.sem("l2"), 1)
        own.step(nc.vector.tensor_copy(stat(3), tsh(self.l2)))
        nc.vector.sem_inc(k.sem("stats"), 1)
        dve.wait_ge(k.sem("logits"), H2)
        z3 = self.z.rearrange("p (t h) c -> p t h c", t=T)
        z2 = self.z.rearrange("p (t h) c -> p t (h c)", t=T)
        lg = b[3][:, 0:T * 16].rearrange("p (t c) -> p t c", t=T)
        own.step(nc.vector.tensor_tensor(z2, lg, st.prep.bias[:, :].unsqueeze(1).to_broadcast([P, T, 16]), ALU.add))
        for t in range(T):
            own.did(nc.vector.tensor_tensor(z3[:, t], z3[:, t], over(st.prep.rtemp[:, :], P, H2, 4), ALU.mult))
        own.wait()
        own.step(nc.vector.tensor_reduce(self.mx, self.z, AX.X, ALU.max))
        nc.vector.tensor_tensor(self.z, self.z, over(self.mx, P, T * H2, 4), ALU.subtract)\
            .then_inc(k.sem("z_shifted"), 1)
        dve.wait_ge(k.sem("p_exp"), 1)
        for floor in (True, False):
            own.step(nc.vector.tensor_reduce(self.tot, self.p, AX.X, ALU.add))
            own.step(nc.vector.reciprocal(self.rec, self.tot))
            own.step(nc.vector.tensor_tensor(self.p, self.p, over(self.rec, P, T * H2, 4), ALU.mult))
            if floor:
                own.step(nc.vector.tensor_scalar(self.p[:, :, 0:2], self.p[:, :, 0:2], 0.05, None, ALU.max))
        p4 = self.p.rearrange("p (t h) s -> p t h s", t=T)
        own.step(nc.vector.tensor_tensor(p4[:, :, :, 0], p4[:, :, :, 0],
                                         st.prep.share[:, :].unsqueeze(1).to_broadcast([P, T, H2]), ALU.add))
        for t in range(T):
            own.did(nc.vector.tensor_tensor(self.prod[:, t].rearrange("p s (h c) -> p s h c", h=H2),
                                            st.F[:, t].rearrange("p s (h c) -> p s h c", h=H2),
                                            over(p4[:, t].rearrange("p h s -> p s h"), P, 4, H2, 32), ALU.mult))
        own.wait()
        for t in range(T):
            ins = nc.vector.tensor_reduce(self.o[:, t, :], self.prod[:, t].rearrange("p s d -> p d s"), AX.X, ALU.add)
        ins.then_inc(k.sem("mixed"), 1)
        dve.wait_ge(k.sem("o_squared"), 1)
        heads = lambda v: v.rearrange("p t (h c) -> p (t h) c", h=H2)
        own.step(nc.vector.tensor_reduce(self.oss, heads(self.osq), AX.X, ALU.add))
        own.step(nc.vector.tensor_scalar(self.oss, self.oss, 1.0 / 32, 1e-5, ALU.mult, ALU.add))
        nc.vector.reciprocal(self.oss, self.oss).then_inc(k.sem("o_ms"), 1)
        dve.wait_ge(k.sem("o_rs"), 1)
        own.step(nc.vector.tensor_tensor(heads(self.o), heads(self.o), over(self.ors, P, T * H2, 32), ALU.mult))
        nc.vector.tensor_tensor(heads(self.osq), heads(self.o),
                                k.w("L2a_rms_w").unsqueeze(1).to_broadcast([P, T * H2, 32]), ALU.mult)\
            .then_inc(k.sem("o_normal"), 1)
        dve.wait_ge(k.sem("out_made"), 1)
        nc.vector.tensor_tensor(k.x[:, :, :], k.x[:, :, :], b[5][:, :].rearrange("p (t d) -> p t d", t=T), ALU.add)

    def gpsimd(self, pool):
        pass

    def sync(self, sp):
        pass


def l2attn_weights(i, tiles, spread):
    a = {n: i["L2_attn_" + n] for n in ("Wq", "Wk", "Wv", "Wb", "conv_q", "conv_k", "conv_v", "W2", "Wo", "W1")}
    stats = np.zeros((64, H2, P), np.float32)
    for h in range(H2):
        stats[16 * h:16 * h + 16, h] = a["W1"][D:]
    chunk = np.kron(np.eye(4, dtype=np.float32), np.ones((32, 32), np.float32))
    w = {"L2a_" + n: v for n, v in a.items() if n != "W1"}
    w.update({
        "L2a_W1x": a["W1"][:D], "L2a_W1s": stats.reshape(64, H2 * P),
        "L2a_fir_long": i["L2_attn_fir_long"].reshape(P, FIR)[:, :PE_TAPS],
        "L2a_fir_long_rest": i["L2_attn_fir_long"].reshape(P, FIR)[:, PE_TAPS:], "L2a_fir_short": i["L2_attn_fir_short"].reshape(P, 5),
        "L2a_b1": i["L2_attn_b1"].reshape(P, 1),
        "L2a_b2": spread(np.concatenate([i["L2_attn_b2"]] * H2)), "L2a_base_bias": spread(i["L2_attn_base_bias"]),
        "L2a_log_temp": spread(i["L2_attn_log_temp"]), "L2a_residual_logit": spread(i["L2_attn_conv_residual_logit"]),
        "L2a_rms_w": spread(i["L2_attn_rms_w"]),
        "blocks32": chunk, "chunk_lower": np.tril(chunk, -1), "chunk_upper": np.triu(chunk),
    })
    r = np.arange(P)
    for size in (1, 2, 4, 8, 16):
        low = ((r[:, None] // (2 * size) == r[None, :] // (2 * size)) & (r[:, None] // size % 2 == 1)
               & (r[None, :] // size % 2 == 0)).astype(np.float32)
        w[f"above{size}"] = low.T
        if size == 1:
            w["below1"] = low
    return w


MORE_WEIGHTS += [l2attn_weights]


H3 = 16


class PrepL3:

    def __init__(self, kit):
        self.k = kit

        def keep(name, n):
            return kit.ctx.enter_context(kit.nc.sbuf_tensor("l3_" + name, [P, n], F32))
        self.L = keep("decay", H3 * 2 * P)
        self.ad, self.dt = keep("A_dt", H3), keep("dt", H3)
        self.t = [keep(f"t{i}", H3) for i in range(7)]

    def scalar(self, act):
        k, nc, t = self.k, self.k.nc, self.t
        nc.scalar.activation(t[0][:, :], k.w("L3a_dt_bias"), ACT.Abs).then_inc(k.sem("dt_abs"), 1)
        act.wait_ge(k.sem("dt_abs"), 1)
        nc.scalar.activation(t[1][:, :], t[0][:, :], ACT.Exp, scale=-1.0).then_inc(k.sem("dt_exp"), 1)
        nc.scalar.activation(t[6][:, :], k.w("L3a_A_log"), ACT.Exp).then_inc(k.sem("A_exp"), 1)
        act.wait_ge(k.sem("A_dt"), 1)
        for h in range(H3):
            nc.scalar.activation(self.L[:, h * 256:(h + 1) * 256], k.w("L3a_diff"), ACT.Exp,
                                 scale=self.ad[:, h:h + 1]).then_inc(k.sem("decay"), 1)

    def vector(self, dve):
        k, nc, own, t = self.k, self.k.nc, self.k.own["dve"], self.t
        dve.wait_ge(k.sem("dt_exp"), 1)
        own.step(softplus(k, self.dt[:, :], k.w("L3a_dt_bias"), t[1][:, :], t[2][:, :], t[3][:, :]))
        dve.wait_ge(k.sem("A_exp"), 1)
        own.step(nc.vector.scalar_tensor_tensor(t[4][:, :], t[6][:, :], -1.0, self.dt[:, :], ALU.mult, ALU.mult))
        nc.vector.tensor_scalar(self.ad[:, :], t[4][:, :], -1e30, None, ALU.max).then_inc(k.sem("A_dt"), 1)
        for h in range(H3):
            dve.wait_ge(k.sem("decay"), h + 1)
            v = self.L[:, h * 256:(h + 1) * 256]
            nc.vector.scalar_tensor_tensor(v, v, self.dt[:, h:h + 1], k.w("L3a_reach"), ALU.mult, ALU.mult)

    def tensor(self, pe):
        pass

    gpsimd = sync = tensor


class L3State:

    def __init__(self, kit, prep):
        self.prep, self.mem = prep, Arena(kit)
        self.x0, self.xm, self.t = self.mem(T, D), self.mem(T, D), self.mem(T, D)
        self.after = self.mem.at


def rows_of(kit, name, shape):
    return kit.w(name).unsqueeze(1).to_broadcast(shape)


def remix(kit, st, src, name):
    nc, own, sh = kit.nc, kit.own["dve"], [P, T, D]
    own.did(nc.vector.tensor_tensor(st.t, st.x0, rows_of(kit, name + "1", sh), ALU.mult))
    own.step(nc.vector.tensor_tensor(st.xm, src, rows_of(kit, name + "0", sh), ALU.mult))
    own.step(nc.vector.tensor_tensor(st.xm, st.xm, st.t, ALU.add))


def add_scaled(kit, st, y, name):
    nc, own, sh = kit.nc, kit.own["dve"], [P, T, D]
    own.step(nc.vector.tensor_tensor(st.t, y, rows_of(kit, name, sh), ALU.mult))
    ins = nc.vector.tensor_tensor(st.xm, st.xm, st.t, ALU.add)
    return ins


RMS_EPS = float(np.finfo(np.float32).eps)


class L3Mamba:

    def __init__(self, kit, st):
        self.k, self.st = kit, st
        mem = st.mem
        mem.at = st.after
        self.norm0 = Norm(kit, mem, kit.x, 1e-5)
        self.norm = Norm(kit, mem, st.xm, RMS_EPS, rms=True, tag="_m")
        self.xT = mem(GT)
        self.pad = [mem(NB, 3 + SEQ) for _ in range(2)]
        self.c = [[mem(NB, SEQ) for _ in range(2)] for _ in range(2)]
        self.val = [mem(GT) for _ in range(2)]
        self.v = mem(T, H3, 32)
        self.sg = [mem(GT) for _ in range(2)]
        self.gate = [mem(GT) for _ in range(2)]
        self.B = [mem(GT) for _ in range(2)]
        self.C = [mem(GT) for _ in range(2)]
        self.S = [mem(3 * P) for _ in range(4)]
        self.y = [mem(GT) for _ in range(2)]
        self.units = [(j, s, hh) for j in range(8) for s in range(NB) for hh in range(2)]

    def tensor(self, pe):
        k, nc, b = self.k, self.k.nc, self.k.bank
        for t in range(T):
            pe.wait_ge(k.sem("xm_mixed"), 1)
            ins = nc.tensor.transpose(b[6][:, t * P:(t + 1) * P], self.st.xm[:, t, :], k.w("ident"))
        ins.then_inc(k.sem("xm_turned"), 1)
        self.norm.tensor(pe, b[7])
        pe.wait_ge(k.sem("nT_m"), 1)
        for i in range(2):
            nc.tensor.matmul(b[i][:, :], k.row("L3a_in", i * P, (i + 1) * P), k.nT[:, :], start=True, stop=True)\
                .then_inc(k.sem("value_made"), 1)
        for i in range(2):
            nc.tensor.matmul(b[2 + i][:, :], k.row("L3a_in", 256 + i * P, 256 + (i + 1) * P), k.nT[:, :],
                             start=True, stop=True).then_inc(k.sem("gate_made"), 1)
        for i in range(2):
            pe.wait_ge(k.sem("value"), i + 1)
            for t in range(T):
                ins = nc.tensor.transpose(b[4 + i][:, t * P:(t + 1) * P], self.val[i][:, t * P:(t + 1) * P],
                                          k.w("ident"))
            ins.then_inc(k.sem("value_turned"), 1)

        def bc(j):
            if j >= 1:
                pe.wait_ge(k.sem("B"), j)
                pe.wait_ge(k.sem("C"), j)
            nc.tensor.matmul(b[0][:, :], k.row("L3a_B", j * P, (j + 1) * P), self.xT, start=True, stop=True)\
                .then_inc(k.sem("B_made"), 1)
            nc.tensor.matmul(b[1][:, :], k.row("L3a_C", j * P, (j + 1) * P), self.xT, start=True, stop=True)\
                .then_inc(k.sem("C_made"), 1)

        def gram(n):
            j, s, hh = self.units[n]
            pe.wait_ge(k.sem("B"), j + 1)
            pe.wait_ge(k.sem("C"), j + 1)
            if n >= 4:
                pe.wait_ge(k.sem("S"), n - 3)
            rows = slice(64 * hh, 64 * hh + 64)
            B, C, at = self.B[j % 2], self.C[j % 2], s * SEQ
            o = b[2 + n % 4]
            nc.tensor.matmul(o[:, 0:SEQ], B[rows, at:at + P], C[rows, at:at + SEQ], start=True, stop=True)
            nc.tensor.matmul(o[:, SEQ:SEQ + P], B[rows, at + P:at + SEQ], C[rows, at + P:at + SEQ],
                             start=True, stop=True).then_inc(k.sem("gram"), 1)

        def scan(n):
            j, s, hh = self.units[n]
            pe.wait_ge(k.sem("S"), n + 1)
            h, slot, S = 2 * j + hh, j % 4, self.S[n % 4]
            o, at = b[6 + j // 4][32 * slot:32 * slot + 32, :], s * SEQ
            kw = dict(skip_group_check=True, tile_position=(0, 32 * slot))
            nc.tensor.matmul(o[:, at:at + SEQ], self.v[:, 2 * s, h, :], S[:, 0:SEQ], start=(hh == 0), stop=False, **kw)
            nc.tensor.matmul(o[:, at + P:at + SEQ], self.v[:, 2 * s + 1, h, :], S[:, SEQ:3 * P],
                             start=False, stop=(hh == 1), **kw).then_inc(k.sem("scanned"), 1)

        pe.wait_ge(k.sem("padded"), 2)
        pe.wait_ge(k.sem("xT"), 1)
        bc(0)
        pe.wait_ge(k.sem("gate"), 2)
        pe.wait_ge(k.sem("v_tok"), 4)
        pe.wait_ge(k.sem("v_clear"), 1)
        n_units = len(self.units)
        for n in range(n_units + 2):
            if n < n_units:
                if n % 4 == 0 and n // 4 + 1 < 8:
                    bc(n // 4 + 1)
                gram(n)
            if n >= 2:
                scan(n - 2)
        pe.wait_ge(k.sem("y_gated"), 2)
        for t in range(T):
            for i in range(2):
                ins = nc.tensor.matmul(b[2][:, t * D:(t + 1) * D], self.y[i][:, t * P:(t + 1) * P],
                                       k.row("L3a_out", i * D, (i + 1) * D), start=(i == 0), stop=(i == 1))
        ins.then_inc(k.sem("out_made"), 1)

    def scalar(self, act):
        k, nc, b = self.k, self.k.nc, self.k.bank
        act.wait_ge(k.sem("xm_turned"), 1)
        nc.scalar.copy(self.xT, b[6][:, :]).then_inc(k.sem("xT"), 1)
        self.norm.scalar(act, b[7])
        for i in range(2):
            act.wait_ge(k.sem("value_made"), i + 1)
            nc.scalar.copy(self.pad[i][:, :, 3:], b[i][:, :].rearrange("p (b s) -> p b s", b=NB))\
                .then_inc(k.sem("padded"), 1)
        for i in range(2):
            act.wait_ge(k.sem("gate_made"), i + 1)
            nc.scalar.activation(self.sg[i], b[2 + i][:, :], ACT.Sigmoid).then_inc(k.sem("gate_sigmoid"), 1)
        for i in range(2):
            act.wait_ge(k.sem(f"conv{i}"), 4)
            nc.scalar.activation(self.c[i][0], self.c[i][1], ACT.Sigmoid).then_inc(k.sem("value_sigmoid"), 1)
        for j in range(8):
            act.wait_ge(k.sem("B_made"), j + 1)
            if j >= 2:
                act.wait_ge(k.sem("gram"), 4 * (j - 1))
            nc.scalar.copy(self.B[j % 2], b[0][:, :]).then_inc(k.sem("B"), 1)
            act.wait_ge(k.sem("C_made"), j + 1)
            nc.scalar.copy(self.C[j % 2], b[1][:, :]).then_inc(k.sem("C"), 1)

    def vector(self, dve):
        k, nc, b, own, st = self.k, self.k.nc, self.k.bank, self.k.own["dve"], self.st
        for i in range(2):
            own.did(nc.vector.memset(self.pad[i][:, :, 0:3], 0.0))
        self.norm0.vector(dve)
        dve.wait_ge(k.sem("norm_n"), T)
        own.step(nc.vector.tensor_copy(st.x0, k.n[:, :, :]))
        remix(k, st, st.x0, "L3a_mix_m")
        nc.vector.sem_inc(k.sem("xm_mixed"), 1)
        self.norm.vector(dve)
        for i in range(2):
            dve.wait_ge(k.sem("padded"), i + 1)
            for j in range(4):
                s = self.pad[i][:, :, j:j + SEQ]
                w = k.row("L3a_conv", 4 * i + j, 4 * i + j + 1)
                if j == 0:
                    ins = nc.vector.tensor_scalar(self.c[i][0], s, w, k.row("L3a_conv_b", i, i + 1), ALU.mult, ALU.add)
                else:
                    dve.wait_ge(k.sem(f"conv{i}"), j)
                    ins = nc.vector.scalar_tensor_tensor(self.c[i][j % 2], s, w, self.c[i][(j + 1) % 2],
                                                         ALU.mult, ALU.add)
                ins.then_inc(k.sem(f"conv{i}"), 1)
        for i in range(2):
            dve.wait_ge(k.sem("gate_sigmoid"), i + 1)
            nc.vector.tensor_tensor(self.gate[i], self.sg[i], b[2 + i][:, :], ALU.mult)\
                .then_inc(k.sem("gate"), 1)
        for i in range(2):
            dve.wait_ge(k.sem("value_sigmoid"), i + 1)
            nc.vector.tensor_tensor(self.val[i].rearrange("p (b s) -> p b s", b=NB), self.c[i][0], self.c[i][1],
                                    ALU.mult).then_inc(k.sem("value"), 1)
        dve.wait_ge(k.sem("v_clear"), 1)
        for i in range(2):
            dve.wait_ge(k.sem("value_turned"), i + 1)
            for odd in range(2):
                nc.vector.tensor_copy(self.v[:, :, 8 * i + odd:8 * i + 8:2, 16 * odd:16 * odd + 16],
                                      b[4 + i][:, :].rearrange("p (t h c) -> p t h c", t=T, c=16)[:, :, odd::2, :])\
                    .then_inc(k.sem("v_tok"), 1)
        for n, (j, s, hh) in enumerate(self.units):
            h = 2 * j + hh
            L = st.prep.L[:, h * 256:(h + 1) * 256]
            dve.wait_ge(k.sem("gram"), n + 1)
            if n >= 4:
                dve.wait_ge(k.sem("scanned"), n - 3)
            o = b[2 + n % 4]
            nc.vector.tensor_tensor(self.S[n % 4][:, 0:SEQ], o[:, 0:SEQ], L, ALU.mult)
            nc.vector.tensor_tensor(self.S[n % 4][:, SEQ:], o[:, SEQ:3 * P], L[:, 0:P], ALU.mult)\
                .then_inc(k.sem("S"), 1)
        dve.wait_ge(k.sem("value"), 2)
        for i in range(2):
            dve.wait_ge(k.sem("scanned"), 16 * (i + 1))
            own.step(nc.vector.scalar_tensor_tensor(self.y[i], self.val[i], k.row("L3a_D", i, i + 1), b[6 + i][:, :],
                                                    ALU.mult, ALU.add))
            nc.vector.tensor_tensor(self.y[i], self.y[i], self.gate[i], ALU.mult).then_inc(k.sem("y_gated"), 1)
        dve.wait_ge(k.sem("out_made"), 1)
        add_scaled(k, st, b[2][:, :].rearrange("p (t d) -> p t d", t=T), "L3a_mamba_scale")

    def gpsimd(self, pool):
        self.norm0.gpsimd(pool)
        self.k.nc.gpsimd.memset(self.v, 0.0).then_inc(self.k.sem("v_clear"), 1)
        self.norm.gpsimd(pool)

    def sync(self, sp):
        pass


class L3Mlp:

    def __init__(self, kit, st, which, last):
        self.k, self.st, self.which, self.last = kit, st, which, last
        mem = st.mem
        mem.at = st.after
        self.norm = Norm(kit, mem, st.xm, RMS_EPS, rms=True)
        self.mlp = Mlp(kit, mem, kit.nT, 4, 4, "square", ACT.Relu,
                       first=lambda u: kit.row(f"L3a_{which}_fc", u * P, (u + 1) * P),
                       down=lambda u: kit.row(f"L3a_{which}_proj", u * P, (u + 1) * P), use=self.use)

    def use(self, e, y):
        k = self.k
        return add_scaled(k, self.st, y[:, :].rearrange("p (t d) -> p t d", t=T), f"L3a_{self.which}_mlp_scale")

    def tensor(self, pe):
        self.norm.tensor(pe, self.k.bank[7])
        pe.wait_ge(self.k.sem("nT"), 1)
        self.mlp.tensor(pe)

    def scalar(self, act):
        self.norm.scalar(act, self.k.bank[7])
        self.mlp.scalar(act)

    def vector(self, dve):
        self.norm.vector(dve)
        self.mlp.vector(dve)
        if self.last:
            dve.wait_ge(self.k.sem("y_used"), 1)
            self.k.nc.vector.tensor_tensor(self.k.x[:, :, :], self.k.x[:, :, :], self.st.xm, ALU.add)

    def gpsimd(self, pool):
        self.norm.gpsimd(pool)

    def sync(self, sp):
        pass


class L3Attention:

    def __init__(self, kit, st):
        self.k, self.st = kit, st
        mem = st.mem
        mem.at = st.after
        self.norm = Norm(kit, mem, st.xm, RMS_EPS, rms=True)
        self.heads = Heads(kit, mem, 4, "L3a_", True, self.deliver)

    def deliver(self, y):
        add_scaled(self.k, self.st, y, "L3a_attn_scale")

    def tensor(self, pe):
        self.norm.tensor(pe, self.k.bank[7])
        pe.wait_ge(self.k.sem("nT"), 1)
        self.heads.tensor(pe)

    def scalar(self, act):
        self.norm.scalar(act, self.k.bank[7])
        self.heads.scalar(act)

    def vector(self, dve):
        remix(self.k, self.st, self.st.xm, "L3a_mix_a")
        self.norm.vector(dve)
        self.heads.vector(dve)

    def gpsimd(self, pool):
        self.norm.gpsimd(pool)
        self.heads.gpsimd(pool)

    def sync(self, sp):
        pass


def l3attn_weights(i, tiles, spread):
    a = lambda n: i["L3_attn_" + n]
    q, kk = np.arange(P)[None, :], np.arange(P)[:, None]
    return {
        "L3a_in": a("in_proj_w"), "L3a_B": a("B_proj_w"), "L3a_C": a("C_proj_w"), "L3a_out": tiles(a("out_proj_w"), D),
        "L3a_conv": tiles(a("conv_w"), 4), "L3a_conv_b": a("conv_b").reshape(2, P).T,
        "L3a_D": np.repeat(a("D_param"), 16).reshape(2, P).T,
        "L3a_dt_bias": spread(a("dt_bias")), "L3a_A_log": spread(a("A_log")),
        "L3a_diff": np.concatenate([np.maximum(q - kk, 0), q - kk + P], 1).astype(np.float32),
        "L3a_reach": np.concatenate([(q >= kk), np.ones((P, P), bool)], 1).astype(np.float32),
        "L3a_mix_m0": spread(a("resid_mix_m")[0]), "L3a_mix_m1": spread(a("resid_mix_m")[1]),
        "L3a_mix_a0": spread(a("resid_mix_a")[0]), "L3a_mix_a1": spread(a("resid_mix_a")[1]),
        "L3a_mamba_scale": spread(a("mamba_scale")), "L3a_attn_scale": spread(a("attn_scale")),
        "L3a_m_mlp_scale": spread(a("m_mlp_scale")), "L3a_a_mlp_scale": spread(a("a_mlp_scale")),
        "L3a_m_fc": a("m_fc_w"), "L3a_m_proj": tiles(a("m_proj_w"), D),
        "L3a_a_fc": a("a_fc_w"), "L3a_a_proj": tiles(a("a_proj_w"), D),
    }


MORE_WEIGHTS += [l3attn_weights]


def build(nc, dram, out, columns, width):
    with ExitStack() as ctx:
        kit = Kit(nc, ctx, columns, width)
        const = Constants(kit)
        binarised, of_l1, of_l2, of_l3 = Binarise(kit), PrepL1(kit), PrepL2(kit), PrepL3(kit)
        y = [nc.dram_tensor(f"between_{i}", [TOKENS + Stream.AHEAD * GT, D], F32).ap() for i in range(3)]
        n_ext = nc.dram_tensor("n_and_scores", [TOKENS, NEXT], F32).ap()
        l0_ffn, l0_attn = L0Ffn(kit, dram), L0Attn(kit)
        chain = [(l0_ffn, dram["x"], y[0]), (l0_attn, y[0], y[1]), (l0_ffn, y[1], y[2])]
        l1_ffn, l1_attn, l2_ffn, l3_ffn = L1Ffn(kit), L1Attn(kit, of_l1), L2Ffn(kit, binarised), L3Ffn(kit)
        s2, s3 = L2State(kit, of_l2), L3State(kit, of_l3)
        to_l3 = [l1_ffn, l1_attn, l1_ffn, l2_ffn, L2Project(kit, s2), L2Delta(kit, s2), L2Mix(kit, s2), l2_ffn]
        in_l3 = [l3_ffn, L3Mamba(kit, s3), L3Mlp(kit, s3, "m", False), L3Attention(kit, s3),
                 L3Mlp(kit, s3, "a", True), l3_ffn]
        stages = to_l3 + in_l3
        page_to_l3 = 3
        page_to_l1 = len(stages) - 1
        block = ctx.enter_context(nc.Block())

        def whole(eng, name, method):
            kit.stage = 0
            kit.own = {name: Own(eng, kit.own_sems[name])} if name in kit.own_sems else {}
            if name == "sp":
                page_loaded(kit, eng)
            else:
                eng.wait_ge(kit.base_in, 16)
            kit.end(eng, name)
            method(const)(eng)
            kit.end(eng, name)

            def load_rest():
                n = width["resident"]
                step = (n - BASE + WEIGHT_DMAS - 1) // WEIGHT_DMAS
                for i in range(WEIGHT_DMAS if name == "sp" else 0):
                    a, b = BASE + i * step, min(n, BASE + (i + 1) * step)
                    eng.dma_start(kit.W["resident"][:, a:b], dram["weights_resident"][:, a:b])\
                        .then_inc(kit.weights_in, 16)

            def prepare():
                if name != "sp":
                    eng.wait_ge(kit.weights_in, 16 * WEIGHT_DMAS)
                for stage in (binarised, of_l1, of_l2, of_l3):
                    method(stage)(eng)
                    kit.end(eng, name)

            def to_l1():
                if name == "sp":
                    load_page(kit, eng, dram["weights_L1f"])

            for n, (stage, a, b) in enumerate(chain):
                stage.run(eng, name, method, a, b, n_ext, load_rest if n == 0 else None,
                          to_l1 if n == len(chain) - 1 else None)
                if n == 0:
                    prepare()
            stream = Stream(kit, y[2], out)
            if name == "sp":
                page_loaded(kit, eng)
            stream.begin(eng, name)
            with eng.Fori(0, GROUPS) as g:
                for n, stage in enumerate(stages):
                    if name == "sp" and n == page_to_l3:
                        load_page(kit, eng, dram["weights_L3f"])
                    method(stage)(eng)
                    if name == "sp" and n == len(to_l3) - 1:
                        page_loaded(kit, eng)
                    if name == "sp" and n == page_to_l1:
                        used = -(-dram["weights_L1f"].shape[1] // (2 * P))
                        eng.wait_ge(kit.sem("down_done"), used)
                        load_page(kit, eng, dram["weights_L1f"])
                        page_loaded(kit, eng)
                    kit.end(eng, name)
                stream.swap(eng, name, g)
            stream.finish(eng, name)

        @block.sync
        def _(sp):
            sp.dma_start(kit.W["resident"][:, 0:BASE], dram["weights_resident"][:, 0:BASE]).then_inc(kit.base_in, 16)
            for v in y:
                sp.dma_start(v[TOKENS:, :], dram["x"][TOKENS:, :]).then_inc(kit.pads_in, 16)
            load_page(kit, sp, dram["weights_first"])
            sp.wait_ge(kit.pads_in, 16 * len(y))
            whole(sp, "sp", lambda s: s.sync)

        @block.scalar
        def _(act):
            whole(act, "act", lambda s: s.scalar)

        @block.vector
        def _(dve):
            whole(dve, "dve", lambda s: s.vector)

        @block.tensor
        def _(pe):
            whole(pe, "pe", lambda s: s.tensor)

        @block.gpsimd
        def _(pool):
            whole(pool, "pool", lambda s: s.gpsimd)


WEIGHT_DMAS = 8
BASE = 512


def pack(i):
    def tiles(a, cols):
        n = a.shape[0] // P
        return a.reshape(n, P, cols).transpose(1, 0, 2).reshape(P, n * cols)

    def spread(a):
        a = a.reshape(1, -1)
        return np.broadcast_to(a, (P, a.shape[1]))

    w = {
        "ident": np.eye(P, dtype=np.float32),
        "ones": np.ones((P, P), np.float32),
        "minus_half": np.full((P, 8), -0.5, np.float32),
        "iota8": spread(np.arange(8, dtype=np.float32)),
        "L1f_gate": i["L1_ffn_gate_w"].transpose(1, 0, 2).reshape(P, -1),
        "L1f_up": i["L1_ffn_up_w"].transpose(1, 0, 2).reshape(P, -1),
        "L1f_down": tiles(i["L1_ffn_down_w"].reshape(-1, D), D),
        "L1f_gate_b": i["L1_ffn_gate_b"].reshape(-1, P).T,
        "L1f_up_b": i["L1_ffn_up_b"].reshape(-1, P).T,
        "L1f_down_b": i["L1_ffn_down_b"],
        "L1f_router": i["L1_ffn_router_w"].T,
        "L2f_w1": tiles(i["L2_ffn_w1"], D),
        "L2f_w2": i["L2_ffn_w2"],
        "L2f_b1": i["L2_ffn_b1"].reshape(4, P).T,
        "L2f_b2": i["L2_ffn_b2"].reshape(1, D),
    }
    for more in MORE_WEIGHTS:
        w.update(more(i, tiles, spread))
    columns, arrays = {}, {}
    for page, prefixes in PAGES.items():
        mine = [n for n in w if n.startswith(prefixes)] if prefixes else \
            [n for n in w if not any(p and n.startswith(p) for p in PAGES.values())]
        at, parts = 0, []
        for name in mine:
            a = w[name]
            columns[name] = ("page" if prefixes else "resident", at, a.shape[0], a.shape[1])
            if a.shape[0] < P:
                a = np.concatenate([a, np.zeros((P - a.shape[0], a.shape[1]), np.float32)], 0)
            parts.append(a)
            at += a.shape[1]
        assert not prefixes or at <= PAGE
        arrays["weights_" + page] = np.ascontiguousarray(np.concatenate(parts, 1))
    return columns, arrays


PAGES = {
    "first": ("L0f_", "L0a_", "L2f_w", "L3a_diff", "L3a_reach", "L2a_fir_long_pe", "below_", "token_parts", "iota256",
              "mask_neg", "head_rows"),
    "L1f": ("L1f_gate", "L1f_up", "L1f_down"),
    "L3f": ("L3f_tiles",),
    "resident": (),
}


def load_page(kit, sp, src, parts=4):
    n = src.shape[1]
    step = (n + parts - 1) // parts
    for i in range(parts):
        a, b = i * step, min(n, (i + 1) * step)
        sp.dma_start(kit.W["page"][:, a:b], src[:, a:b]).then_inc(kit.page_in, 16)


def page_loaded(kit, sp, parts=4):
    sp.wait_ge(kit.page_in, 16 * parts)
    sp.sem_clear(kit.page_in)


def kernel(**inputs):
    from concourse import bacc
    from concourse.bass_utils import run_bass_kernel_spmd

    i = {name: np.asarray(a) for name, a in inputs.items()}
    columns, arrays = pack(i)
    arrays.update(extra_inputs(i))
    arrays["x"] = np.concatenate([i["L0_attn_x"].reshape(TOKENS, D), np.zeros((Stream.AHEAD * GT, D), np.float32)], 0)
    nc = bacc.Bacc("TRN2", target_bir_lowering=False, num_devices=1)
    dram = {name: nc.dram_tensor(name, a.shape, F32, kind="ExternalInput").ap() for name, a in arrays.items()}
    out = nc.dram_tensor("out", (TOKENS, D), F32, kind="ExternalOutput").ap()
    build(nc, dram, out, columns, {"resident": arrays["weights_resident"].shape[1]})
    r = run_bass_kernel_spmd(nc, [arrays], core_ids=[0])
    return r.results[0]["out"].reshape(i["L0_attn_x"].shape)
```
